# Optimizing a Trainium2 kernel written in Bass

```python
import numpy as np
import jax
import jax.numpy as jnp

def _softmax(x, axis=-1):
    return jax.nn.softmax(x, axis=axis)

def _gelu(x):
    return jax.nn.gelu(x, approximate=True)

def _silu(x):
    return jax.nn.silu(x)

def _sigmoid(x):
    return jax.nn.sigmoid(x)

def _layernorm(x, axis=-1, eps=1e-05):
    m = jnp.mean(x, axis=axis, keepdims=True)
    v = jnp.var(x, axis=axis, keepdims=True)
    return (x - m) / jnp.sqrt(v + eps)

def _scatter_add(tgt, idx, src, axis=0):
    return tgt.at[idx].add(src)

def _segment_sum(src, seg, n):
    return jax.ops.segment_sum(src, seg, n)
kernel_name = 'mk_perceiver_d2_seqx_r8_b070ca'

def setup_inputs(seed: int=0):
    np.random.seed(seed)
    _w = jnp.asarray

    def _rec_inputs():
        import jax
        import jax.numpy as jnp
        _rk = jax.random.key(seed)
        x = 7.22e-05 + 1 * jax.random.normal(jax.random.fold_in(_rk, 1), (64, 32, 256), jnp.float32)
        _lenS = 32 - jax.random.randint(jax.random.fold_in(_rk, 7), (64,), 0, max(1, 32 // 4) + 1, jnp.int32)
        _lenS2 = 257 - jax.random.randint(jax.random.fold_in(_rk, 8), (64,), 0, max(1, 257 // 4) + 1, jnp.int32)
        _ctx_512P = jax.random.normal(jax.random.fold_in(_rk, 11), (64, 16, 64), jnp.float32)
        _ctx_512c = jax.random.dirichlet(jax.random.fold_in(_rk, 511), 0.3 * jnp.ones((16,), jnp.float32), (64, 257))
        _ctx_512t = jnp.einsum('bsk,bkd->bsd', _ctx_512c, _ctx_512P)
        _ctx_512t = _ctx_512t * jax.lax.rsqrt(jnp.mean(jnp.square(_ctx_512t)) + 1e-12) * 0.953939
        ctx_512 = -0.000514642 + 1.00011 * (_ctx_512t + 0.3 * jax.random.normal(jax.random.fold_in(_rk, 611), (64, 257, 64), jnp.float32))
        return (x, ctx_512)
    x, ctx_512 = _rec_inputs()

    def _L0_xattn_setup():
        import jax, jax.numpy as jnp
        import numpy as np
        B, S, H, NH, L = (2, 256, 256, 16, 64)
        HD = H // NH
        key = jax.random.key(seed)
        k1, k2, k3, k4, k5 = jax.random.split(key, 5)
        scale = 0.02
        return {'q': jax.random.normal(k1, (B, S, H), dtype=jnp.float32), 'latent_kv': jax.random.normal(k2, (B, S, L), dtype=jnp.float32), 'Wq': jax.random.normal(k3, (H, H), dtype=jnp.float32) * scale, 'Wkv_expand': jax.random.normal(k4, (2 * H, L), dtype=jnp.float32) * scale, 'Wout': jax.random.normal(k5, (H, H), dtype=jnp.float32) * scale}
    _L0_xattn_all = _L0_xattn_setup()
    _L0_xattn_in = {k: v for k, v in _L0_xattn_all.items() if k in ('Wq', 'Wkv_expand', 'Wout')}
    del _L0_xattn_all

    def _L0_attn_setup():
        import jax, jax.numpy as jnp
        import numpy as np
        HEADS = 16
        DIM_HEAD = 128
        SCALE = 16.0
        EPS = 1e-05

        def _layernorm(x, g):
            mu = jnp.mean(x, axis=-1, keepdims=True)
            var = jnp.mean((x - mu) ** 2, axis=-1, keepdims=True)
            return (x - mu) * jax.lax.rsqrt(var + EPS) * g

        def _l2norm(t):
            return t * jax.lax.rsqrt(jnp.sum(t * t, axis=-1, keepdims=True) + 1e-12)
        key = jax.random.key(seed)
        ks = jax.random.split(key, 5)
        B, N, dim = (2, 256, 256)
        hidden = HEADS * DIM_HEAD
        x = jax.random.normal(ks[0], (B, N, dim), dtype=jnp.float32)
        g_norm = jnp.ones((dim,), dtype=jnp.float32)
        Wq = jax.random.normal(ks[1], (dim, hidden), dtype=jnp.float32) * dim ** (-0.5)
        Wkv = jax.random.normal(ks[2], (dim, 2 * DIM_HEAD), dtype=jnp.float32) * dim ** (-0.5)
        Wout = jax.random.normal(ks[3], (hidden, dim), dtype=jnp.float32) * hidden ** (-0.5)
        g_out = jnp.ones((dim,), dtype=jnp.float32)
        return {'x': x, 'g_norm': g_norm, 'Wq': Wq, 'Wkv': Wkv, 'Wout': Wout, 'g_out': g_out}
    _L0_attn_all = _L0_attn_setup()
    _L0_attn_in = {k: v for k, v in _L0_attn_all.items() if k in ('g_norm', 'Wq', 'Wkv', 'Wout', 'g_out')}
    del _L0_attn_all

    def _L0_ffn_setup():
        import jax, jax.numpy as jnp
        import numpy as np
        N_BLOCKS = 16
        BLOCK_SIZE = 64
        TOP_K = N_BLOCKS // 4
        key = jax.random.key(seed)
        k1, k2, k3, k4, k5 = jax.random.split(key, 5)
        in_f, out_f = (256, 1024)
        x = jax.random.normal(k1, (2, 512, in_f), dtype=jnp.float32)
        Wr = jax.random.normal(k2, (N_BLOCKS, in_f), dtype=jnp.float32) * in_f ** (-0.5)
        br = jnp.zeros((N_BLOCKS,), dtype=jnp.float32)
        W1 = jax.random.normal(k3, (out_f, in_f), dtype=jnp.float32) * in_f ** (-0.5)
        W2 = jax.random.normal(k4, (in_f, out_f), dtype=jnp.float32) * out_f ** (-0.5)
        return {'x': x, 'Wr': Wr, 'br': br, 'W1': W1, 'W2': W2}
    _L0_ffn_all = _L0_ffn_setup()
    _L0_ffn_in = {k: v for k, v in _L0_ffn_all.items() if k in ('Wr', 'br', 'W1', 'W2')}
    del _L0_ffn_all

    def _L1_xattn_setup():
        import jax, jax.numpy as jnp
        import numpy as np
        B, S, L = (2, 128, 128)
        DIM_Q, H, K, D_C, D_CQ, R = (256, 16, 128, 64, 192, 64)

        def _rope_tables(seq_len, dim, dtype):
            inv_freq = 1.0 / 10000.0 ** (jnp.arange(0, dim, 2, dtype=dtype) / dim)
            t = jnp.arange(seq_len, dtype=dtype)
            freqs = t[:, None] * inv_freq[None, :]
            sin = jnp.repeat(jnp.sin(freqs), 2, axis=-1)
            cos = jnp.repeat(jnp.cos(freqs), 2, axis=-1)
            return (sin, cos)

        def _rotate_half(x):
            h = x.shape[-1] // 2
            return jnp.concatenate([-x[..., h:], x[..., :h]], axis=-1)
        key = jax.random.key(seed)
        ks = jax.random.split(key, 8)
        s_in = 1.0 / np.sqrt(DIM_Q)
        s_k = 1.0 / np.sqrt(K)
        s_cq = 1.0 / np.sqrt(D_CQ)
        s_c = 1.0 / np.sqrt(D_C)
        return {'hidden_q': jax.random.normal(ks[0], (B, S, DIM_Q), jnp.float32), 'kv_c': jax.random.normal(ks[1], (B, L, D_C), jnp.float32), 'Wq': jax.random.normal(ks[2], (H * K, DIM_Q), jnp.float32) * s_in, 'w_kc_q': jax.random.normal(ks[3], (H, K, D_CQ), jnp.float32) * s_k, 'w_kc_kv': jax.random.normal(ks[4], (H, K, D_C), jnp.float32) * s_k, 'W_qr': jax.random.normal(ks[5], (H, D_CQ, R), jnp.float32) * s_cq / np.sqrt(R), 'W_kr': jax.random.normal(ks[6], (H, D_C, R), jnp.float32) * s_c, 'Wo': jax.random.normal(ks[7], (DIM_Q, H * K), jnp.float32) * s_k}
    _L1_xattn_all = _L1_xattn_setup()
    _L1_xattn_in = {k: v for k, v in _L1_xattn_all.items() if k in ('Wq', 'w_kc_q', 'w_kc_kv', 'W_qr', 'W_kr', 'Wo')}
    del _L1_xattn_all

    def _L1_attn_setup():
        import jax, jax.numpy as jnp
        import numpy as np
        B, S, E, H, G = (2, 256, 256, 16, 4)
        D = E // H
        key = jax.random.key(seed)
        ks = jax.random.split(key, 7)
        scale = 1.0 / np.sqrt(E)
        x = jax.random.normal(ks[0], (B, S, E), dtype=jnp.float32)
        Wq = jax.random.normal(ks[1], (H, E, D), dtype=jnp.float32) * scale
        bq = jax.random.normal(ks[2], (H, D), dtype=jnp.float32) * 0.02
        Wk = jax.random.normal(ks[3], (G, E, D), dtype=jnp.float32) * scale
        bk = jax.random.normal(ks[4], (G, D), dtype=jnp.float32) * 0.02
        Wv = jax.random.normal(ks[5], (G, E, D), dtype=jnp.float32) * scale
        bv = jax.random.normal(ks[6], (G, D), dtype=jnp.float32) * 0.02
        return {'x': x, 'Wq': Wq, 'bq': bq, 'Wk': Wk, 'bk': bk, 'Wv': Wv, 'bv': bv}
    _L1_attn_all = _L1_attn_setup()
    _L1_attn_in = {k: v for k, v in _L1_attn_all.items() if k in ('Wq', 'bq', 'Wk', 'bk', 'Wv', 'bv')}
    del _L1_attn_all

    def _L1_ffn_setup():
        import jax, jax.numpy as jnp
        import numpy as np
        H, I, E = (256, 512, 8)
        B, S = (2, 256)
        key = jax.random.key(seed)
        ks = jax.random.split(key, 5)
        scale = 0.02
        return {'hidden_states': jax.random.normal(ks[0], (B, S, H), dtype=jnp.float32), 'router_w': jax.random.normal(ks[1], (H, E), dtype=jnp.float32) * scale, 'gate_w': jax.random.normal(ks[2], (E, H, I), dtype=jnp.float32) * scale, 'up_w': jax.random.normal(ks[3], (E, H, I), dtype=jnp.float32) * scale, 'down_w': jax.random.normal(ks[4], (E, I, H), dtype=jnp.float32) * scale}
    _L1_ffn_all = _L1_ffn_setup()
    _L1_ffn_in = {k: v for k, v in _L1_ffn_all.items() if k in ('router_w', 'gate_w', 'up_w', 'down_w')}
    del _L1_ffn_all
    return {'x': x, 'ctx_512': ctx_512, 'L0_xattn_Wq': _L0_xattn_in['Wq'], 'L0_xattn_Wkv_expand': _L0_xattn_in['Wkv_expand'], 'L0_xattn_Wout': _L0_xattn_in['Wout'], 'L0_attn_g_norm': _L0_attn_in['g_norm'], 'L0_attn_Wq': _L0_attn_in['Wq'], 'L0_attn_Wkv': _L0_attn_in['Wkv'], 'L0_attn_Wout': _L0_attn_in['Wout'], 'L0_attn_g_out': _L0_attn_in['g_out'], 'L0_ffn_Wr': _L0_ffn_in['Wr'], 'L0_ffn_br': _L0_ffn_in['br'], 'L0_ffn_W1': _L0_ffn_in['W1'], 'L0_ffn_W2': _L0_ffn_in['W2'], 'L1_xattn_Wq': _L1_xattn_in['Wq'], 'L1_xattn_w_kc_q': _L1_xattn_in['w_kc_q'], 'L1_xattn_w_kc_kv': _L1_xattn_in['w_kc_kv'], 'L1_xattn_W_qr': _L1_xattn_in['W_qr'], 'L1_xattn_W_kr': _L1_xattn_in['W_kr'], 'L1_xattn_Wo': _L1_xattn_in['Wo'], 'L1_attn_Wq': _L1_attn_in['Wq'], 'L1_attn_bq': _L1_attn_in['bq'], 'L1_attn_Wk': _L1_attn_in['Wk'], 'L1_attn_bk': _L1_attn_in['bk'], 'L1_attn_Wv': _L1_attn_in['Wv'], 'L1_attn_bv': _L1_attn_in['bv'], 'L1_ffn_router_w': _L1_ffn_in['router_w'], 'L1_ffn_gate_w': _L1_ffn_in['gate_w'], 'L1_ffn_up_w': _L1_ffn_in['up_w'], 'L1_ffn_down_w': _L1_ffn_in['down_w']}

def reference(x, ctx_512, L0_xattn_Wq, L0_xattn_Wkv_expand, L0_xattn_Wout, L0_attn_g_norm, L0_attn_Wq, L0_attn_Wkv, L0_attn_Wout, L0_attn_g_out, L0_ffn_Wr, L0_ffn_br, L0_ffn_W1, L0_ffn_W2, L1_xattn_Wq, L1_xattn_w_kc_q, L1_xattn_w_kc_kv, L1_xattn_W_qr, L1_xattn_W_kr, L1_xattn_Wo, L1_attn_Wq, L1_attn_bq, L1_attn_Wk, L1_attn_bk, L1_attn_Wv, L1_attn_bv, L1_ffn_router_w, L1_ffn_gate_w, L1_ffn_up_w, L1_ffn_down_w):
    import jax
    import jax.numpy as jnp

    def _L0_xattn_ref(q, latent_kv, Wq, Wkv_expand, Wout):
        import jax, jax.numpy as jnp
        import numpy as np
        B, S, H, NH, L = (2, 256, 256, 16, 64)
        HD = H // NH
        b, sq, _ = q.shape
        sk = latent_kv.shape[1]
        qp = q @ Wq.T
        kv = latent_kv @ Wkv_expand.T
        k, v = jnp.split(kv, 2, axis=-1)
        qh = qp.reshape(b, sq, NH, HD).transpose(0, 2, 1, 3)
        kh = k.reshape(b, sk, NH, HD).transpose(0, 2, 1, 3)
        vh = v.reshape(b, sk, NH, HD).transpose(0, 2, 1, 3)
        inv_sqrt_d = 1.0 / jnp.sqrt(jnp.float32(HD))
        scores = jnp.einsum('bhqd,bhkd->bhqk', qh, kh) * inv_sqrt_d
        causal = jnp.tril(jnp.ones((sq, sk), dtype=bool))
        scores = jnp.where(causal, scores, jnp.finfo(scores.dtype).min)
        attn = jax.nn.softmax(scores, axis=-1)
        out = jnp.einsum('bhqk,bhkd->bhqd', attn, vh)
        out = out.transpose(0, 2, 1, 3).reshape(b, sq, H)
        return out @ Wout.T

    def _L0_attn_ref(x, g_norm, Wq, Wkv, Wout, g_out):
        import jax, jax.numpy as jnp
        import numpy as np
        HEADS = 16
        DIM_HEAD = 128
        SCALE = 16.0
        EPS = 1e-05

        def _layernorm(x, g):
            mu = jnp.mean(x, axis=-1, keepdims=True)
            var = jnp.mean((x - mu) ** 2, axis=-1, keepdims=True)
            return (x - mu) * jax.lax.rsqrt(var + EPS) * g

        def _l2norm(t):
            return t * jax.lax.rsqrt(jnp.sum(t * t, axis=-1, keepdims=True) + 1e-12)
        B, N, dim = x.shape
        xn = _layernorm(x, g_norm)
        q = xn @ Wq
        kv = xn @ Wkv
        k, v = (kv[..., :DIM_HEAD], kv[..., DIM_HEAD:])
        q = q.reshape(B, N, HEADS, DIM_HEAD).transpose(0, 2, 1, 3)
        q = q * SCALE
        q = _l2norm(q)
        k = _l2norm(k)
        s = jnp.sqrt(SCALE).astype(x.dtype)
        q = q * s
        k = k * s
        sim = jnp.einsum('bhid,bjd->bhij', q, k)
        attn = jax.nn.softmax(sim.astype(jnp.float32), axis=-1).astype(sim.dtype)
        out = jnp.einsum('bhij,bjd->bhid', attn, v)
        out = out.transpose(0, 2, 1, 3).reshape(B, N, HEADS * DIM_HEAD)
        out = out @ Wout
        return _layernorm(out, g_out)

    def _L0_ffn_ref(x, Wr, br, W1, W2):
        import jax, jax.numpy as jnp
        import numpy as np
        N_BLOCKS = 16
        BLOCK_SIZE = 64
        TOP_K = N_BLOCKS // 4
        x_shape = x.shape
        in_f = x_shape[-1]
        xf = x.reshape(-1, in_f)
        n = xf.shape[0]
        prob = jax.nn.softmax(xf @ Wr.T + br, axis=-1)
        _, idx = jax.lax.top_k(prob, TOP_K)
        mask = jnp.zeros((n, N_BLOCKS), dtype=xf.dtype)
        mask = mask.at[jnp.arange(n)[:, None], idx].set(1.0)
        W1b = W1.reshape(N_BLOCKS, BLOCK_SIZE, in_f)
        h = jnp.einsum('nf,ibf->nib', xf, W1b)
        h = jax.nn.gelu(h, approximate=False) * mask[:, :, None]
        W2b = W2.reshape(in_f, N_BLOCKS, BLOCK_SIZE)
        y = jnp.einsum('nib,fib->nf', h, W2b)
        return y.reshape(x_shape)

    def _L1_xattn_ref(hidden_q, kv_c, Wq, w_kc_q, w_kc_kv, W_qr, W_kr, Wo):
        import jax, jax.numpy as jnp
        import numpy as np
        B, S, L = (2, 128, 128)
        DIM_Q, H, K, D_C, D_CQ, R = (256, 16, 128, 64, 192, 64)

        def _rope_tables(seq_len, dim, dtype):
            inv_freq = 1.0 / 10000.0 ** (jnp.arange(0, dim, 2, dtype=dtype) / dim)
            t = jnp.arange(seq_len, dtype=dtype)
            freqs = t[:, None] * inv_freq[None, :]
            sin = jnp.repeat(jnp.sin(freqs), 2, axis=-1)
            cos = jnp.repeat(jnp.cos(freqs), 2, axis=-1)
            return (sin, cos)

        def _rotate_half(x):
            h = x.shape[-1] // 2
            return jnp.concatenate([-x[..., h:], x[..., :h]], axis=-1)
        b, s, _ = hidden_q.shape
        l = kv_c.shape[1]
        q_hk = (hidden_q @ Wq.T).reshape(b, s, H, K)
        q_big = jnp.einsum('bshk,hkq->bshq', q_hk, w_kc_q)
        sin, cos = _rope_tables(l, D_C, kv_c.dtype)
        kv_rope = kv_c * cos[None] + _rotate_half(kv_c) * sin[None]
        q_r = jnp.einsum('bshq,hqr->bhsr', q_big, W_qr)
        k_r = jnp.einsum('bld,hdr->bhlr', kv_rope, W_kr)
        scores = jnp.einsum('bhsr,bhlr->bhsl', q_r, k_r)
        attn = jax.nn.softmax(scores, axis=-1)
        ctx_c = jnp.einsum('bhsl,bld->bhsd', attn, kv_rope)
        ctx_lat = jnp.einsum('bhsd,hkd->bshk', ctx_c, w_kc_kv)
        out = ctx_lat.reshape(b, s, H * K) @ Wo.T
        return out

    def _L1_attn_ref(x, Wq, bq, Wk, bk, Wv, bv):
        import jax, jax.numpy as jnp
        import numpy as np
        B, S, E, H, G = (2, 256, 256, 16, 4)
        D = E // H
        h, e, d = Wq.shape
        g = Wk.shape[0]
        per = h // g
        s = x.shape[1]
        q = jnp.einsum('bse,hed->bhsd', x, Wq) + bq[None, :, None, :]
        kg = jnp.einsum('bse,ged->bgsd', x, Wk) + bk[None, :, None, :]
        vg = jnp.einsum('bse,ged->bgsd', x, Wv) + bv[None, :, None, :]
        k = jnp.repeat(kg, per, axis=1)
        v = jnp.repeat(vg, per, axis=1)
        scores = jnp.einsum('bhqd,bhkd->bhqk', q, k) * (1.0 / np.sqrt(d))
        causal = jnp.triu(jnp.ones((s, s), dtype=bool), k=1)
        scores = jnp.where(causal[None, None, :, :], -jnp.inf, scores)
        attn = jax.nn.softmax(scores, axis=-1)
        out = jnp.einsum('bhqk,bhkd->bhqd', attn, v)
        return out.transpose(0, 2, 1, 3).reshape(x.shape[0], s, h * d)

    def _L1_ffn_ref(hidden_states, router_w, gate_w, up_w, down_w):
        import jax, jax.numpy as jnp
        import numpy as np
        H, I, E = (256, 512, 8)
        B, S = (2, 256)
        hidden_shape = hidden_states.shape
        x = hidden_states.reshape(-1, hidden_shape[-1])
        route = jax.nn.sigmoid(x @ router_w)
        max_ind = jnp.argmax(route, axis=1)
        max_prob = jnp.take_along_axis(route, max_ind[:, None], axis=1)
        out = jnp.zeros_like(x)
        num_experts = gate_w.shape[0]
        for e in range(num_experts):
            mask = (max_ind == e)[:, None]
            h = jax.nn.silu(x @ gate_w[e]) * (x @ up_w[e])
            out = out + jnp.where(mask, h @ down_w[e], 0.0)
        out = out * max_prob
        return out.reshape(hidden_shape)
    x = x + _L0_xattn_ref(_layernorm(x, axis=-1), ctx_512, L0_xattn_Wq, L0_xattn_Wkv_expand, L0_xattn_Wout)
    x = x + _L0_attn_ref(_layernorm(x, axis=-1), L0_attn_g_norm, L0_attn_Wq, L0_attn_Wkv, L0_attn_Wout, L0_attn_g_out)
    x = x + _L0_ffn_ref(_layernorm(x, axis=-1), L0_ffn_Wr, L0_ffn_br, L0_ffn_W1, L0_ffn_W2)
    x = x + _L1_xattn_ref(_layernorm(x, axis=-1), ctx_512, L1_xattn_Wq, L1_xattn_w_kc_q, L1_xattn_w_kc_kv, L1_xattn_W_qr, L1_xattn_W_kr, L1_xattn_Wo)
    x = x + _L1_attn_ref(_layernorm(x, axis=-1), L1_attn_Wq, L1_attn_bq, L1_attn_Wk, L1_attn_bk, L1_attn_Wv, L1_attn_bv)
    x = x + _L1_ffn_ref(_layernorm(x, axis=-1), L1_ffn_router_w, L1_ffn_gate_w, L1_ffn_up_w, L1_ffn_down_w)
    return x

_drawn_inputs = setup_inputs


def setup_inputs(seed=0):
    import zlib

    import numpy as np

    out = dict(_drawn_inputs(seed))
    spreads = {'L0_attn_g_norm': (1.0, 0.2), 'L0_attn_g_out': (1.0, 0.2), 'L0_ffn_br': (0.0, 0.1)}
    factors = {'L0_xattn_Wq': 8.0,
     'L1_attn_bq': 8.0,
     'L1_attn_bk': 8.0,
     'L1_attn_bv': 5.027,
     'L1_ffn_router_w': 8.0,
     'L1_ffn_gate_w': 7.806,
     'L1_ffn_up_w': 7.742,
     'L1_ffn_down_w': 7.739}
    for name, (base, spread) in spreads.items():
        noise = np.random.default_rng([zlib.crc32(name.encode()), seed]).standard_normal(out[name].shape)
        drawn = base * np.exp(spread * noise) if base else spread * noise
        out[name] = jnp.asarray(drawn.astype(out[name].dtype))
    for name, factor in factors.items():
        out[name] = (out[name] * factor).astype(out[name].dtype)
    return out
```

```python
import concourse.bass as bass
from concourse import mybir
from contextlib import ExitStack

F32 = mybir.dt.float32
BF16 = mybir.dt.bfloat16
I32 = mybir.dt.int32
U32 = mybir.dt.uint32
ALU = mybir.AluOpType
ACT = mybir.ActivationFunctionType
X_AXIS = mybir.AxisListType.X

P = 128
BATCH, SEQ, DIM = 64, 32, 256
KEYS, CTX = 257, 64
TOKENS = BATCH * SEQ
TILES = TOKENS // P
TB = P // SEQ
KC = DIM // P
HEADS = 16
HD = DIM // HEADS
GROUPS = 4
PER = HEADS // GROUPS
DH = 128
LN_EPS = 1e-5
MASKED = -1e30

C_IDENT = 0
C_QMASK = 128
C_RMASK = 132
C_CAUSAL = 136
C_BEFORE = 168
C_LN = 296
C_LOWER = 304
C_STEPS = 560
C_RANKS = 576
C_SLOT = 584
C_SEL = 608
C_COS = 1632
C_SIN = 1760
C_LASTCOS = 1888
C_LASTSIN = 1952
C_ONE = 2016
C_ALL = 2017

EPS_LN, EPS_LN2, EPS_L2 = range(3)


class Link:

    def __init__(self, engine, semaphore, per):
        self.engine, self.semaphore, self.per = engine, semaphore, per

    def tile(self, t):
        self.base, self.made = t * self.per, 0

    def __call__(self, instruction):
        self.made += 1
        assert self.made <= self.per
        instruction.then_inc(self.semaphore, 1)
        self.engine.wait_ge(self.semaphore, self.base + self.made)

    def end(self):
        assert self.made == self.per, (self.made, self.per)


def run_steps(engine, step, first, last, full_from, full_to, unroll=2, tiles=TILES):

    def alone(i):
        step(i, i % 2, lambda d: 0 <= i + d < tiles)

    for i in range(first, full_from):
        alone(i)
    count = (full_to - full_from + 1) // unroll * unroll
    with engine.Fori(full_from, full_from + count - unroll + 1, unroll) as r:
        for k in range(unroll):
            step(r + k if k else r, (full_from + k) % 2, lambda d: True)
    for i in range(full_from + count, last + 1):
        alone(i)


def row(tensor, t):
    return tensor[:, bass.ds(t, 1), :].rearrange("p a n -> p (a n)")


class Moments:

    def __init__(self, nc, sb, consts):
        self.nc, self.consts = nc, consts
        self.stats = sb("row_stats", [P, TILES, 6])
        self.carrier = sb("carrier", [P, 1])
        self.moments = sb("moments", [P, TILES, 2])
        self.work = sb("moments_work", [P, 8 * TILES])
        self.root = Root(nc, self.work, TILES)

    def take(self, t, x):
        if not isinstance(t, int):
            self.nc.vector.memset(self.carrier[:, :], 0.0)
        return self.nc.vector.bn_stats(row(self.stats, t), x)

    def roots(self, engine, semaphore, eps, scale=1.0):
        link = Link(engine, semaphore, Root.LINKS + 5)
        link.tile(0)
        for t in range(TILES):
            last = self.nc.vector.bn_aggr(self.moments[:, t, :], self.stats[:, t, :])
        link(last)
        eps = self.consts[:, C_LN + eps:C_LN + eps + 1]
        link(self.nc.vector.tensor_scalar(self.work[:, 0:TILES], self.moments[:, :, 1], scale, eps, ALU.mult, ALU.add))
        self.factors = self.root(link)
        link.end()

    def apply(self, t, x, out):
        return self.nc.vector.tensor_scalar(out, x, row(self.moments, t)[:, 0:1], self.factors[:, bass.ds(t, 1)],
                                            ALU.subtract, ALU.mult)


class RowNorm:

    LINKS = 12

    def __init__(self, nc, sb, name, consts, eps):
        self.nc = nc
        self.eps = consts[:, C_LN + eps:C_LN + eps + 1]
        self.stats = sb(name + "_stats", [P, 6])
        self.carrier = sb(name + "_carrier", [P, 1])
        self.moments = sb(name + "_moments", [P, 2])
        self.work = sb(name + "_work", [P, 8])
        self.root = Root(nc, self.work)

    def __call__(self, link, x, out):
        nc = self.nc
        link(nc.vector.bn_stats(self.stats[:, :], x))
        nc.vector.memset(self.carrier[:, :], 0.0)
        link(nc.vector.bn_aggr(self.moments[:, :], self.stats[:, :]))
        link(nc.vector.tensor_scalar(self.work[:, 0:1], self.moments[:, 1:2], self.eps, None, ALU.add))
        rstd = self.root(link)
        return nc.vector.tensor_scalar(out, x, self.moments[:, 0:1], rstd, ALU.subtract, ALU.mult)


class Root:

    LINKS = 9
    MAGIC = 0x5F3759DF

    def __init__(self, nc, work, n=1):
        self.nc, self.n = nc, n
        self.v, self.guess, self.y0, self.a, self.y1, self.y2, self.b, self.y3 = (
            work[:, k * n:(k + 1) * n] for k in range(8))

    def __call__(self, link):
        v = self.nc.vector
        link(v.tensor_scalar(self.guess.bitcast(I32), self.v.bitcast(I32), 1, None, ALU.logical_shift_right))
        link(v.tensor_scalar(self.y0.bitcast(I32), self.guess.bitcast(I32), -1.0, float(self.MAGIC), ALU.mult, ALU.add))
        for y, three, out in ((self.y0, 3.0, self.y1), (self.y1, 12.0, self.y2)):
            self.square(link, y)
            link(v.scalar_tensor_tensor(out=out, in0=self.a, scalar=three, in1=y, op0=ALU.subtract, op1=ALU.mult))
        self.square(link, self.y2)
        link(v.tensor_scalar(self.b, self.a, -0.5 / 16 ** 3, 1.5 / 16, ALU.mult, ALU.add))
        link(v.tensor_tensor(self.y3, self.y2, self.b, ALU.mult))
        return self.y3

    def square(self, link, y):
        v = self.nc.vector
        if self.n == 1:
            link(v.scalar_tensor_tensor(out=self.a, in0=y, scalar=self.v, in1=y, op0=ALU.mult, op1=ALU.mult))
        else:
            link(v.tensor_tensor(self.b, y, self.v, ALU.mult))
            link(v.tensor_tensor(self.a, self.b, y, ALU.mult))


def wait_count(engine, semaphore, count):
    if not isinstance(count, int) or count > 0:
        engine.wait_ge(semaphore, count)


def small_attention(nc, name, scope, moments, x_sb, consts, ident, ident16, causal16, loaded, cross, w, ctx32=None, beside=None, background=None):
    sb, pb, sem = scope(name)
    kin = CTX if cross else P
    kchunks = 1 if cross else KC

    xn = sb("xn", [P, DIM])
    xnT = sb("xnT", [P, KC, P])
    srcT = sb("srcT", [kin, kchunks, TB, 4, SEQ])
    q_blocks = sb("q_blocks", [P, KC, TB, PER, SEQ])
    kT = sb("kT", [P, KC, P])
    v_blocks = [sb(f"v_blocks{u}", [P, TB * GROUPS, PER, HD]) for u in range(2)]
    scores_sb = sb("scores", [P, HEADS * SEQ])
    shifted = sb("shifted", [P, HEADS, SEQ])
    exps = sb("exps", [P, HEADS, SEQ])
    probs = sb("probs", [P, HEADS * SEQ])
    probsT = sb("probsT", [P, HEADS * SEQ])
    top = sb("top", [P, HEADS])
    total = sb("total", [P, HEADS])
    inverse = sb("inverse", [P, HEADS])
    oT = sb("oT", [P, KC, P])

    ps_T, ps_k = pb("ps_T"), pb("ps_k")
    ps_q, ps_v = pb("ps_q"), pb("ps_v")
    ps_scores = [pb("ps_scores0"), pb("ps_scores1")]
    ps_pT, ps_o = pb("ps_pT"), pb("ps_o")
    ps_out = ps_o
    vw = DIM if cross else GROUPS * HD

    xn_ready, turned, xnT_ready = sem("xn_ready"), sem("turned"), sem("xnT_ready")
    qk_made, v_made, q_ready, k_ready, v_ready = (sem(n) for n in ("qk_made", "v_made", "q_ready", "k_ready", "v_ready"))
    scores_made, scores_out, shifted_ready, exps_ready = (sem(n) for n in ("scores_made", "scores_out", "shifted_ready", "exps_ready"))
    probs_turned, probsT_ready = sem("probs_turned"), sem("probsT_ready")
    probs_ready, o_made, oT_ready, out_made, x_ready = (sem(n) for n in ("probs_ready", "o_made", "oT_ready", "out_made", "x_ready"))
    dve_roots, dve_s1, dve_s2 = (sem(n) for n in ("dve_roots", "dve_s1", "dve_s2"))

    with nc.Block() as block:

        @block.tensor
        def _(pe):
            for s, n in loaded:
                pe.wait_ge(s, n)

            def turn(t):
                pe.wait_ge(xn_ready, t + 1)
                for c in range(KC):
                    last = nc.tensor.transpose(ps_T[:, c * P:(c + 1) * P], xn[:, c * P:(c + 1) * P], ident)
                last.then_inc(turned, 1)

            def keys_queries(t):
                pe.wait_ge(xnT_ready, t + 1)
                for m in range(KC):
                    for c in range(kchunks):
                        nc.tensor.matmul(ps_k[:, m * P:(m + 1) * P], w["k"][:, c, m * P:(m + 1) * P],
                                         srcT[:, c, :, 0, :], start=(c == 0), stop=(c == kchunks - 1))
                for m in range(KC):
                    for c in range(KC):
                        last = nc.tensor.matmul(ps_q[:, m * P:(m + 1) * P], w["q"][:, c, m * P:(m + 1) * P],
                                                xnT[:, c, :], start=(c == 0), stop=(c == KC - 1))
                last.then_inc(qk_made, 1)

            def values(t, half):
                wait_count(pe, v_ready, 2 * t + half)
                for n in range(2):
                    b = 2 * half + n
                    for c in range(kchunks):
                        last = nc.tensor.matmul(ps_v[:, n * DIM:n * DIM + vw], srcT[:, c, b, :, :].rearrange("p r k -> p (r k)"),
                                                w["v"][:, c, :], start=(c == 0), stop=(c == kchunks - 1))
                last.then_inc(v_made, 1)

            def scores(t):
                pe.wait_ge(q_ready, t + 1)
                pe.wait_ge(k_ready, t + 1)
                wait_count(pe, scores_out, t)
                for p in range(2):
                    nc.tensor.matmul(ps_scores[p][:, 0:256], ident16, causal16, start=True, stop=False, skip_group_check=True)
                    half = slice(64 * p, 64 * p + 64)
                    for m in range(KC):
                        for b in range(TB):
                            rows = slice(b * SEQ, (b + 1) * SEQ)
                            last = nc.tensor.matmul(ps_scores[p][rows, m * P:(m + 1) * P], kT[half, m, rows],
                                                    q_blocks[half, m, b, :, :].rearrange("p h q -> p (h q)"),
                                                    start=False, stop=True, skip_group_check=True)
                last.then_inc(scores_made, 1)

            def turn_probs(t):
                pe.wait_ge(probs_ready, t + 1)
                for g in range(GROUPS):
                    last = nc.tensor.transpose(ps_pT[:, g * P:(g + 1) * P], probs[:, g * P:(g + 1) * P], ident)
                last.then_inc(probs_turned, 1)

            def weigh(t, u):
                pe.wait_ge(v_ready, 2 * t + 2)
                pe.wait_ge(probsT_ready, t + 1)
                wait_count(pe, x_ready, t)
                for g in range(GROUPS):
                    m, p = g // 2, g % 2
                    half = slice(64 * p, 64 * p + 64)
                    for b in range(TB):
                        at = ((p * KC + m) * TB + b) * SEQ
                        last = nc.tensor.matmul(ps_o[half, m * P + b * SEQ:m * P + (b + 1) * SEQ],
                                                v_blocks[u][:, b * GROUPS + g, :, :].rearrange("p h d -> p (h d)"),
                                                probsT[:, at:at + SEQ], start=True, stop=True)
                last.then_inc(o_made, 1)

            def finish(t):
                pe.wait_ge(oT_ready, t + 1)
                for c in range(KC):
                    if cross:
                        last = nc.tensor.matmul(ps_out[:, 0:DIM], oT[:, c, :], w["o"][:, c, :], start=(c == 0), stop=(c == KC - 1))
                    else:
                        last = nc.tensor.transpose(ps_out[:, c * P:(c + 1) * P], oT[:, c, :], ident)
                last.then_inc(out_made, 1)

            def step(i, u, live):
                if live(0):
                    scores(i)
                if live(-1):
                    turn_probs(i - 1)
                if live(1):
                    keys_queries(i + 1)
                if live(-1):
                    weigh(i - 1, 1 - u)
                if live(1):
                    values(i + 1, 0)
                if live(-1):
                    finish(i - 1)
                if live(2):
                    turn(i + 2)
                if live(1):
                    values(i + 1, 1)

            run_steps(pe, step, -2, TILES, 2, TILES - 3)

        if background:
            block.sync(background)
        if beside:
            block.gpsimd(beside)

        @block.scalar
        def _(act):
            def turned_out(t):
                act.wait_ge(turned, t + 1)
                wait_count(act, v_made, 2 * t)
                last = nc.scalar.copy(xnT[:, :, :], ps_T[:, 0:DIM].rearrange("p (c t) -> p c t", c=KC))
                if cross:
                    last = nc.scalar.copy(srcT[:, 0, :, :, :], ctx32[:, bass.ds(t, 1), :].rearrange("p a (b k) -> p (a b) k", b=TB)
                                          .unsqueeze(2).to_broadcast([CTX, TB, 4, SEQ]))
                else:
                    for c in range(KC):
                        last = nc.scalar.copy(srcT[:, c, :, :, :], ps_T[:, c * P:(c + 1) * P].rearrange("p (b k) -> p b k", b=TB)
                                              .unsqueeze(2).to_broadcast([P, TB, 4, SEQ]))
                last.then_inc(xnT_ready, 1)

            def keys_out(t):
                act.wait_ge(qk_made, t + 1)
                if cross:
                    last = nc.scalar.copy(kT[:, :, :], ps_k[:, 0:DIM].rearrange("p (c t) -> p c t", c=KC))
                else:
                    for m in range(KC):
                        last = nc.scalar.activation(kT[:, m, :], ps_k[:, m * P:(m + 1) * P], ACT.Identity, bias=w["bk"][:, m:m + 1])
                last.then_inc(k_ready, 1)

            def values_out(t, u, half):
                act.wait_ge(v_made, 2 * t + half + 1)
                if half == 0:
                    wait_count(act, o_made, t - 1)
                for r in range(PER):
                    src = ps_v[:, :].rearrange("p (b n) -> p b n", b=2)[:, :, 0:vw]
                    if cross:
                        src = src.rearrange("p b (g r d) -> p b g r d", g=GROUPS, r=PER)[:, :, :, r, :]
                    else:
                        src = src.rearrange("p b (g d) -> p b g d", g=GROUPS)
                    dst = v_blocks[u][:, half * 8:(half + 1) * 8, r, :].rearrange("p (b g) d -> p b g d", b=2)
                    last = nc.scalar.activation(dst, src, ACT.Copy, scale=consts[:, C_RMASK + r:C_RMASK + r + 1])
                last.then_inc(v_ready, 1)

            def probsT_out(t):
                act.wait_ge(probs_turned, t + 1)
                nc.scalar.copy(probsT[:, :], ps_pT[:, :]).then_inc(probsT_ready, 1)

            def outputs_out(t):
                act.wait_ge(o_made, t + 1)
                o_view = ps_o[:, 0:DIM].rearrange("p (c t) -> p c t", c=KC)
                if cross:
                    nc.scalar.copy(oT[:, :, :], o_view).then_inc(oT_ready, 1)
                else:
                    for m in range(KC):
                        last = nc.scalar.activation(oT[:, m, :], o_view[:, m, :], ACT.Identity, bias=w["bv"][:, m:m + 1])
                    last.then_inc(oT_ready, 1)

            def exponentials(t):
                act.wait_ge(shifted_ready, t + 1)
                nc.scalar.activation(exps[:, :, :], shifted[:, :, :], ACT.Exp).then_inc(exps_ready, 1)

            for s, n in loaded:
                act.wait_ge(s, n)

            def step(i, u, live):
                if live(-1):
                    probsT_out(i - 1)
                if live(1):
                    keys_out(i + 1)
                if live(0):
                    exponentials(i)
                if live(-1):
                    outputs_out(i - 1)
                if live(1):
                    values_out(i + 1, 1 - u, 0)
                    values_out(i + 1, 1 - u, 1)
                if live(2):
                    turned_out(i + 2)

            run_steps(act, step, -2, TILES, 2, TILES - 3)

        @block.vector
        def _(dve):
            s1, s2 = Link(dve, dve_s1, 1), Link(dve, dve_s2, 2)
            for s, n in loaded:
                dve.wait_ge(s, n)
            moments.roots(dve, dve_roots, EPS_LN)

            def queries_out(t):
                dve.wait_ge(qk_made, t + 1)
                for m in range(KC):
                    src = ps_q[:, m * P:(m + 1) * P].rearrange("p (b q) -> p b q", b=TB)
                    mask = consts[:, C_QMASK:C_QMASK + PER]
                    src = src.unsqueeze(2).to_broadcast([P, TB, PER, SEQ])
                    mask = mask.unsqueeze(1).unsqueeze(3).to_broadcast([P, TB, PER, SEQ])
                    if cross:
                        last = nc.vector.tensor_tensor(q_blocks[:, m, :, :, :], src, mask, ALU.mult)
                    else:
                        last = None
                        for b in range(TB):
                            last = nc.vector.scalar_tensor_tensor(
                                out=q_blocks[:, m, b, :, :], in0=src[:, b, :, :], scalar=w["bq"][:, m:m + 1],
                                in1=mask[:, b, :, :], op0=ALU.add, op1=ALU.mult)
                last.then_inc(q_ready, 1)

            def softmax_tail(t):
                dve.wait_ge(exps_ready, t + 1)
                s2.tile(t)
                s2(nc.vector.reduce_sum(total[:, :], exps[:, :, :], axis=X_AXIS))
                s2(nc.vector.reciprocal(inverse[:, :], total[:, :]))
                s2.end()
                wait_count(dve, probs_turned, t)
                nc.vector.tensor_tensor(probs[:, :].rearrange("p (h k) -> p h k", h=HEADS), exps[:, :, :],
                                        inverse[:, :].unsqueeze(2).to_broadcast([P, HEADS, SEQ]), ALU.mult).then_inc(probs_ready, 1)

            def residual(t):
                dve.wait_ge(out_made, t + 1)
                nc.vector.tensor_tensor(row(x_sb, t), row(x_sb, t), ps_out[:, 0:DIM], ALU.add).then_inc(x_ready, 1)
                dve.wait_ge(x_ready, t + 1)
                moments.take(t, row(x_sb, t))

            def softmax_head(t):
                dve.wait_ge(scores_made, t + 1)
                for p in range(2):
                    last = nc.vector.transpose(scores_sb[:, p * 256:(p + 1) * 256], ps_scores[p][:, 0:256])
                last.then_inc(scores_out, 1)
                dve.wait_ge(scores_out, t + 1)
                s1.tile(t)
                view = scores_sb[:, :].rearrange("p (h k) -> p h k", h=HEADS)
                s1(nc.vector.reduce_max(top[:, :], view, axis=X_AXIS))
                nc.vector.tensor_tensor(shifted[:, :, :], view, top[:, :].unsqueeze(2).to_broadcast([P, HEADS, SEQ]),
                                        ALU.subtract).then_inc(shifted_ready, 1)
                s1.end()

            def normalise(t):
                wait_count(dve, turned, t)
                moments.apply(t, row(x_sb, t), xn[:, :]).then_inc(xn_ready, 1)

            def step(i, u, live):
                if live(0):
                    softmax_head(i)
                if live(1):
                    queries_out(i + 1)
                if live(2):
                    normalise(i + 2)
                if live(0):
                    softmax_tail(i)
                if live(-1):
                    residual(i - 1)

            run_steps(dve, step, -2, TILES, 2, TILES - 3)


def shared_key_attention(nc, name, scope, moments, x_sb, consts, ident, loaded, wq, wkv, wo, g_out):
    sb, pb, sem = scope(name)
    out_norm = RowNorm(nc, sb, "out_norm", consts, EPS_LN)
    xn = sb("xn", [P, DIM])
    xnT = [sb(f"xnT{u}", [P, KC, P]) for u in range(2)]
    xn4T = sb("xn4T", [P, KC, TB, 4, SEQ])
    qT = sb("qT", [P, GROUPS, TB, PER, SEQ])
    qT_squared = sb("qT_squared", [P, GROUPS, TB, PER, SEQ])
    k_squared = sb("k_squared", [P, DH])
    k_work = sb("k_work", [P, 8])
    k_sum = sb("k_sum", [P, 1])
    k_root = Root(nc, k_work)
    k_norm = sb("k_norm", [P, DH])
    kT = [sb(f"kT{u}", [P, P]) for u in range(2)]
    v4 = [sb(f"v4{u}", [P, TB, DH]) for u in range(2)]
    q_work = sb("q_work", [P, 8 * HEADS])
    q_root = Root(nc, q_work, HEADS)
    scaled = sb("scaled", [P, HEADS, SEQ])
    exps = sb("exps", [P, HEADS, SEQ])
    probs = sb("probs", [P, HEADS * SEQ])
    probsT = sb("probsT", [P, GROUPS, TB, SEQ])
    total = sb("total", [P, HEADS])
    inverse = sb("inverse", [P, HEADS])
    oT = sb("oT", [P, PER, GROUPS, P])
    out_normed = sb("out_normed", [P, DIM])
    out_scaled = sb("out_scaled", [P, DIM])

    ps_T, ps_k, ps_v = pb("ps_T"), pb("ps_k"), pb("ps_v")
    ps_q = [pb("ps_q0"), pb("ps_q1")]
    ps_scores, ps_o, ps_out = pb("ps_scores"), pb("ps_o"), pb("ps_out")
    ps_norms = ps_T[:, DIM:DIM + HEADS]
    ps_kT = ps_k[:, DH:DH + P]

    names = ("xn_ready turned xnT_ready k_made k_sum_ready k_normed k_turned kT_ready v_made v_ready q_made q_ready "
             "squares_ready scores_made scaled_ready exps_ready probs_ready o_made oT_ready out_made x_ready "
             "dve_roots dve_k dve_q dve_tail dve_out").split()
    s = {n: sem(n) for n in names}

    with nc.Block() as block:

        @block.tensor
        def _(pe):
            for semaphore, n in loaded:
                pe.wait_ge(semaphore, n)

            def queries(t, u, g):
                if g == 0:
                    pe.wait_ge(s["xnT_ready"], t + 1)
                wait_count(pe, s["q_ready"], 4 * t + g - 1)
                for h in range(PER):
                    head = PER * g + h
                    for c in range(KC):
                        last = nc.tensor.matmul(ps_q[g % 2][:, h * P:(h + 1) * P], wq[:, c, head * DH:(head + 1) * DH],
                                                xnT[u][:, c, :], start=(c == 0), stop=(c == KC - 1))
                last.then_inc(s["q_made"], 1)

            def turn(t):
                pe.wait_ge(s["xn_ready"], t + 1)
                wait_count(pe, s["scaled_ready"], t - 1)
                for c in range(KC):
                    last = nc.tensor.transpose(ps_T[:, c * P:(c + 1) * P], xn[:, c * P:(c + 1) * P], ident)
                last.then_inc(s["turned"], 1)

            def keys(t, u):
                pe.wait_ge(s["xnT_ready"], t + 1)
                wait_count(pe, s["kT_ready"], t)
                for c in range(KC):
                    last = nc.tensor.matmul(ps_k[:, 0:DH], xnT[u][:, c, :], wkv[:, c, 0:DH], start=(c == 0), stop=(c == KC - 1))
                last.then_inc(s["k_made"], 1)

            def turn_keys(t):
                pe.wait_ge(s["k_normed"], t + 1)
                nc.tensor.transpose(ps_kT, k_norm[:, :], ident).then_inc(s["k_turned"], 1)

            def values(t):
                wait_count(pe, s["v_ready"], t)
                for b in range(TB):
                    for c in range(KC):
                        last = nc.tensor.matmul(ps_v[:, b * DH:(b + 1) * DH], xn4T[:, c, b, :, :].rearrange("p r k -> p (r k)"),
                                                wkv[:, c, DH:2 * DH], start=(c == 0), stop=(c == KC - 1))
                last.then_inc(s["v_made"], 1)

            def scores(t, u, g, more):
                if g == 0:
                    pe.wait_ge(s["kT_ready"], t + 1)
                    wait_count(pe, s["scaled_ready"], t)
                    if more:
                        pe.wait_ge(s["xnT_ready"], t + 2)
                pe.wait_ge(s["squares_ready"], 4 * t + g + 1)
                for b in range(TB):
                    at = g * TB + b
                    nc.tensor.matmul(ps_scores[:, at * SEQ:(at + 1) * SEQ], qT[:, g, b, :, :].rearrange("p h q -> p (h q)"),
                                     kT[u][:, b * SEQ:(b + 1) * SEQ], start=True, stop=True)
                    last = nc.tensor.matmul(ps_norms[:, at:at + 1], qT_squared[:, g, b, :, :].rearrange("p h q -> p (h q)"),
                                            ones, start=True, stop=True)
                last.then_inc(s["scores_made"], 1)

            def weigh(t, u, r):
                if r == 0:
                    pe.wait_ge(s["v_ready"], t + 1)
                    pe.wait_ge(s["probs_ready"], t + 1)
                wait_count(pe, s["oT_ready"], 4 * t + r)
                rows = slice(SEQ * r, SEQ * (r + 1))
                for b in range(TB):
                    last = nc.tensor.matmul(ps_o[:, :].rearrange("p (g b q) -> p g b q", g=GROUPS, b=TB)[:, :, b, :],
                                            v4[u][rows, b, :], probsT[rows, :, b, :], start=True, stop=True)
                last.then_inc(s["o_made"], 1)

            def finish(t):
                wait_count(pe, s["x_ready"], t)
                for r in range(PER):
                    pe.wait_ge(s["oT_ready"], 4 * t + r + 1)
                    for g in range(GROUPS):
                        last = nc.tensor.matmul(ps_out[:, 0:DIM], oT[:, r, g, :], wo[:, PER * g + r, :],
                                                start=(r == 0 and g == 0), stop=(r == PER - 1 and g == GROUPS - 1))
                last.then_inc(s["out_made"], 1)

            ones = consts[:, C_ONE:C_ONE + 1]

            def step(i, u, live):
                for g in range(GROUPS):
                    if live(0):
                        queries(i, u, g)
                    if live(1) and g == 0:
                        turn(i + 1)
                    if live(1) and g == 2:
                        keys(i + 1, 1 - u)
                    if live(0) and g >= 1:
                        scores(i, u, g - 1, live(1))
                    if live(-1):
                        weigh(i - 1, 1 - u, g)
                if live(1):
                    values(i + 1)
                    turn_keys(i + 1)
                if live(0):
                    scores(i, u, GROUPS - 1, live(1))
                if live(-1):
                    finish(i - 1)

            run_steps(pe, step, -1, TILES, 2, TILES - 2)

        @block.scalar
        def _(act):
            for semaphore, n in loaded:
                act.wait_ge(semaphore, n)

            def queries_out(t, g):
                act.wait_ge(s["q_made"], 4 * t + g + 1)
                nc.scalar.copy(qT[:, g, :, :, :].rearrange("p b h q -> p h b q"),
                               ps_q[g % 2][:, :].rearrange("p (h b q) -> p h b q", h=PER, b=TB)).then_inc(s["q_ready"], 1)

            def turned_out(t, u):
                act.wait_ge(s["turned"], t + 1)
                nc.scalar.copy(xnT[u][:, :, :], ps_T[:, 0:DIM].rearrange("p (c t) -> p c t", c=KC))
                for c in range(KC):
                    last = nc.scalar.copy(xn4T[:, c, :, :, :], ps_T[:, c * P:(c + 1) * P].rearrange("p (b k) -> p b k", b=TB)
                                          .unsqueeze(2).to_broadcast([P, TB, 4, SEQ]))
                last.then_inc(s["xnT_ready"], 1)

            def key_sums(t):
                act.wait_ge(s["k_made"], t + 1)
                nc.scalar.activation(k_squared[:, :], ps_k[:, 0:DH], ACT.Square, accum_out=k_sum[:, :]).then_inc(s["k_sum_ready"], 1)

            def keys_out(t, u):
                act.wait_ge(s["k_turned"], t + 1)
                nc.scalar.copy(kT[u][:, :], ps_kT).then_inc(s["kT_ready"], 1)

            def outputs_out(t, r):
                act.wait_ge(s["o_made"], 4 * t + r + 1)
                nc.scalar.copy(oT[:, r, :, :], ps_o[:, :].rearrange("p (g t) -> p g t", g=GROUPS)).then_inc(s["oT_ready"], 1)

            def values_out(t, u):
                act.wait_ge(s["v_made"], t + 1)
                nc.scalar.copy(v4[u][:, :, :], ps_v[:, :].rearrange("p (b d) -> p b d", b=TB)).then_inc(s["v_ready"], 1)

            def exponentials(t):
                act.wait_ge(s["scaled_ready"], t + 1)
                nc.scalar.activation(exps[:, :, :], scaled[:, :, :], ACT.Exp).then_inc(s["exps_ready"], 1)

            def step(i, u, live):
                for g in range(GROUPS):
                    if live(0):
                        queries_out(i, g)
                    if live(1) and g == 0:
                        turned_out(i + 1, 1 - u)
                    if live(1) and g == 2:
                        key_sums(i + 1)
                    if live(-1):
                        outputs_out(i - 1, g)
                if live(1):
                    values_out(i + 1, 1 - u)
                    keys_out(i + 1, 1 - u)
                if live(0):
                    exponentials(i)

            run_steps(act, step, -1, TILES, 2, TILES - 2)

        @block.gpsimd
        def _(pool):
            def step(i, u, live):
                for g in range(GROUPS):
                    if live(0):
                        pool.wait_ge(s["q_ready"], 4 * i + g + 1)
                        flat = qT[:, g, :, :, :].rearrange("p b h q -> p (b h q)")
                        nc.gpsimd.tensor_tensor(qT_squared[:, g, :, :, :].rearrange("p b h q -> p (b h q)"), flat, flat,
                                                ALU.mult).then_inc(s["squares_ready"], 1)

            run_steps(pool, step, 0, TILES - 1, 0, TILES - 1, 1)

        @block.vector
        def _(dve):
            k_link, q_link = (Link(dve, s["dve_k"], Root.LINKS + 1),
                                  Link(dve, s["dve_q"], Root.LINKS + 4))
            tail, out_link = Link(dve, s["dve_tail"], 3), Link(dve, s["dve_out"], RowNorm.LINKS + 2)
            for semaphore, n in loaded:
                dve.wait_ge(semaphore, n)
            moments.roots(dve, s["dve_roots"], EPS_LN2, 1.0 + LN_EPS)

            def normalise(t):
                moments.apply(t, row(x_sb, t), xn[:, :]).then_inc(s["xn_ready"], 1)

            def normalise_keys(t):
                dve.wait_ge(s["k_sum_ready"], t + 1)
                k_link.tile(t)
                k_link(nc.vector.tensor_scalar(k_work[:, 0:1], k_sum[:, :], eps_l2, None, ALU.add))
                rstd = k_root(k_link)
                k_link.end()
                nc.vector.tensor_scalar(k_norm[:, :], ps_k[:, 0:DH], rstd, 256.0, ALU.mult, ALU.mult).then_inc(s["k_normed"], 1)

            def softmax_head(t):
                dve.wait_ge(s["scores_made"], 4 * t + 4)
                q_link.tile(t)
                q_link(nc.vector.tensor_scalar(q_work[:, 0:HEADS], ps_norms, 256.0, eps_l2, ALU.mult, ALU.add))
                rstd = q_root(q_link)
                nc.vector.tensor_tensor(scaled[:, :, :], ps_scores[:, :].rearrange("p (h k) -> p h k", h=HEADS),
                                        rstd.unsqueeze(2).to_broadcast([P, HEADS, SEQ]), ALU.mult).then_inc(s["scaled_ready"], 1)
                q_link.end()

            def softmax_tail(t):
                dve.wait_ge(s["exps_ready"], t + 1)
                tail.tile(t)
                tail(nc.vector.reduce_sum(total[:, :], exps[:, :, :], axis=X_AXIS))
                tail(nc.vector.reciprocal(inverse[:, :], total[:, :]))
                tail(nc.vector.tensor_tensor(probs[:, :].rearrange("p (h k) -> p h k", h=HEADS), exps[:, :, :],
                                             inverse[:, :].unsqueeze(2).to_broadcast([P, HEADS, SEQ]), ALU.mult))
                nc.vector.transpose(probsT[:, :, :, :].rearrange("p g b q -> p (g b q)"), probs[:, :]).then_inc(s["probs_ready"], 1)
                tail.end()

            def residual(t):
                dve.wait_ge(s["out_made"], t + 1)
                out_link.tile(t)
                out_link(out_norm(out_link, ps_out[:, 0:DIM], out_normed[:, :]))
                out_link(nc.vector.tensor_tensor(out_scaled[:, :], out_normed[:, :], g_out[:, :], ALU.mult))
                nc.vector.tensor_tensor(row(x_sb, t), row(x_sb, t), out_scaled[:, :], ALU.add).then_inc(s["x_ready"], 1)
                out_link.end()
                dve.wait_ge(s["x_ready"], t + 1)
                moments.take(t, row(x_sb, t))

            eps_l2 = consts[:, C_LN + EPS_L2:C_LN + EPS_L2 + 1]

            def step(i, u, live):
                if live(1):
                    normalise_keys(i + 1)
                if live(2):
                    normalise(i + 2)
                if live(0):
                    softmax_head(i)
                    softmax_tail(i)
                if live(-1):
                    residual(i - 1)

            run_steps(dve, step, -2, TILES, 2, TILES - 3)


def block_routed_ffn(nc, name, scope, moments, x_sb, consts, ident, loaded, wr, br, w1, w2, sel16, background=None):
    sb, pb, sem = scope(name)
    blocks, top_k, chunks = 16, 4, 8
    xn = sb("xn", [P, DIM])
    xnT = sb("xnT", [P, KC, P])
    logits = sb("logits", [P, blocks])
    above = sb("above", [P, blocks, blocks])
    level = sb("level", [P, blocks, blocks])
    tied = sb("tied", [P, blocks, blocks])
    beaten = sb("beaten", [P, blocks, blocks])
    rank = sb("rank", [P, blocks])
    mask = sb("mask", [P, blocks])
    maskT = sb("maskT", [blocks, P], BF16)
    hidden = [sb(f"hidden{u}", [P, chunks, P]) for u in range(2)]
    masked = [sb(f"masked{u}", [P, chunks, P]) for u in range(2)]

    ps_T, ps_router, ps_out = pb("ps_T"), pb("ps_router"), pb("ps_out")
    ps_h = [pb("ps_h0"), pb("ps_h1")]
    ps_mask = pb("ps_mask", 1024)

    names = ("xn_ready turned xnT_ready logits_made mask_ready mask_turned maskT_ready h_made h_ready spread masked_ready "
             "out_made x_ready dve_roots dve_router").split()
    s = {n: sem(n) for n in names}

    with nc.Block() as block:
        if background:
            block.sync(background)

        @block.tensor
        def _(pe):
            for semaphore, n in loaded:
                pe.wait_ge(semaphore, n)

            def turn(t):
                pe.wait_ge(s["xn_ready"], t + 1)
                for c in range(KC):
                    last = nc.tensor.transpose(ps_T[:, c * P:(c + 1) * P], xn[:, c * P:(c + 1) * P], ident)
                last.then_inc(s["turned"], 1)

            def route(t):
                pe.wait_ge(s["xnT_ready"], t + 1)
                for c in range(KC):
                    last = nc.tensor.matmul(ps_router[:, 0:blocks], xnT[:, c, :], wr[:, c, :], start=(c == 0), stop=(c == KC - 1))
                last.then_inc(s["logits_made"], 1)

            def turn_mask(t):
                pe.wait_ge(s["mask_ready"], t + 1)
                nc.tensor.transpose(ps_router[0:blocks, P:2 * P], mask[:, :], ident).then_inc(s["mask_turned"], 1)

            def up(t):
                for half in range(2):
                    wait_count(pe, s["h_ready"], 2 * t + half - 1)
                    for j in range(chunks // 2):
                        f = half * chunks // 2 + j
                        for c in range(KC):
                            last = nc.tensor.matmul(ps_h[half][:, j * P:(j + 1) * P], w1[:, c, f * P:(f + 1) * P], xnT[:, c, :],
                                                    start=(c == 0), stop=(c == KC - 1))
                    last.then_inc(s["h_made"], 1)

            def spread(t):
                pe.wait_ge(s["maskT_ready"], t + 1)
                wait_count(pe, s["masked_ready"], t)
                for f in range(chunks):
                    last = nc.tensor.matmul(ps_mask[:, f * P:(f + 1) * P], sel16[:, f * P:(f + 1) * P], maskT[:, :],
                                            start=True, stop=True)
                last.then_inc(s["spread"], 1)

            def down(t, u):
                pe.wait_ge(s["masked_ready"], t + 1)
                wait_count(pe, s["x_ready"], t)
                for f in range(chunks):
                    last = nc.tensor.matmul(ps_out[:, 0:DIM], masked[u][:, f, :], w2[:, f, :], start=(f == 0), stop=(f == chunks - 1))
                last.then_inc(s["out_made"], 1)

            def step(i, u, live):
                if live(0):
                    up(i)
                if live(1):
                    turn(i + 1)
                if live(-1):
                    down(i - 1, 1 - u)
                if live(0):
                    turn_mask(i)
                    spread(i)
                if live(1):
                    route(i + 1)

            run_steps(pe, step, -1, TILES, 2, TILES - 2)

        @block.scalar
        def _(act):
            def maskT_out(t):
                act.wait_ge(s["mask_turned"], t + 1)
                nc.scalar.copy(maskT[:, :], ps_router[0:blocks, P:2 * P]).then_inc(s["maskT_ready"], 1)

            def gelu(t, u):
                for half in range(2):
                    act.wait_ge(s["h_made"], 2 * t + half + 1)
                    n = chunks // 2
                    nc.scalar.activation(hidden[u][:, half * n:(half + 1) * n, :], ps_h[half][:, :].rearrange("p (f t) -> p f t", f=n),
                                         ACT.Gelu).then_inc(s["h_ready"], 1)

            def turned_out(t):
                act.wait_ge(s["turned"], t + 1)
                nc.scalar.copy(xnT[:, :, :], ps_T[:, 0:DIM].rearrange("p (c t) -> p c t", c=KC)).then_inc(s["xnT_ready"], 1)

            def step(i, u, live):
                if live(0):
                    gelu(i, u)
                if live(1):
                    turned_out(i + 1)
                if live(0):
                    maskT_out(i)

            run_steps(act, step, -1, TILES - 1, 2, TILES - 2)

        @block.vector
        def _(dve):
            router = Link(dve, s["dve_router"], 5)
            for semaphore, n in loaded:
                dve.wait_ge(semaphore, n)
            moments.roots(dve, s["dve_roots"], EPS_LN)

            def normalise(t):
                wait_count(dve, s["turned"], t)
                moments.apply(t, row(x_sb, t), xn[:, :]).then_inc(s["xn_ready"], 1)

            def choose(t):
                square = [P, blocks, blocks]
                dve.wait_ge(s["logits_made"], t + 1)
                router.tile(t)
                router(nc.vector.tensor_tensor(logits[:, :], ps_router[:, 0:blocks], br[:, :], ALU.add))
                own, other = logits[:, :].unsqueeze(2).to_broadcast(square), logits[:, :].unsqueeze(1).to_broadcast(square)
                nc.vector.tensor_tensor(above[:, :, :], other, own, ALU.is_gt)
                router(nc.vector.tensor_tensor(level[:, :, :], other, own, ALU.is_ge))
                router(nc.vector.tensor_tensor(tied[:, :, :], level[:, :, :],
                                               consts[:, C_LOWER:C_LOWER + 256].rearrange("p (i j) -> p i j", i=blocks), ALU.mult))
                router(nc.vector.tensor_tensor(beaten[:, :, :], above[:, :, :], tied[:, :, :], ALU.max))
                router(nc.vector.reduce_sum(rank[:, :], beaten[:, :, :], axis=X_AXIS))
                nc.vector.tensor_scalar(mask[:, :], rank[:, :], float(top_k), None, ALU.is_lt).then_inc(s["mask_ready"], 1)
                router.end()

            def apply_mask(t, u):
                dve.wait_ge(s["h_ready"], 2 * t + 2)
                dve.wait_ge(s["spread"], t + 1)
                nc.vector.tensor_tensor(masked[u][:, :, :].rearrange("p f t -> p (f t)"), ps_mask[:, :],
                                        hidden[u][:, :, :].rearrange("p f t -> p (f t)"), ALU.mult).then_inc(s["masked_ready"], 1)

            def residual(t):
                dve.wait_ge(s["out_made"], t + 1)
                nc.vector.tensor_tensor(row(x_sb, t), row(x_sb, t), ps_out[:, 0:DIM], ALU.add).then_inc(s["x_ready"], 1)
                dve.wait_ge(s["x_ready"], t + 1)
                moments.take(t, row(x_sb, t))

            def step(i, u, live):
                if live(-1):
                    residual(i - 1)
                if live(0):
                    apply_mask(i, u)
                if live(1):
                    choose(i + 1)
                if live(2):
                    normalise(i + 2)

            run_steps(dve, step, -2, TILES, 2, TILES - 3)

DC, DCQ, DR, HK = 64, 192, 64, 128
QC = DCQ // 2


def fold_weights(nc, name, scope, consts, ident, loaded, raw, a_w, b_w, lastT, last_roped, diag):
    sb, pb, sem = scope(name)
    half = HEADS // 2
    r1 = sb("r1", [QC, 2, half * DC])
    r2 = sb("r2", [P, half * DC])
    last_cos = sb("last_cos", [BATCH, CTX])
    last_sin = sb("last_sin", [BATCH, CTX])
    last_twice = sb("last_twice", [BATCH, 2, CTX])
    ps_r1 = [pb("ps_r1_0"), pb("ps_r1_1")]
    ps_r2, ps_last = pb("ps_r2"), pb("ps_last")
    ps_a = [pb("ps_a0"), pb("ps_a1")]
    ps_b = [pb("ps_b0"), pb("ps_b1")]
    names = "r1_made r1_ready r2_made r2_ready a_made a_ready b_made b_ready last_products last_ready last_turned last_out stored zeroed".split()
    s = {n: sem(n) for n in names}

    with nc.Block() as block:

        @block.gpsimd
        def _(pool):
            for u in range(2):
                nc.gpsimd.memset(diag[u][:, :, :], 0.0).then_inc(s["zeroed"], 1)
            for semaphore, n in loaded:
                pool.wait_ge(semaphore, n)
            low, high = slice(0, CTX // 2), slice(CTX // 2, CTX)
            kv = raw["last"]
            cos = consts[0:BATCH, C_LASTCOS:C_LASTCOS + CTX]
            sin = consts[0:BATCH, C_LASTSIN:C_LASTSIN + CTX]
            nc.gpsimd.tensor_tensor(last_cos[:, :], kv[:, :], cos, ALU.mult).then_inc(s["last_products"], 1)
            nc.gpsimd.tensor_tensor(last_sin[:, low], kv[:, high], sin[:, low], ALU.mult).then_inc(s["last_products"], 1)
            nc.gpsimd.tensor_tensor(last_sin[:, high], kv[:, low], sin[:, high], ALU.mult).then_inc(s["last_products"], 1)
            pool.wait_ge(s["last_products"], 3)
            for n in range(2):
                nc.gpsimd.tensor_tensor(last_twice[:, n, :], last_cos[:, :], last_sin[:, :], ALU.add).then_inc(s["last_ready"], 1)

        @block.sync
        def _(sp):
            sp.wait_ge(s["last_ready"], 2)
            sp.dma_start(last_roped, last_twice[:, 0, :]).then_inc(s["stored"], 16)
            sp.wait_ge(s["stored"], 16)

        @block.tensor
        def _(pe):
            for semaphore, n in loaded:
                pe.wait_ge(semaphore, n)

            def out_weights(pair):
                if pair >= 2:
                    pe.wait_ge(s["b_ready"], pair - 1)
                for n in range(2):
                    for odd in range(2):
                        h = 4 * pair + 2 * n + odd
                        last = nc.tensor.matmul(ps_b[pair % 2][64 * odd:64 * odd + 64, n * DIM:(n + 1) * DIM],
                                                raw["ckv"][:, h, :], raw["o"][:, h, :], start=True, stop=True)
                last.then_inc(s["b_made"], 1)

            for g in range(2):
                if g:
                    pe.wait_ge(s["r1_ready"], g)
                for j in range(2):
                    for n in range(half):
                        h = g * half + n
                        last = nc.tensor.matmul(ps_r1[j][0:QC, n * DC:(n + 1) * DC], raw["qr"][:, h, j * QC:(j + 1) * QC],
                                                raw["kr"][:, h, :], start=True, stop=True)
                last.then_inc(s["r1_made"], 1)
                out_weights(2 * g)
                pe.wait_ge(s["r1_ready"], g + 1)
                if g:
                    pe.wait_ge(s["r2_ready"], g)
                for n in range(half):
                    for j in range(2):
                        last = nc.tensor.matmul(ps_r2[:, n * DC:(n + 1) * DC], raw["cq"][:, j, g * half + n, :],
                                                r1[:, j, n * DC:(n + 1) * DC], start=(j == 0), stop=(j == 1))
                last.then_inc(s["r2_made"], 1)
                out_weights(2 * g + 1)
                pe.wait_ge(s["r2_ready"], g + 1)
                if g:
                    pe.wait_ge(s["a_ready"], g)
                for c in range(KC):
                    for n in range(half):
                        last = nc.tensor.matmul(ps_a[c][:, n * DC:(n + 1) * DC], raw["q"][:, g * half + n, c * P:(c + 1) * P],
                                                r2[:, n * DC:(n + 1) * DC], start=True, stop=True)
                last.then_inc(s["a_made"], 1)
            pe.wait_ge(s["last_ready"], 2)
            nc.tensor.transpose(ps_last[:, 0:BATCH], last_twice[:, :, :].rearrange("b n d -> b (n d)"),
                                ident[0:BATCH, 0:BATCH]).then_inc(s["last_turned"], 1)

        @block.vector
        def _(dve):
            for g in range(2):
                dve.wait_ge(s["r1_made"], g + 1)
                if g:
                    dve.wait_ge(s["r2_made"], g)
                for j in range(2):
                    last = nc.vector.tensor_copy(r1[:, j, :], ps_r1[j][0:QC, :])
                last.then_inc(s["r1_ready"], 1)
                dve.wait_ge(s["r2_made"], g + 1)
                if g:
                    dve.wait_ge(s["a_made"], g)
                nc.vector.tensor_copy(r2[:, :], ps_r2[:, :]).then_inc(s["r2_ready"], 1)
                dve.wait_ge(s["a_made"], g + 1)
                for c in range(KC):
                    last = nc.vector.tensor_copy(a_w[:, c, g * half * DC:(g + 1) * half * DC], ps_a[c][:, :])
                last.then_inc(s["a_ready"], 1)

        @block.scalar
        def _(act):
            for pair in range(4):
                act.wait_ge(s["b_made"], pair + 1)
                nc.scalar.copy(b_w[:, 2 * pair:2 * pair + 2, :].rearrange("p m n -> p (m n)"), ps_b[pair % 2][:, :])\
                  .then_inc(s["b_ready"], 1)
            act.wait_ge(s["last_turned"], 1)
            nc.scalar.copy(lastT[:, :], ps_last[:, 0:BATCH]).then_inc(s["last_out"], 1)


def latent_attention(nc, name, scope, moments, x_sb, consts, ident, ctx_d, last_roped, a_w, b_w, lastT, diag, background=None):
    sb, pb, sem = scope(name)
    blocks = 4
    nkeys = KEYS - 1
    xn = sb("xn", [P, DIM])
    xnT = sb("xnT", [P, KC, P])
    qT = [sb(f"qT{u}", [P, TB, HEADS // 2, SEQ]) for u in range(2)]
    kv_raw = [sb(f"kv_raw{u}", [P, TB, 2 * CTX]) for u in range(2)]
    kv_cos = sb("kv_cos", [P, TB, 2 * CTX])
    kv_sin = sb("kv_sin", [P, TB, 2, CTX])
    kv = [sb(f"kv{u}", [P, TB, 2, 2, CTX]) for u in range(2)]
    kT = [sb(f"kT{u}", [P, TB, KEYS]) for u in range(2)]
    exps = [sb(f"exps{u}", [P, blocks, KEYS]) for u in range(2)]
    top = sb("top", [P, blocks])
    total = [sb(f"total{u}", [P, blocks]) for u in range(2)]
    inverse = [sb(f"inverse{u}", [P, blocks]) for u in range(2)]
    expsT = [[sb(f"expsT{u}{j}", [P, blocks, P]) for j in range(2)] for u in range(2)]
    lastT_exps = [sb(f"last_exps{u}", [blocks, P]) for u in range(2)]
    ctx = sb("ctx", [P, TB, blocks, CTX])
    ctxT = sb("ctxT", [P, HEADS // 2, TB, SEQ])

    ps_scores = pb("ps_scores", 2048)
    ps_t = [pb("ps_t0"), pb("ps_t1")]
    ps_o, ps_m = pb("ps_o"), pb("ps_m")

    names = ("xn_ready turned xnT_ready q_made q_out k_turned k_out kv_ready scores_made top_ready exps_ready "
             "last_turned last_out turned0 turned1 out0 out1 weighed ctx_ready c_turned c_out out_made x_ready "
             "raw_in0 raw_in1 diag_in0 diag_in1 dve_roots pool_rope dve_inverse").split()
    s = {n: sem(n) for n in names}

    with nc.Block() as block:

        @block.sync
        def _(sp):
            def step(t, u, live):
                wait_count(sp, s["pool_rope"], t - 1)
                sp.dma_start(kv_raw[u][:, :, :], ctx_d[bass.ds(t * TB, TB), 0:nkeys * CTX].rearrange("b (p n) -> p b n", p=P))\
                  .then_inc(s[f"raw_in{u}"], 16)
                wait_count(sp, s["weighed"], TB * (t - 1))
                for n in range(blocks):
                    sp.dma_start(diag[u][n:n + 1, :, n * CTX:(n + 1) * CTX], last_roped[bass.ds(t * TB, TB), :].unsqueeze(0))\
                      .then_inc(s[f"diag_in{u}"], 16)

            run_steps(sp, step, 0, TILES - 1, 2, TILES - 1)
            if background:
                background(sp)

        @block.gpsimd
        def _(pool):
            rope = Link(pool, s["pool_rope"], 1)
            low, high = slice(0, CTX // 2), slice(CTX // 2, CTX)
            cos = consts[:, C_COS:C_COS + 2 * CTX].unsqueeze(1).to_broadcast([P, TB, 2 * CTX])
            sin = consts[:, C_SIN:C_SIN + 2 * CTX].rearrange("p (j d) -> p j d", j=2)

            def step(t, u, live):
                pool.wait_ge(s[f"raw_in{u}"], 8 * t + 16 - 8 * u)
                if not isinstance(t, int) or t > 0:
                    pool.wait_ge(s["kv_ready"], t)
                rope.tile(t)
                raw = kv_raw[u][:, :, :].rearrange("p b (j d) -> p b j d", j=2)
                nc.gpsimd.tensor_tensor(kv_cos[:, :, :], kv_raw[u][:, :, :], cos, ALU.mult)
                for to, come in ((low, high), (high, low)):
                    last = nc.gpsimd.tensor_tensor(kv_sin[:, :, :, to], raw[:, :, :, come],
                                                   sin[:, :, to].unsqueeze(1).to_broadcast([P, TB, 2, CTX // 2]), ALU.mult)
                rope(last)
                rope.end()
                wait_count(pool, s["weighed"], TB * (t - 1))
                twice = [P, TB * 2, 2, CTX]
                nc.gpsimd.tensor_tensor(kv[u][:, :, :, :, :].rearrange("p b j n d -> p (b j) n d"),
                                        kv_cos[:, :, :].rearrange("p b (j d) -> p (b j) d", j=2).unsqueeze(2).to_broadcast(twice),
                                        kv_sin[:, :, :, :].rearrange("p b j d -> p (b j) d").unsqueeze(2).to_broadcast(twice),
                                        ALU.add).then_inc(s["kv_ready"], 1)

            run_steps(pool, step, 0, TILES - 1, 2, TILES - 1)

        @block.tensor
        def _(pe):
            def turn(t):
                pe.wait_ge(s["xn_ready"], t + 1)
                wait_count(pe, s["k_out"], 2 * t)
                wait_count(pe, s["x_ready"], t - 2)
                for c in range(KC):
                    last = nc.tensor.transpose(ps_m[:, c * P:(c + 1) * P], xn[:, c * P:(c + 1) * P], ident)
                last.then_inc(s["turned"], 1)

            def queries(t, part):
                if part == 0:
                    pe.wait_ge(s["xnT_ready"], t + 1)
                else:
                    pe.wait_ge(s["q_out"], 2 * t + 1)
                for n in range(4):
                    m = 4 * part + n
                    for c in range(KC):
                        last = nc.tensor.matmul(ps_m[:, n * P:(n + 1) * P], a_w[:, c, m * P:(m + 1) * P], xnT[:, c, :],
                                                start=(c == 0), stop=(c == KC - 1))
                last.then_inc(s["q_made"], 1)

            def keys(t, u, part):
                pe.wait_ge(s["kv_ready"], t + 1)
                for b in range(2):
                    for j in range(2):
                        last = nc.tensor.transpose(ps_m[:, (2 * b + j) * P:(2 * b + j + 1) * P],
                                                   kv[u][:, 2 * part + b, j, :, :].rearrange("p n d -> p (n d)"), ident)
                last.then_inc(s["k_turned"], 1)

            def turn_ctx(t, part):
                pe.wait_ge(s["ctx_ready"], TB * t + 2 * part + 2)
                for b in range(2):
                    for n in range(2):
                        last = nc.tensor.transpose(ps_m[:, (2 * b + n) * P:(2 * b + n + 1) * P],
                                                   ctx[:, 2 * part + b, 2 * n:2 * n + 2, :].rearrange("p k d -> p (k d)"), ident)
                last.then_inc(s["c_turned"], 1)

            def finish(t):
                pe.wait_ge(s["c_out"], 2 * t + 2)
                for m in range(HEADS // 2):
                    last = nc.tensor.matmul(ps_m[:, 0:DIM], ctxT[:, m, :, :].rearrange("p b s -> p (b s)"), b_w[:, m, :],
                                            start=(m == 0), stop=(m == HEADS // 2 - 1))
                last.then_inc(s["out_made"], 1)

            def scores(t, u, b):
                if b == 0:
                    pe.wait_ge(s["q_out"], 2 * t + 2)
                    pe.wait_ge(s["k_out"], 2 * t + 2)
                for k in range(blocks):
                    wait_count(pe, s["exps_ready"], 4 * (TB * t + b) - 3 + k)
                    rows = slice(64 * (k % 2), 64 * (k % 2) + 64)
                    last = nc.tensor.matmul(ps_scores[:, 512 * k:512 * k + KEYS],
                                            qT[u][rows, b, 4 * (k // 2):4 * (k // 2) + 4, :].rearrange("p m q -> p (m q)"),
                                            kT[u][rows, b, :], start=True, stop=True)
                last.then_inc(s["scores_made"], 1)

            def turn_exps(n, v):
                pe.wait_ge(s["exps_ready"], 4 * n + 4)
                if isinstance(n, int) and n == 1:
                    pe.wait_ge(s["last_out"], 1)
                wait_count(pe, s["ctx_ready"], n - 1)
                nc.tensor.transpose(ps_o[0:blocks, DIM:DIM + P], exps[v][:, :, KEYS - 1], ident).then_inc(s["last_turned"], 1)
                for j in range(2):
                    wait_count(pe, s[f"out{j}"], n)
                    for k in range(blocks):
                        last = nc.tensor.transpose(ps_t[j][:, k * P:(k + 1) * P], exps[v][:, k, j * P:(j + 1) * P], ident)
                    last.then_inc(s[f"turned{j}"], 1)

            def weigh(n, v, t_par, diag_count, b, is_last):
                if is_last:
                    pe.wait_ge(s["ctx_ready"], n)
                else:
                    pe.wait_ge(s["last_out"], n + 2)
                for j in range(2):
                    pe.wait_ge(s[f"out{j}"], n + 1)
                if b == 0:
                    pe.wait_ge(s[f"diag_in{t_par}"], diag_count)
                nc.tensor.matmul(ps_o[:, 0:DIM], lastT_exps[v][:, :], diag[t_par][:, b, :], start=True, stop=False,
                                 skip_group_check=True)
                for k in range(blocks):
                    for j in range(2):
                        last = nc.tensor.matmul(ps_o[:, k * CTX:(k + 1) * CTX], expsT[v][j][:, k, :], kv[t_par][:, b, j, 0, :],
                                                start=False, stop=(j == 1), skip_group_check=True)
                last.then_inc(s["weighed"], 1)

            def step(t, u, live):
                for b in range(TB):
                    if live(0):
                        scores(t, u, b)
                    if b == 0 and live(1):
                        turn(t + 1)
                    if b == 1 and live(1):
                        queries(t + 1, 1)
                    if b == 2 and live(1):
                        if live(-1):
                            pe.wait_ge(s["c_out"], 2 * t - 1)
                        else:
                            pe.wait_ge(s["q_out"], 2 * t + 4)
                        keys(t + 1, 1 - u, 0)
                    if b == 3 and live(1):
                        if live(-1):
                            pe.wait_ge(s["c_out"], 2 * t)
                        else:
                            pe.wait_ge(s["k_out"], 2 * t + 3)
                        keys(t + 1, 1 - u, 1)
                    if live(0) if b else live(-1):
                        turn_exps(TB * t + b - 1, (b - 1) % 2)
                    if live(0) if b >= 2 else live(-1):
                        tile_d = 0 if b >= 2 else -1
                        tu = u if b >= 2 else 1 - u
                        is_last = b == 1 and not live(0)
                        weigh(TB * t + b - 2, b % 2, tu, 32 * (t + tile_d) + 64 - 32 * tu, (b - 2) % TB, is_last)
                    if b == 0 and live(1):
                        queries(t + 1, 0)
                    if b == 1 and live(-1):
                        if live(1):
                            pe.wait_ge(s["q_out"], 2 * t + 4)
                        else:
                            wait_count(pe, s["x_ready"], t - 1)
                            pe.wait_ge(s["k_out"], 2 * TILES)
                        turn_ctx(t - 1, 0)
                    if b == 2 and live(-1):
                        if live(1):
                            pe.wait_ge(s["k_out"], 2 * t + 3)
                        else:
                            pe.wait_ge(s["c_out"], 2 * t - 1)
                        turn_ctx(t - 1, 1)
                    if b == 3 and live(-1):
                        if live(1):
                            pe.wait_ge(s["k_out"], 2 * t + 4)
                        finish(t - 1)

            run_steps(pe, step, -1, TILES, 3, TILES - 2)

        @block.scalar
        def _(act):
            def exponentials(t, b, k):
                if k == 0:
                    act.wait_ge(s["top_ready"], TB * t + b + 1)
                v = b % 2
                nc.scalar.activation(exps[v][:, k, :], ps_scores[:, 512 * k:512 * k + KEYS], ACT.Exp, bias=top[:, k:k + 1],
                                     accum_out=total[v][:, k:k + 1]).then_inc(s["exps_ready"], 1)

            def turned_out(t):
                act.wait_ge(s["turned"], t + 1)
                nc.scalar.copy(xnT[:, :, :], ps_m[:, 0:DIM].rearrange("p (c t) -> p c t", c=KC)).then_inc(s["xnT_ready"], 1)

            def queries_out(t, u, part):
                act.wait_ge(s["q_made"], 2 * t + part + 1)
                nc.scalar.copy(qT[u][:, :, 4 * part:4 * part + 4, :].rearrange("p b m q -> p m b q"),
                               ps_m[:, :].rearrange("p (m b q) -> p m b q", m=4, b=TB)).then_inc(s["q_out"], 1)

            def keys_out(t, u, part):
                if part == 0:
                    nc.scalar.copy(kT[u][:, :, KEYS - 1], lastT[:, bass.ds(t * TB, TB)])
                act.wait_ge(s["k_turned"], 2 * t + part + 1)
                nc.scalar.copy(kT[u][:, 2 * part:2 * part + 2, 0:nkeys], ps_m[:, :].rearrange("p (b n) -> p b n", b=2))\
                  .then_inc(s["k_out"], 1)

            def ctx_out(t, part):
                act.wait_ge(s["c_turned"], 2 * t + part + 1)
                nc.scalar.copy(ctxT[:, :, 2 * part:2 * part + 2, :].rearrange("p m b s -> p b m s"),
                               ps_m[:, :].rearrange("p (b m s) -> p b m s", b=2, m=HEADS // 2)).then_inc(s["c_out"], 1)

            def exps_out(n, v):
                act.wait_ge(s["turned1"], n + 1)
                nc.scalar.copy(expsT[v][1][:, :, :], ps_t[1][:, :].rearrange("p (k q) -> p k q", k=blocks)).then_inc(s["out1"], 1)

            def step(t, u, live):
                for b in range(TB):
                    if live(0):
                        exponentials(t, b, 0)
                        exponentials(t, b, 1)
                    if b == 0 and live(1):
                        turned_out(t + 1)
                    if b == 1 and live(1):
                        queries_out(t + 1, 1 - u, 1)
                    if b >= 2 and live(1):
                        keys_out(t + 1, 1 - u, b - 2)
                    if live(0):
                        exponentials(t, b, 2)
                        exponentials(t, b, 3)
                    if live(0) if b else live(-1):
                        exps_out(TB * t + b - 1, (b - 1) % 2)
                    if b == 0 and live(1):
                        queries_out(t + 1, 1 - u, 0)
                    if b in (1, 2) and live(-1):
                        ctx_out(t - 1, b - 1)

            run_steps(act, step, -1, TILES, 2, TILES - 2)

        @block.vector
        def _(dve):
            moments.roots(dve, s["dve_roots"], EPS_LN)

            def normalise(t):
                wait_count(dve, s["turned"], t)
                moments.apply(t, row(x_sb, t), xn[:, :]).then_inc(s["xn_ready"], 1)

            def maxima(n):
                dve.wait_ge(s["scores_made"], n + 1)
                view = ps_scores[:, :].rearrange("p (k n) -> p k n", k=blocks)[:, :, 0:KEYS]
                nc.vector.tensor_reduce(top[:, :], view, X_AXIS, ALU.max, negate=True).then_inc(s["top_ready"], 1)

            def exps_out(n, v):
                dve.wait_ge(s["last_turned"], n + 1)
                nc.vector.tensor_copy(lastT_exps[v][:, :], ps_o[0:blocks, DIM:DIM + P]).then_inc(s["last_out"], 1)
                nc.vector.reciprocal(inverse[v][:, :], total[v][:, :]).then_inc(s["dve_inverse"], 1)
                dve.wait_ge(s["turned0"], n + 1)
                nc.vector.tensor_copy(expsT[v][0][:, :, :], ps_t[0][:, :].rearrange("p (k q) -> p k q", k=blocks))\
                  .then_inc(s["out0"], 1)

            def ctx_out(n, v, b):
                dve.wait_ge(s["weighed"], n + 1)
                dve.wait_ge(s["dve_inverse"], n + 1)
                nc.vector.tensor_tensor(ctx[:, b, :, :], ps_o[:, 0:DIM].rearrange("p (k d) -> p k d", k=blocks),
                                        inverse[v][:, :].unsqueeze(2).to_broadcast([P, blocks, CTX]), ALU.mult)\
                  .then_inc(s["ctx_ready"], 1)

            def residual(t):
                dve.wait_ge(s["out_made"], t + 1)
                nc.vector.tensor_tensor(row(x_sb, t), row(x_sb, t), ps_m[:, 0:DIM], ALU.add).then_inc(s["x_ready"], 1)
                dve.wait_ge(s["x_ready"], t + 1)
                moments.take(t, row(x_sb, t))

            def step(t, u, live):
                for b in range(TB):
                    if live(0):
                        maxima(TB * t + b)
                    if live(0) if b else live(-1):
                        exps_out(TB * t + b - 1, (b - 1) % 2)
                    if live(0) if b >= 2 else live(-1):
                        ctx_out(TB * t + b - 2, b % 2, (b - 2) % TB)
                    if b == 2 and live(2):
                        normalise(t + 2)
                    if b == 3 and live(-1):
                        residual(t - 1)

            run_steps(dve, step, -2, TILES, 2, TILES - 3)

EXPERTS, INNER = 8, 512
SLOTS = TILES + EXPERTS - 1


def route_tokens(nc, name, scope, moments, x_sb, consts, ident, loaded, router_w, xn_all, best_prob, position, slot_expert, sorted_x):
    sb, pb, sem = scope(name)
    flat = TILES * EXPERTS
    xn = sb("xn", [P, DIM])
    xnT = sb("xnT", [P, KC, P])
    ones = sb("ones", [P, P])
    logits, exps, denominator, prob, score, own, counts, sum_a, sum_b, rows = (
        sb(n, [P, TILES, EXPERTS]) for n in "logits exps denominator prob score own counts sum_a sum_b rows".split())
    started = sb("started", [P, EXPERTS, TILES])
    needed, end_a, end_b, base = (sb(n, [P, EXPERTS]) for n in "needed end_a end_b base".split())
    best = sb("best", [P, TILES])
    row_of = sb("row_of", [P, TILES])
    passed = sb("passed", [P, SLOTS, EXPERTS])
    slot_sum = sb("slot_sum", [P, SLOTS])
    ps_T, ps_logits, ps_before, ps_counts = pb("ps_T"), pb("ps_logits"), pb("ps_before"), pb("ps_counts")
    names = "xn_ready turned xnT_ready xn_kept logits_made logits_out exps_ready chosen counted placed ones_ready dve_roots dve_route scattered".split()
    s = {n: sem(n) for n in names}

    with nc.Block() as block:

        @block.tensor
        def _(pe):
            for semaphore, n in loaded:
                pe.wait_ge(semaphore, n)

            def step(t, u, live):
                pe.wait_ge(s["xn_ready"], t + 1)
                for c in range(KC):
                    last = nc.tensor.transpose(ps_T[:, c * P:(c + 1) * P], xn[:, c * P:(c + 1) * P], ident)
                last.then_inc(s["turned"], 1)
                pe.wait_ge(s["xnT_ready"], t + 1)
                wait_count(pe, s["logits_out"], t)
                for c in range(KC):
                    last = nc.tensor.matmul(ps_logits[:, 0:EXPERTS], xnT[:, c, :], router_w[:, c, :], start=(c == 0), stop=(c == KC - 1))
                last.then_inc(s["logits_made"], 1)

            run_steps(pe, step, 0, TILES - 1, 2, TILES - 1)
            pe.wait_ge(s["chosen"], 1)
            pe.wait_ge(s["ones_ready"], 1)
            chosen = own[:, :, :].rearrange("p t e -> p (t e)")
            nc.tensor.matmul(ps_before[:, 0:flat], consts[:, C_BEFORE:C_BEFORE + P], chosen, start=True, stop=True)
            nc.tensor.matmul(ps_counts[:, 0:flat], ones[:, :], chosen, start=True, stop=True).then_inc(s["counted"], 1)

        @block.scalar
        def _(act):
            def step(t, u, live):
                act.wait_ge(s["turned"], t + 1)
                nc.scalar.copy(xnT[:, :, :], ps_T[:, 0:DIM].rearrange("p (c t) -> p c t", c=KC)).then_inc(s["xnT_ready"], 1)
                nc.scalar.copy(row(xn_all, t), xn[:, :]).then_inc(s["xn_kept"], 1)

            run_steps(act, step, 0, TILES - 1, 0, TILES - 1, 1)
            act.wait_ge(s["logits_out"], TILES)
            nc.scalar.activation(exps[:, :, :], logits[:, :, :], ACT.Exp, scale=-1.0).then_inc(s["exps_ready"], 1)

        @block.vector
        def _(dve):
            nc.vector.memset(ones[:, :], 1.0).then_inc(s["ones_ready"], 1)
            for semaphore, n in loaded:
                dve.wait_ge(semaphore, n)
            moments.roots(dve, s["dve_roots"], EPS_LN)

            def step(t, u, live):
                if live(1):
                    wait_count(dve, s["xn_kept"], t + 1)
                    moments.apply(t + 1, row(x_sb, t + 1), xn[:, :]).then_inc(s["xn_ready"], 1)
                if live(0):
                    dve.wait_ge(s["logits_made"], t + 1)
                    nc.vector.tensor_copy(row(logits, t), ps_logits[:, 0:EXPERTS]).then_inc(s["logits_out"], 1)

            run_steps(dve, step, -1, TILES - 1, 1, TILES - 2)

            link = Link(dve, s["dve_route"], 64)
            link.tile(0)
            v = nc.vector
            wide = [P, TILES, EXPERTS]
            dve.wait_ge(s["exps_ready"], 1)
            link(v.tensor_scalar(denominator[:, :, :], exps[:, :, :], 1.0, None, ALU.add))
            link(v.reciprocal(prob[:, :, :], denominator[:, :, :]))
            link(v.reduce_max(best_prob[:, :], prob[:, :, :], axis=X_AXIS))
            link(v.tensor_tensor(own[:, :, :], prob[:, :, :], best_prob[:, :].unsqueeze(2).to_broadcast(wide), ALU.is_equal))
            link(v.tensor_tensor(score[:, :, :], own[:, :, :],
                                 consts[:, C_RANKS:C_RANKS + EXPERTS].unsqueeze(1).to_broadcast(wide), ALU.mult))
            link(v.reduce_max(best[:, :], score[:, :, :], axis=X_AXIS))
            v.tensor_tensor(own[:, :, :], score[:, :, :], best[:, :].unsqueeze(2).to_broadcast(wide), ALU.is_equal)\
             .then_inc(s["chosen"], 1)
            dve.wait_ge(s["counted"], 1)
            link(v.tensor_copy(counts[:, :, :], ps_counts[:, 0:flat].rearrange("p (t e) -> p t e", t=TILES)))
            a, b = counts, sum_a
            for n in (1, 2, 4, 8):
                v.tensor_copy(b[:, 0:n, :], a[:, 0:n, :])
                link(v.tensor_tensor(b[:, n:TILES, :], a[:, n:TILES, :], a[:, 0:TILES - n, :], ALU.add))
                a, b = b, (sum_b if b is sum_a else sum_a)
            running = a
            square = [P, EXPERTS, TILES]
            link(v.tensor_tensor(started[:, :, :], running[:, TILES - 1, :].unsqueeze(2).to_broadcast(square),
                                 consts[:, C_STEPS:C_STEPS + TILES].unsqueeze(1).to_broadcast(square), ALU.is_gt))
            link(v.reduce_sum(needed[:, :], started[:, :, :], axis=X_AXIS))
            a, b = needed, end_a
            for n in (1, 2, 4):
                v.tensor_copy(b[:, 0:n], a[:, 0:n])
                link(v.tensor_tensor(b[:, n:EXPERTS], a[:, n:EXPERTS], a[:, 0:EXPERTS - n], ALU.add))
                a, b = b, (end_b if b is end_a else end_a)
            ends = a
            link(v.tensor_tensor(base[:, :], ends[:, :], needed[:, :], ALU.subtract))
            link(v.tensor_scalar(base[:, :], base[:, :], float(P), None, ALU.mult))
            link(v.tensor_tensor(rows[:, :, :], running[:, :, :], counts[:, :, :], ALU.subtract))
            link(v.tensor_tensor(rows[:, :, :], rows[:, :, :], ps_before[:, 0:flat].rearrange("p (t e) -> p t e", t=TILES), ALU.add))
            link(v.tensor_tensor(rows[:, :, :], rows[:, :, :], base[:, :].unsqueeze(1).to_broadcast(wide), ALU.add))
            link(v.tensor_tensor(rows[:, :, :], rows[:, :, :], own[:, :, :], ALU.mult))
            link(v.reduce_sum(row_of[:, :], rows[:, :, :], axis=X_AXIS))
            v.tensor_copy(position[:, :], row_of[:, :]).then_inc(s["placed"], 1)
            slot = [P, SLOTS, EXPERTS]
            link(v.tensor_tensor(passed[:, :, :], ends[:, :].unsqueeze(1).to_broadcast(slot),
                                 consts[:, C_SLOT:C_SLOT + SLOTS].unsqueeze(2).to_broadcast(slot), ALU.is_le))
            link(v.reduce_sum(slot_sum[:, :], passed[:, :, :], axis=X_AXIS))
            v.tensor_scalar(slot_expert[:, :], slot_sum[:, :], float(EXPERTS - 1), None, ALU.min).then_inc(s["placed"], 1)

        @block.gpsimd
        def _(pool):
            pool.wait_ge(s["placed"], 1)
            pool.wait_ge(s["xn_kept"], TILES)
            for t in range(TILES):
                nc.gpsimd.indirect_dma_start(sorted_x, bass.IndirectOffsetOnAxis(position[:, t:t + 1], 0), xn_all[:, t, :], None)\
                  .then_inc(s["scattered"], 16)
            pool.wait_ge(s["scattered"], 16 * TILES)


def expert_ffn(nc, name, scope, ident, loaded, gate_w, up_w, down_w, slot_expert, sorted_x, sorted_y):
    sb, pb, sem = scope(name)
    fc = INNER // P
    x_in = [sb(f"x_in{u}", [P, DIM]) for u in range(2)]
    xT = [sb(f"xT{u}", [P, KC, P]) for u in range(2)]
    silu = sb("silu", [P, INNER])
    hidden = sb("hidden", [P, INNER])
    hT = sb("hT", [P, fc, P])
    y_out = [sb(f"y_out{u}", [P, DIM]) for u in range(2)]
    ps_x, ps_h, ps_y = pb("ps_x"), pb("ps_h"), pb("ps_y")
    ps_g, ps_u = [pb("ps_g0"), pb("ps_g1")], [pb("ps_u0"), pb("ps_u1")]
    names = ("x_got0 x_got1 x_turned xT_ready gated lifted silu_ready hidden_ready h_turned hT_ready y_made y_ready "
             "y_stored0 y_stored1").split()
    s = {n: sem(n) for n in names}

    with nc.Block() as block:

        @block.sync
        def _(sp):
            def step(j, u, live):
                wait_count(sp, s["x_turned"], j - 1)
                sp.dma_start(x_in[u][:, :], sorted_x[bass.ds(j * P, P), :]).then_inc(s[f"x_got{u}"], 16)

            run_steps(sp, step, 0, SLOTS - 1, 2, SLOTS - 1, 2, SLOTS)

        @block.gpsimd
        def _(pool):
            def step(j, u, live):
                pool.wait_ge(s["y_ready"], j + 1)
                pool.dma_start(sorted_y[bass.ds(j * P, P), :], y_out[u][:, :]).then_inc(s[f"y_stored{u}"], 16)

            run_steps(pool, step, 0, SLOTS - 1, 0, SLOTS - 1, 2, SLOTS)
            for u in range(2):
                pool.wait_ge(s[f"y_stored{u}"], 16 * ((SLOTS + 1 - u) // 2))

        @block.tensor
        def _(pe):
            for semaphore, n in loaded:
                pe.wait_ge(semaphore, n)

            def expert_of(j):
                return pe.value_load(slot_expert[0:1, bass.ds(j, 1)], min_val=0, max_val=EXPERTS - 1)

            def turn(j, u):
                pe.wait_ge(s[f"x_got{u}"], 8 * j + 16 - 8 * u)
                for c in range(KC):
                    last = nc.tensor.transpose(ps_x[:, c * P:(c + 1) * P], x_in[u][:, c * P:(c + 1) * P], ident)
                last.then_inc(s["x_turned"], 1)

            def product(j, u, expert, w, out, made):
                for c in range(KC):
                    last = nc.tensor.matmul(out[u][:, :], xT[u][:, c, :], w[:, bass.ds(expert, 1), c, :].rearrange("p a n -> p (a n)"),
                                            start=(c == 0), stop=(c == KC - 1))
                last.then_inc(made, 1)

            def turn_hidden(j):
                pe.wait_ge(s["hidden_ready"], j + 1)
                for f in range(fc):
                    last = nc.tensor.transpose(ps_h[:, f * P:(f + 1) * P], hidden[:, f * P:(f + 1) * P], ident)
                last.then_inc(s["h_turned"], 1)

            def down(j, expert):
                pe.wait_ge(s["hT_ready"], j + 1)
                wait_count(pe, s["y_ready"], j)
                for f in range(fc):
                    last = nc.tensor.matmul(ps_y[:, 0:DIM], hT[:, f, :], down_w[:, bass.ds(expert, 1), f, :].rearrange("p a n -> p (a n)"),
                                            start=(f == 0), stop=(f == fc - 1))
                last.then_inc(s["y_made"], 1)

            def step(j, u, live):
                if live(0):
                    expert = expert_of(j)
                    pe.wait_ge(s["xT_ready"], j + 1)
                    product(j, u, expert, gate_w, ps_g, s["gated"])
                if live(-1):
                    turn_hidden(j - 1)
                if live(1):
                    turn(j + 1, 1 - u)
                if live(0):
                    product(j, u, expert, up_w, ps_u, s["lifted"])
                if live(-1):
                    down(j - 1, expert_of(j - 1))

            run_steps(pe, step, -1, SLOTS, 1, SLOTS - 2, 2, SLOTS)

        @block.scalar
        def _(act):
            def step(j, u, live):
                if live(0):
                    act.wait_ge(s["gated"], j + 1)
                    wait_count(act, s["hidden_ready"], j)
                    nc.scalar.activation(silu[:, :], ps_g[u][:, :], ACT.Silu).then_inc(s["silu_ready"], 1)
                if live(1):
                    act.wait_ge(s["x_turned"], j + 2)
                    nc.scalar.copy(xT[1 - u][:, :, :], ps_x[:, 0:DIM].rearrange("p (c t) -> p c t", c=KC)).then_inc(s["xT_ready"], 1)
                if live(-1):
                    act.wait_ge(s["y_made"], j)
                    if not isinstance(j, int) or j >= 3:
                        act.wait_ge(s[f"y_stored{1 - u}"], 8 * (j - 1) - 8 * (1 - u))
                    nc.scalar.copy(y_out[1 - u][:, :], ps_y[:, 0:DIM]).then_inc(s["y_ready"], 1)

            run_steps(act, step, -1, SLOTS, 3, SLOTS - 2, 2, SLOTS)

        @block.vector
        def _(dve):
            def step(j, u, live):
                if live(-1):
                    dve.wait_ge(s["h_turned"], j)
                    nc.vector.tensor_copy(hT[:, :, :], ps_h[:, :].rearrange("p (f t) -> p f t", f=fc)).then_inc(s["hT_ready"], 1)
                if live(0):
                    dve.wait_ge(s["silu_ready"], j + 1)
                    dve.wait_ge(s["lifted"], j + 1)
                    nc.vector.tensor_tensor(hidden[:, :], silu[:, :], ps_u[u][:, :], ALU.mult).then_inc(s["hidden_ready"], 1)

            run_steps(dve, step, 0, SLOTS, 1, SLOTS - 1, 2, SLOTS)


def combine(nc, name, scope, x_sb, best_prob, position, sorted_y, out):
    sb, pb, sem = scope(name)
    y_in = sb("y_in", [P, TILES, DIM])
    got = [sem(f"got{t}") for t in range(TILES)]
    added, stored = sem("added"), sem("stored")
    out_v = out.rearrange("(t p) n -> p t n", p=P)
    part = 4

    with nc.Block() as block:

        @block.gpsimd
        def _(pool):
            for t in range(TILES):
                nc.gpsimd.indirect_dma_start(y_in[:, t, :], None, sorted_y, bass.IndirectOffsetOnAxis(position[:, t:t + 1], 0))\
                  .then_inc(got[t], 16)

        @block.vector
        def _(dve):
            for t in range(TILES):
                dve.wait_ge(got[t], 16)
                nc.vector.scalar_tensor_tensor(out=x_sb[:, t, :], in0=y_in[:, t, :], scalar=best_prob[:, t:t + 1],
                                               in1=x_sb[:, t, :], op0=ALU.mult, op1=ALU.add).then_inc(added, 1)

        @block.sync
        def _(sp):
            for t in range(0, TILES, part):
                sp.wait_ge(added, t + part)
                sp.dma_start(out_v[:, t:t + part, :], x_sb[:, t:t + part, :]).then_inc(stored, 16)
            sp.wait_ge(stored, 16 * TILES // part)


def program(nc, d, out):
    outer = ExitStack()
    of_phase = []

    def release_semaphores():
        nc.clear_and_free_semaphores(of_phase)
        of_phase.clear()
        nc.all_engine_barrier()

    with outer:
        def scope(name, stack=outer):
            def sb(n, shape, dt=F32):
                return stack.enter_context(nc.sbuf_tensor(f"{name}_{n}", shape, dt))

            def pb(n, width=512, dt=F32):
                return stack.enter_context(nc.psum_tensor(f"{name}_{n}", [P, width], dt))

            def sem(n):
                semaphore = nc.alloc_semaphore(f"{name}_{n}")
                if stack is not outer:
                    of_phase.append(semaphore)
                return semaphore

            return sb, pb, sem

        sb, pb, sem = scope("all")
        x_sb = sb("x", [P, TILES, DIM])
        consts = sb("consts", [P, C_ALL])
        ident16 = sb("ident16", [P, P], BF16)
        causal16 = sb("causal16", [P, HEADS * SEQ // 2], BF16)
        ident = consts[:, C_IDENT:C_IDENT + P]
        x_part = 4
        got_consts, got_x = sem("got_consts"), [sem(f"got_x{n}") for n in range(TILES // x_part)]
        made16 = sem("made16")
        moments = Moments(nc, sb, consts)

        c_r = sb("c_r", [P, KC, 16])
        c_br = sb("c_br", [P, 16])
        c_1 = sb("c_1", [P, KC, 1024])
        c_2 = sb("c_2", [P, 8, DIM])
        sel16 = sb("sel16", [16, 1024], BF16)
        got_c = sem("got_c")

        d_a = sb("d_a", [P, KC, HEADS * DC])
        d_b = sb("d_b", [P, HEADS // 2, DIM])
        zeros = sb("zeros", [P, DIM])
        lastT = sb("lastT", [P, BATCH])
        diag = [sb(f"diag{u}", [4, TB, 4 * CTX]) for u in range(2)]
        last_roped = nc.dram_tensor("last_roped", (BATCH, CTX), F32, kind="Internal").ap()
        got_d = sem("got_d")
        e_q = sb("e_q", [P, KC, DIM])
        e_k = sb("e_k", [P, KC, DIM])
        e_v = sb("e_v", [P, KC, GROUPS * HD])
        e_bias = {n: sb(f"e_{n}", [P, KC]) for n in ("bq", "bk", "bv")}
        f_r = sb("f_r", [P, KC, EXPERTS])
        got_e = sem("got_e")
        sorted_x = nc.dram_tensor("sorted_x", (SLOTS * P, DIM), F32, kind="Internal").ap()
        sorted_y = nc.dram_tensor("sorted_y", (SLOTS * P, DIM), F32, kind="Internal").ap()
        zero_filled, zeros_made, got_f = sem("zero_filled"), sem("zeros_made"), sem("got_f")

        era1 = outer.enter_context(ExitStack())
        sb1, _, _ = scope("w", era1)
        a_q = sb1("a_q", [P, KC, DIM])
        a_kv = sb1("a_kv", [CTX, 1, 2 * DIM])
        a_o = sb1("a_o", [P, KC, DIM])
        ctx32 = sb1("ctx32", [CTX, TILES, P])
        got_a = sem("got_a")
        b_q = sb1("b_q", [P, KC, HEADS * DH])
        b_kv = sb1("b_kv", [P, KC, 2 * DH])
        b_o = sb1("b_o", [P, HEADS, DIM])
        b_g = sb1("b_g", [P, KC])
        b_gout = sb1("b_gout", [P, DIM])
        got_b, b_scaled = sem("got_b"), sem("b_scaled")

        def chunks(ap):
            return ap.rearrange("(c p) n -> p c n", p=P)

        with nc.Block() as block:

            @block.sync
            def _(sp):
                sp.dma_start(consts[:, :], d["consts"]).then_inc(got_consts, 16)
                for n in range(0, TILES, x_part):
                    sp.dma_start(x_sb[:, n:n + x_part, :], chunks(d["x"])[:, n:n + x_part, :]).then_inc(got_x[n // x_part], 16)
                sp.dma_start(a_q[:, :, :], chunks(d["a_wq"])).then_inc(got_a, 16)
                sp.dma_start(a_kv[:, 0, :], d["a_wkv"]).then_inc(got_a, 16)
                sp.dma_start(ctx32[:, :, :], d["ctx32"].rearrange("c (t k) -> c t k", t=TILES)).then_inc(got_a, 16)
                sp.dma_start(a_o[:, :, :], chunks(d["a_wo"])).then_inc(got_a, 16)
                sp.dma_start(b_q[:, :, :], chunks(d["b_wq"])).then_inc(got_b, 16)
                sp.dma_start(b_kv[:, :, :], chunks(d["b_wkv"])).then_inc(got_b, 16)
                sp.dma_start(b_g[:, :], d["b_g"]).then_inc(got_b, 16)
                sp.dma_start(b_gout[:, :], d["b_gout"].partition_broadcast(P)).then_inc(got_b, 16)
                sp.dma_start(b_o[:, :, :], chunks(d["b_wo"])).then_inc(got_b, 16)
                sp.dma_start(c_r[:, :, :], chunks(d["c_wr"])).then_inc(got_c, 16)
                sp.dma_start(c_br[:, :], d["c_br"].partition_broadcast(P)).then_inc(got_c, 16)
                sp.dma_start(c_1[:, :, :], chunks(d["c_w1"])).then_inc(got_c, 16)
                sp.dma_start(c_2[:, :, :], chunks(d["c_w2"])).then_inc(got_c, 16)

            @block.vector
            def _(dve):
                dve.wait_ge(got_consts, 16)
                nc.vector.memset(zeros[:, :], 0.0).then_inc(zeros_made, 1)
                nc.vector.tensor_copy(sel16[:, :], consts[0:16, C_SEL:C_SEL + 1024]).then_inc(made16, 1)
                nc.vector.tensor_copy(ident16[:, :], ident).then_inc(made16, 1)
                nc.vector.tensor_copy(causal16[:, :].rearrange("p (h k) -> p h k", h=HEADS // 2),
                                      consts[:, C_CAUSAL:C_CAUSAL + SEQ].unsqueeze(1).to_broadcast([P, HEADS // 2, SEQ]))\
                  .then_inc(made16, 1)
                for t in range(TILES):
                    if t % x_part == 0:
                        dve.wait_ge(got_x[t // x_part], 16)
                    moments.take(t, x_sb[:, t, :])

        def scale_b(pool):
            pool.wait_ge(got_b, 80)
            for c in range(KC):
                nc.gpsimd.tensor_scalar(b_q[:, c, :], b_q[:, c, :], b_g[:, c:c + 1], None, ALU.mult).then_inc(b_scaled, 1)
                nc.gpsimd.tensor_scalar(b_kv[:, c, :], b_kv[:, c, :], b_g[:, c:c + 1], None, ALU.mult).then_inc(b_scaled, 1)

        phase = ExitStack()
        with phase:
            small_attention(nc, "xattn0", lambda n: scope(n, phase), moments, x_sb, consts, ident, ident16[:, :], causal16[:, :],
                            [(got_consts, 16), (made16, 3), (got_a, 64)], True,
                            {"q": a_q, "k": a_kv[:, :, 0:DIM], "v": a_kv[:, :, DIM:2 * DIM], "o": a_o}, ctx32, scale_b)
        release_semaphores()

        phase = ExitStack()
        with phase:
            shared_key_attention(nc, "attn0", lambda n: scope(n, phase), moments, x_sb, consts, ident, [(got_b, 80), (b_scaled, 2 * KC)],
                                 b_q, b_kv, b_o, b_gout)
        release_semaphores()
        era1.close()

        era2 = outer.enter_context(ExitStack())
        sb2, _, _ = scope("raw", era2)
        raw = {
            "q": sb2("q", [P, HEADS, DIM]),
            "cq": sb2("cq", [QC, 2, HEADS, HK]),
            "qr": sb2("qr", [DR, HEADS, DCQ]),
            "kr": sb2("kr", [DR, HEADS, DC]),
            "ckv": sb2("ckv", [HK, HEADS, DC]),
            "o": sb2("o", [HK, HEADS, DIM]),
            "last": sb2("last", [BATCH, CTX]),
        }

        def load_d(sp):
            sp.dma_start(raw["qr"][:, :, :], d["d_wqr"]).then_inc(got_d, 16)
            sp.dma_start(raw["kr"][:, :, :], d["d_wkr"]).then_inc(got_d, 16)
            sp.dma_start(raw["cq"][:, :, :, :], d["d_wcq"].rearrange("(j q) h k -> q j h k", j=2)).then_inc(got_d, 16)
            sp.dma_start(raw["ckv"][:, :, :], d["d_wckv"]).then_inc(got_d, 16)
            sp.dma_start(raw["o"][:, :, :], chunks(d["d_wo"])).then_inc(got_d, 16)
            sp.dma_start(raw["q"][:, :, :], chunks(d["d_wq"])).then_inc(got_d, 16)
            sp.dma_start(raw["last"][:, :], d["ctx"][:, (KEYS - 1) * CTX:]).then_inc(got_d, 16)
            for dst, src in ((e_q, d["e_wq"]), (e_k, d["e_wk"]), (e_v, d["e_wv"]), (f_r, d["f_wr"])):
                sp.dma_start(dst[:, :, :], chunks(src)).then_inc(got_e, 16)
            for n in ("bq", "bk", "bv"):
                sp.dma_start(e_bias[n][:, :], d[f"e_{n}"]).then_inc(got_e, 16)
            sp.wait_ge(zeros_made, 1)
            sp.dma_start(sorted_x.rearrange("(j p) n -> p j n", p=P), zeros[:, :].unsqueeze(1).to_broadcast([P, SLOTS, DIM]))\
              .then_inc(zero_filled, 16)

        phase = ExitStack()
        with phase:
            block_routed_ffn(nc, "ffn0", lambda n: scope(n, phase), moments, x_sb, consts, ident, [(got_c, 64)],
                             c_r, c_br, c_1, c_2, sel16, load_d)
        release_semaphores()

        phase = ExitStack()
        with phase:
            fold_weights(nc, "fold", lambda n: scope(n, phase), consts, ident, [(got_d, 7 * 16)], raw,
                         d_a, d_b, lastT, last_roped, diag)
        release_semaphores()
        era2.close()

        era3 = outer.enter_context(ExitStack())
        sb3, _, _ = scope("moe", era3)
        f_gate = sb3("gate", [P, EXPERTS, KC, INNER])
        f_up = sb3("up", [P, EXPERTS, KC, INNER])

        def load_experts(sp, dst, src):
            for e in range(EXPERTS):
                sp.dma_start(dst[:, e, :, :], chunks(src[e])).then_inc(got_f, 16)

        def load_gates(sp):
            load_experts(sp, f_gate, d["f_gate"])
            load_experts(sp, f_up, d["f_up"])

        def load_downs(sp):
            load_experts(sp, f_down, d["f_down"])

        phase = ExitStack()
        with phase:
            latent_attention(nc, "xattn1", lambda n: scope(n, phase), moments, x_sb, consts, ident, d["ctx"], last_roped,
                             d_a, d_b, lastT, diag, load_gates)
        release_semaphores()
        f_down = sb3("down", [P, EXPERTS, INNER // P, DIM])

        phase = ExitStack()
        with phase:
            small_attention(nc, "attn1", lambda n: scope(n, phase), moments, x_sb, consts, ident, ident16[:, :], causal16[:, :],
                            [(got_e, 7 * 16)], False, {"q": e_q, "k": e_k, "v": e_v, **e_bias}, background=load_downs)
        release_semaphores()

        phase = ExitStack()
        with phase:
            own_sb, _, _ = scope("moe_tokens", phase)
            best_prob = own_sb("best_prob", [P, TILES])
            position = own_sb("position", [P, TILES], U32)
            slot_expert = own_sb("slot_expert", [P, SLOTS], I32)
            with ExitStack() as inner:
                xn_all = scope("moe_x", inner)[0]("xn_all", [P, TILES, DIM])
                route_tokens(nc, "route", lambda n: scope(n, inner), moments, x_sb, consts, ident, [(got_e, 7 * 16), (zero_filled, 16)],
                             f_r, xn_all, best_prob, position, slot_expert, sorted_x)
            release_semaphores()
            with ExitStack() as inner:
                expert_ffn(nc, "experts", lambda n: scope(n, inner), ident, [(got_f, 16 * 3 * EXPERTS)],
                           f_gate, f_up, f_down, slot_expert, sorted_x, sorted_y)
            release_semaphores()
            with ExitStack() as inner:
                combine(nc, "combine", lambda n: scope(n, inner), x_sb, best_prob, position, sorted_y, out)


def _tables(np):
    t = np.zeros((P, C_ALL), np.float32)
    p = np.arange(P)
    t[:, C_IDENT:C_IDENT + P] = np.eye(P)
    t[:, C_QMASK:C_QMASK + PER] = ((p // HD % PER)[:, None] == np.arange(PER)) * HD ** -0.5
    t[:, C_RMASK:C_RMASK + 4] = (p // SEQ)[:, None] == np.arange(4)
    t[:, C_CAUSAL:C_CAUSAL + SEQ] = np.where(np.arange(SEQ) < (p % SEQ)[:, None], MASKED, 0.0)
    t[:, C_BEFORE:C_BEFORE + P] = p[:, None] < p
    t[:, C_LN:C_LN + 3] = LN_EPS, LN_EPS ** 2, 1e-12
    i = np.arange(16)
    t[:, C_LOWER:C_LOWER + 256] = (i < i[:, None]).reshape(-1)
    t[:, C_STEPS:C_STEPS + 16] = 128 * i
    t[:, C_RANKS:C_RANKS + 8] = 8 - i[:8]
    t[:, C_SLOT:C_SLOT + 24] = np.arange(24)
    t[:16, C_SEL:C_SEL + 1024] = (np.arange(1024) // 64) == i[:, None]
    freq = (np.float32(1.0) / np.float32(10000.0) ** (np.arange(0, CTX, 2, dtype=np.float32) / np.float32(CTX)))
    angle = np.arange(KEYS, dtype=np.float32)[:, None] * freq[None, :].astype(np.float32)
    cos = np.repeat(np.cos(angle), 2, axis=-1)
    sin = np.repeat(np.sin(angle), 2, axis=-1)
    sin[:, :CTX // 2] *= -1
    t[:, C_COS:C_COS + P] = cos[:2 * P].reshape(P, 2 * CTX)
    t[:, C_SIN:C_SIN + P] = sin[:2 * P].reshape(P, 2 * CTX)
    t[:, C_LASTCOS:C_LASTCOS + CTX] = cos[-1]
    t[:, C_LASTSIN:C_LASTSIN + CTX] = sin[-1]
    t[:, C_ONE] = 1
    return t


def kernel(**inputs):
    import numpy as _np
    import concourse.bacc as _bacc
    from concourse import mybir as _mybir
    from concourse.bass_utils import run_bass_kernel_spmd as _run

    a = {k: _np.asarray(v) for k, v in inputs.items()}
    ctx = a["ctx_512"]
    laid = {
        "consts": _tables(_np),
        "x": a["x"].reshape(TOKENS, DIM),
        "ctx32": ctx[:, :SEQ].transpose(2, 0, 1).reshape(CTX, TOKENS),
        "a_wq": a["L0_xattn_Wq"].T,
        "a_wkv": a["L0_xattn_Wkv_expand"].T,
        "a_wo": a["L0_xattn_Wout"].T,
        "b_wq": a["L0_attn_Wq"],
        "b_wkv": a["L0_attn_Wkv"],
        "b_wo": a["L0_attn_Wout"],
        "b_g": a["L0_attn_g_norm"].reshape(KC, P).T,
        "b_gout": a["L0_attn_g_out"].reshape(1, DIM),
        "c_wr": a["L0_ffn_Wr"].T,
        "c_br": a["L0_ffn_br"].reshape(1, 16),
        "c_w1": a["L0_ffn_W1"].T,
        "c_w2": a["L0_ffn_W2"].T,
        "ctx": ctx.reshape(BATCH, KEYS * CTX),
        "d_wq": a["L1_xattn_Wq"],
        "d_wcq": a["L1_xattn_w_kc_q"].transpose(2, 0, 1),
        "d_wqr": a["L1_xattn_W_qr"].transpose(2, 0, 1),
        "d_wkr": a["L1_xattn_W_kr"].transpose(2, 0, 1),
        "d_wckv": a["L1_xattn_w_kc_kv"].transpose(1, 0, 2),
        "d_wo": a["L1_xattn_Wo"].T,
        "e_wq": a["L1_attn_Wq"].transpose(1, 0, 2).reshape(DIM, DIM),
        "e_wk": _np.repeat(a["L1_attn_Wk"].transpose(1, 0, 2), PER, axis=1).reshape(DIM, DIM),
        "e_wv": a["L1_attn_Wv"].transpose(1, 0, 2).reshape(DIM, GROUPS * HD),
        "e_bq": a["L1_attn_bq"].reshape(KC, P).T,
        "e_bk": _np.repeat(a["L1_attn_bk"], PER, axis=0).reshape(KC, P).T,
        "e_bv": _np.repeat(a["L1_attn_bv"], PER, axis=0).reshape(KC, P).T,
        "f_wr": a["L1_ffn_router_w"],
        "f_gate": a["L1_ffn_gate_w"],
        "f_up": a["L1_ffn_up_w"],
        "f_down": a["L1_ffn_down_w"],
    }
    nc = _bacc.Bacc("TRN2", target_bir_lowering=False, num_devices=1)
    arrays, drams = {}, {}
    for name, v in laid.items():
        v = _np.ascontiguousarray(v)
        arrays[f"in_{name}"] = v
        drams[name] = nc.dram_tensor(f"in_{name}", v.shape, _mybir.dt.from_np(v.dtype), kind="ExternalInput").ap()
    out = nc.dram_tensor("out", (TOKENS, DIM), _mybir.dt.float32, kind="ExternalOutput").ap()
    program(nc, drams, out)
    r = _run(nc, [arrays], core_ids=[0])
    return r.results[0]["out"].reshape(BATCH, SEQ, DIM)
```

```python
import concourse.bass as bass
from concourse import mybir
from contextlib import ExitStack

F32 = mybir.dt.float32
BF16 = mybir.dt.bfloat16
I32 = mybir.dt.int32
U32 = mybir.dt.uint32
ALU = mybir.AluOpType
ACT = mybir.ActivationFunctionType
X_AXIS = mybir.AxisListType.X

P = 128
BATCH, SEQ, DIM = 64, 32, 256
KEYS, CTX = 257, 64
TOKENS = BATCH * SEQ
TILES = TOKENS // P
TB = P // SEQ
KC = DIM // P
HEADS = 16
HD = DIM // HEADS
GROUPS = 4
PER = HEADS // GROUPS
DH = 128
LN_EPS = 1e-5
MASKED = -1e30

C_IDENT = 0
C_QMASK = 128
C_RMASK = 132
C_CAUSAL = 136
C_BEFORE = 168
C_LN = 296
C_LOWER = 304
C_STEPS = 560
C_RANKS = 576
C_SLOT = 584
C_SEL = 608
C_COS = 1632
C_SIN = 1760
C_LASTCOS = 1888
C_LASTSIN = 1952
C_ALL = 2016

EPS_LN, EPS_LN2, EPS_L2 = range(3)


class Link:

    def __init__(self, engine, semaphore, per):
        self.engine, self.semaphore, self.per = engine, semaphore, per

    def tile(self, t):
        self.base, self.made = t * self.per, 0

    def __call__(self, instruction):
        self.made += 1
        assert self.made <= self.per
        instruction.then_inc(self.semaphore, 1)
        self.engine.wait_ge(self.semaphore, self.base + self.made)

    def end(self):
        assert self.made == self.per, (self.made, self.per)


def run_steps(engine, step, first, last, full_from, full_to, unroll=2, tiles=TILES):

    def alone(i):
        step(i, i % 2, lambda d: 0 <= i + d < tiles)

    for i in range(first, full_from):
        alone(i)
    count = (full_to - full_from + 1) // unroll * unroll
    with engine.Fori(full_from, full_from + count - unroll + 1, unroll) as r:
        for k in range(unroll):
            step(r + k if k else r, (full_from + k) % 2, lambda d: True)
    for i in range(full_from + count, last + 1):
        alone(i)


def row(tensor, t):
    return tensor[:, bass.ds(t, 1), :].rearrange("p a n -> p (a n)")


class Moments:

    def __init__(self, nc, sb, consts):
        self.nc, self.consts = nc, consts
        self.stats = sb("row_stats", [P, TILES, 6])
        self.carrier = sb("carrier", [P, 1])
        self.moments = sb("moments", [P, TILES, 2])
        self.work = sb("moments_work", [P, 8 * TILES])
        self.root = Root(nc, self.work, TILES)

    def take(self, t, x):
        if not isinstance(t, int):
            self.nc.vector.memset(self.carrier[:, :], 0.0)
        return self.nc.vector.bn_stats(row(self.stats, t), x)

    def roots(self, engine, semaphore, eps, scale=1.0):
        link = Link(engine, semaphore, Root.LINKS + 5)
        link.tile(0)
        for t in range(TILES):
            last = self.nc.vector.bn_aggr(self.moments[:, t, :], self.stats[:, t, :])
        link(last)
        eps = self.consts[:, C_LN + eps:C_LN + eps + 1]
        link(self.nc.vector.tensor_scalar(self.work[:, 0:TILES], self.moments[:, :, 1], scale, eps, ALU.mult, ALU.add))
        self.factors = self.root(link)
        link.end()

    def apply(self, t, x, out):
        return self.nc.vector.tensor_scalar(out, x, row(self.moments, t)[:, 0:1], self.factors[:, bass.ds(t, 1)],
                                            ALU.subtract, ALU.mult)


class RowNorm:

    LINKS = 12

    def __init__(self, nc, sb, name, consts, eps):
        self.nc = nc
        self.eps = consts[:, C_LN + eps:C_LN + eps + 1]
        self.stats = sb(name + "_stats", [P, 6])
        self.carrier = sb(name + "_carrier", [P, 1])
        self.moments = sb(name + "_moments", [P, 2])
        self.work = sb(name + "_work", [P, 8])
        self.root = Root(nc, self.work)

    def __call__(self, link, x, out):
        nc = self.nc
        link(nc.vector.bn_stats(self.stats[:, :], x))
        nc.vector.memset(self.carrier[:, :], 0.0)
        link(nc.vector.bn_aggr(self.moments[:, :], self.stats[:, :]))
        link(nc.vector.tensor_scalar(self.work[:, 0:1], self.moments[:, 1:2], self.eps, None, ALU.add))
        rstd = self.root(link)
        return nc.vector.tensor_scalar(out, x, self.moments[:, 0:1], rstd, ALU.subtract, ALU.mult)


class Root:

    LINKS = 9
    MAGIC = 0x5F3759DF

    def __init__(self, nc, work, n=1):
        self.nc, self.n = nc, n
        self.v, self.guess, self.y0, self.a, self.y1, self.y2, self.b, self.y3 = (
            work[:, k * n:(k + 1) * n] for k in range(8))

    def __call__(self, link):
        v = self.nc.vector
        link(v.tensor_scalar(self.guess.bitcast(I32), self.v.bitcast(I32), 1, None, ALU.logical_shift_right))
        link(v.tensor_scalar(self.y0.bitcast(I32), self.guess.bitcast(I32), -1.0, float(self.MAGIC), ALU.mult, ALU.add))
        for y, three, out in ((self.y0, 3.0, self.y1), (self.y1, 12.0, self.y2)):
            self.square(link, y)
            link(v.scalar_tensor_tensor(out=out, in0=self.a, scalar=three, in1=y, op0=ALU.subtract, op1=ALU.mult))
        self.square(link, self.y2)
        link(v.tensor_scalar(self.b, self.a, -0.5 / 16 ** 3, 1.5 / 16, ALU.mult, ALU.add))
        link(v.tensor_tensor(self.y3, self.y2, self.b, ALU.mult))
        return self.y3

    def square(self, link, y):
        v = self.nc.vector
        if self.n == 1:
            link(v.scalar_tensor_tensor(out=self.a, in0=y, scalar=self.v, in1=y, op0=ALU.mult, op1=ALU.mult))
        else:
            link(v.tensor_tensor(self.b, y, self.v, ALU.mult))
            link(v.tensor_tensor(self.a, self.b, y, ALU.mult))


def wait_count(engine, semaphore, count):
    if not isinstance(count, int) or count > 0:
        engine.wait_ge(semaphore, count)


def small_attention(nc, name, scope, moments, x_sb, consts, ident, ident16, causal16, loaded, cross, w,
                    ctx32=None, beside=None, background=None):
    sb, pb, sem = scope(name)
    kin = CTX if cross else P
    kchunks = 1 if cross else KC

    xn = sb("xn", [P, DIM])
    xnT = [sb(f"xnT{u}", [P, KC, P]) for u in range(2)]
    srcT = [sb(f"srcT{u}", [kin, kchunks, TB, 4, SEQ]) for u in range(2)]
    q_blocks = sb("q_blocks", [P, KC, TB, PER, SEQ])
    kT = sb("kT", [P, KC, P])
    v_blocks = [sb(f"v_blocks{u}", [P, TB * GROUPS, PER, HD]) for u in range(2)]
    scores_sb = sb("scores", [P, HEADS * SEQ])
    shifted = sb("shifted", [P, HEADS, SEQ])
    exps = sb("exps", [P, HEADS, SEQ])
    probs = sb("probs", [P, HEADS * SEQ])
    probsT = sb("probsT", [P, HEADS * SEQ])
    top = sb("top", [P, HEADS])
    total = sb("total", [P, HEADS])
    inverse = sb("inverse", [P, HEADS])
    oT = sb("oT", [P, KC, P])

    ps_T, ps_k = pb("ps_T"), pb("ps_k")
    ps_q, ps_v = pb("ps_q"), pb("ps_v")
    ps_scores = [pb("ps_scores0"), pb("ps_scores1")]
    ps_pT, ps_o = pb("ps_pT"), pb("ps_o")
    ps_out = ps_o
    vw = DIM if cross else GROUPS * HD
    parts = 2 if cross else 1
    per_part = TB // parts

    xn_ready, turned, xnT_ready = sem("xn_ready"), sem("turned"), sem("xnT_ready")
    qk_made, v_made, q_ready, k_ready, v_ready = (sem(n) for n in ("qk_made", "v_made", "q_ready", "k_ready", "v_ready"))
    scores_made, scores_out, shifted_ready, exps_ready = (sem(n) for n in ("scores_made", "scores_out", "shifted_ready", "exps_ready"))
    probs_turned, probsT_ready = sem("probs_turned"), sem("probsT_ready")
    probs_ready, o_made, oT_ready, out_made, x_ready = (sem(n) for n in ("probs_ready", "o_made", "oT_ready", "out_made", "x_ready"))
    dve_roots, dve_s1, dve_s2 = (sem(n) for n in ("dve_roots", "dve_s1", "dve_s2"))

    with nc.Block() as block:

        @block.tensor
        def _(pe):
            for s, n in loaded:
                pe.wait_ge(s, n)

            def turn(t):
                pe.wait_ge(xn_ready, t + 1)
                for c in range(KC):
                    last = nc.tensor.transpose(ps_T[:, c * P:(c + 1) * P], xn[:, c * P:(c + 1) * P], ident)
                last.then_inc(turned, 1)

            def keys_queries(t, u):
                pe.wait_ge(xnT_ready, t + 1)
                for m in range(KC):
                    for c in range(kchunks):
                        nc.tensor.matmul(ps_k[:, m * P:(m + 1) * P], w["k"][:, c, m * P:(m + 1) * P],
                                         srcT[u][:, c, :, 0, :], start=(c == 0), stop=(c == kchunks - 1))
                for m in range(KC):
                    for c in range(KC):
                        last = nc.tensor.matmul(ps_q[:, m * P:(m + 1) * P], w["q"][:, c, m * P:(m + 1) * P],
                                                xnT[u][:, c, :], start=(c == 0), stop=(c == KC - 1))
                last.then_inc(qk_made, 1)

            def values(t, u, part):
                wait_count(pe, v_ready, parts * t + part)
                for n in range(per_part):
                    b = per_part * part + n
                    for c in range(kchunks):
                        last = nc.tensor.matmul(ps_v[:, n * vw:(n + 1) * vw], srcT[u][:, c, b, :, :].rearrange("p r k -> p (r k)"),
                                                w["v"][:, c, :], start=(c == 0), stop=(c == kchunks - 1))
                last.then_inc(v_made, 1)

            def scores(t):
                pe.wait_ge(q_ready, t + 1)
                pe.wait_ge(k_ready, t + 1)
                wait_count(pe, scores_out, t)
                for p in range(2):
                    nc.tensor.matmul(ps_scores[p][:, 0:256], ident16, causal16, start=True, stop=False, skip_group_check=True)
                    half = slice(64 * p, 64 * p + 64)
                    for m in range(KC):
                        for b in range(TB):
                            rows = slice(b * SEQ, (b + 1) * SEQ)
                            last = nc.tensor.matmul(ps_scores[p][rows, m * P:(m + 1) * P], kT[half, m, rows],
                                                    q_blocks[half, m, b, :, :].rearrange("p h q -> p (h q)"),
                                                    start=False, stop=True, skip_group_check=True)
                last.then_inc(scores_made, 1)

            def turn_probs(t):
                pe.wait_ge(probs_ready, t + 1)
                for g in range(GROUPS):
                    last = nc.tensor.transpose(ps_pT[:, g * P:(g + 1) * P], probs[:, g * P:(g + 1) * P], ident)
                last.then_inc(probs_turned, 1)

            def weigh(t, u):
                pe.wait_ge(v_ready, parts * (t + 1))
                pe.wait_ge(probsT_ready, t + 1)
                wait_count(pe, x_ready, t)
                for g in range(GROUPS):
                    m, p = g // 2, g % 2
                    half = slice(64 * p, 64 * p + 64)
                    for b in range(TB):
                        at = ((p * KC + m) * TB + b) * SEQ
                        last = nc.tensor.matmul(ps_o[half, m * P + b * SEQ:m * P + (b + 1) * SEQ],
                                                v_blocks[u][:, b * GROUPS + g, :, :].rearrange("p h d -> p (h d)"),
                                                probsT[:, at:at + SEQ], start=True, stop=True)
                last.then_inc(o_made, 1)

            def finish(t):
                pe.wait_ge(oT_ready, t + 1)
                for c in range(KC):
                    if cross:
                        last = nc.tensor.matmul(ps_out[:, 0:DIM], oT[:, c, :], w["o"][:, c, :], start=(c == 0), stop=(c == KC - 1))
                    else:
                        last = nc.tensor.transpose(ps_out[:, c * P:(c + 1) * P], oT[:, c, :], ident)
                last.then_inc(out_made, 1)

            def step(i, u, live):
                if live(0):
                    scores(i)
                if live(-1):
                    turn_probs(i - 1)
                if live(1):
                    keys_queries(i + 1, 1 - u)
                if live(2):
                    turn(i + 2)
                if live(-1):
                    weigh(i - 1, 1 - u)
                if live(1):
                    values(i + 1, 1 - u, 0)
                if live(-1):
                    finish(i - 1)
                if live(1) and parts > 1:
                    values(i + 1, 1 - u, 1)

            run_steps(pe, step, -2, TILES, 2, TILES - 3)

        if background:
            block.sync(background)
        if beside:
            block.gpsimd(beside)

        @block.scalar
        def _(act):
            def turned_out(t, u):
                act.wait_ge(turned, t + 1)
                last = nc.scalar.copy(xnT[u][:, :, :], ps_T[:, 0:DIM].rearrange("p (c t) -> p c t", c=KC))
                if cross:
                    last = nc.scalar.copy(srcT[u][:, 0, :, :, :], ctx32[:, bass.ds(t, 1), :].rearrange("p a (b k) -> p (a b) k", b=TB)
                                          .unsqueeze(2).to_broadcast([CTX, TB, 4, SEQ]))
                else:
                    for c in range(KC):
                        last = nc.scalar.copy(srcT[u][:, c, :, :, :], ps_T[:, c * P:(c + 1) * P].rearrange("p (b k) -> p b k", b=TB)
                                              .unsqueeze(2).to_broadcast([P, TB, 4, SEQ]))
                last.then_inc(xnT_ready, 1)

            def keys_out(t):
                act.wait_ge(qk_made, t + 1)
                if cross:
                    last = nc.scalar.copy(kT[:, :, :], ps_k[:, 0:DIM].rearrange("p (c t) -> p c t", c=KC))
                else:
                    for m in range(KC):
                        last = nc.scalar.activation(kT[:, m, :], ps_k[:, m * P:(m + 1) * P], ACT.Identity, bias=w["bk"][:, m:m + 1])
                last.then_inc(k_ready, 1)

            def values_out(t, u, part):
                act.wait_ge(v_made, parts * t + part + 1)
                if part == 0:
                    wait_count(act, o_made, t - 1)
                for r in range(PER):
                    src = ps_v[:, 0:per_part * vw].rearrange("p (b n) -> p b n", b=per_part)
                    if cross:
                        src = src.rearrange("p b (g r d) -> p b g r d", g=GROUPS, r=PER)[:, :, :, r, :]
                    else:
                        src = src.rearrange("p b (g d) -> p b g d", g=GROUPS)
                    dst = v_blocks[u][:, part * per_part * GROUPS:(part + 1) * per_part * GROUPS, r, :]\
                        .rearrange("p (b g) d -> p b g d", b=per_part)
                    last = nc.scalar.activation(dst, src, ACT.Copy, scale=consts[:, C_RMASK + r:C_RMASK + r + 1])
                last.then_inc(v_ready, 1)

            def probsT_out(t):
                act.wait_ge(probs_turned, t + 1)
                nc.scalar.copy(probsT[:, :], ps_pT[:, :]).then_inc(probsT_ready, 1)

            def outputs_out(t):
                act.wait_ge(o_made, t + 1)
                o_view = ps_o[:, 0:DIM].rearrange("p (c t) -> p c t", c=KC)
                if cross:
                    nc.scalar.copy(oT[:, :, :], o_view).then_inc(oT_ready, 1)
                else:
                    for m in range(KC):
                        last = nc.scalar.activation(oT[:, m, :], o_view[:, m, :], ACT.Identity, bias=w["bv"][:, m:m + 1])
                    last.then_inc(oT_ready, 1)

            def exponentials(t):
                act.wait_ge(shifted_ready, t + 1)
                nc.scalar.activation(exps[:, :, :], shifted[:, :, :], ACT.Exp).then_inc(exps_ready, 1)

            for s, n in loaded:
                act.wait_ge(s, n)

            def step(i, u, live):
                if live(-1):
                    probsT_out(i - 1)
                if live(1):
                    keys_out(i + 1)
                if live(0):
                    exponentials(i)
                if live(-1):
                    outputs_out(i - 1)
                if live(1) and parts > 1:
                    values_out(i + 1, 1 - u, 0)
                if live(2):
                    turned_out(i + 2, u)
                if live(1):
                    values_out(i + 1, 1 - u, parts - 1)

            run_steps(act, step, -2, TILES, 2, TILES - 3)

        @block.vector
        def _(dve):
            s1, s2 = Link(dve, dve_s1, 1), Link(dve, dve_s2, 2)
            for s, n in loaded:
                dve.wait_ge(s, n)
            moments.roots(dve, dve_roots, EPS_LN)

            def queries_out(t):
                dve.wait_ge(qk_made, t + 1)
                for m in range(KC):
                    src = ps_q[:, m * P:(m + 1) * P].rearrange("p (b q) -> p b q", b=TB)
                    mask = consts[:, C_QMASK:C_QMASK + PER]
                    src = src.unsqueeze(2).to_broadcast([P, TB, PER, SEQ])
                    mask = mask.unsqueeze(1).unsqueeze(3).to_broadcast([P, TB, PER, SEQ])
                    if cross:
                        last = nc.vector.tensor_tensor(q_blocks[:, m, :, :, :], src, mask, ALU.mult)
                    else:
                        last = None
                        for b in range(TB):
                            last = nc.vector.scalar_tensor_tensor(
                                out=q_blocks[:, m, b, :, :], in0=src[:, b, :, :], scalar=w["bq"][:, m:m + 1],
                                in1=mask[:, b, :, :], op0=ALU.add, op1=ALU.mult)
                last.then_inc(q_ready, 1)

            def softmax_tail(t):
                dve.wait_ge(exps_ready, t + 1)
                s2.tile(t)
                s2(nc.vector.reduce_sum(total[:, :], exps[:, :, :], axis=X_AXIS))
                s2(nc.vector.reciprocal(inverse[:, :], total[:, :]))
                s2.end()
                wait_count(dve, probs_turned, t)
                nc.vector.tensor_tensor(probs[:, :].rearrange("p (h k) -> p h k", h=HEADS), exps[:, :, :],
                                        inverse[:, :].unsqueeze(2).to_broadcast([P, HEADS, SEQ]), ALU.mult).then_inc(probs_ready, 1)

            def residual(t):
                dve.wait_ge(out_made, t + 1)
                nc.vector.tensor_tensor(row(x_sb, t), row(x_sb, t), ps_out[:, 0:DIM], ALU.add).then_inc(x_ready, 1)
                dve.wait_ge(x_ready, t + 1)
                moments.take(t, row(x_sb, t))

            def softmax_head(t):
                dve.wait_ge(scores_made, t + 1)
                for p in range(2):
                    last = nc.vector.transpose(scores_sb[:, p * 256:(p + 1) * 256], ps_scores[p][:, 0:256])
                last.then_inc(scores_out, 1)
                dve.wait_ge(scores_out, t + 1)
                s1.tile(t)
                view = scores_sb[:, :].rearrange("p (h k) -> p h k", h=HEADS)
                s1(nc.vector.reduce_max(top[:, :], view, axis=X_AXIS))
                nc.vector.tensor_tensor(shifted[:, :, :], view, top[:, :].unsqueeze(2).to_broadcast([P, HEADS, SEQ]),
                                        ALU.subtract).then_inc(shifted_ready, 1)
                s1.end()

            def normalise(t):
                wait_count(dve, turned, t)
                moments.apply(t, row(x_sb, t), xn[:, :]).then_inc(xn_ready, 1)

            def step(i, u, live):
                if live(2):
                    normalise(i + 2)
                if live(0):
                    softmax_head(i)
                if live(1):
                    queries_out(i + 1)
                if live(0):
                    softmax_tail(i)
                if live(-1):
                    residual(i - 1)

            run_steps(dve, step, -2, TILES, 2, TILES - 3)


def shared_key_attention(nc, name, scope, moments, x_sb, consts, ident, loaded, wq, wkv, wo, g_out):
    sb, pb, sem = scope(name)
    out_norm = RowNorm(nc, sb, "out_norm", consts, EPS_LN)
    xn = sb("xn", [P, DIM])
    xnT = [sb(f"xnT{u}", [P, KC, P]) for u in range(2)]
    qT = sb("qT", [P, TB, GROUPS, PER * SEQ])
    qT_squared = sb("qT_squared", [P, TB, GROUPS, PER * SEQ])
    ones = sb("ones", [P, SEQ])
    k_squared = sb("k_squared", [P, DH])
    k_work = sb("k_work", [P, 8])
    k_sum = sb("k_sum", [P, 1])
    k_root = Root(nc, k_work)
    k_norm = sb("k_norm", [P, DH])
    kT = sb("kT", [P, P])
    v = [sb(f"v{u}", [P, DH]) for u in range(2)]
    norms = sb("norms", [P, HEADS, SEQ])
    scores_sb = sb("scores", [P, HEADS, SEQ])
    q_work = sb("q_work", [P, 8 * HEADS])
    q_root = Root(nc, q_work, HEADS)
    scaled = sb("scaled", [P, HEADS, SEQ])
    exps = sb("exps", [P, HEADS, SEQ])
    probs = sb("probs", [P, HEADS * SEQ])
    probsT = sb("probsT", [P, HEADS * SEQ])
    total = sb("total", [P, HEADS])
    inverse = sb("inverse", [P, HEADS])
    oT = sb("oT", [P, HEADS, TB, SEQ])
    out_normed = sb("out_normed", [P, DIM])
    out_scaled = sb("out_scaled", [P, DIM])

    ps_T, ps_kv = pb("ps_T"), pb("ps_kv")
    ps_k, ps_v, ps_kT = ps_kv[:, 0:DH], ps_kv[:, DH:2 * DH], ps_kv[:, 2 * DH:2 * DH + P]
    ps_q = [pb("ps_q0"), pb("ps_q1")]
    ps_norms, ps_scores, ps_o, ps_out = pb("ps_norms"), pb("ps_scores"), pb("ps_o"), pb("ps_out")

    names = ("xn_ready turned xnT_ready ones_ready kv_made k_sum_ready k_normed k_turned kT_ready q_made q_ready "
             "squares_ready scores_made scores_out scaled_ready exps_ready probs_ready o_made oT_ready out_made x_ready "
             "dve_roots dve_k dve_q dve_tail dve_out").split()
    s = {n: sem(n) for n in names}

    with nc.Block() as block:

        @block.tensor
        def _(pe):
            for semaphore, n in loaded:
                pe.wait_ge(semaphore, n)

            def queries(t, u, g):
                if g == 0:
                    pe.wait_ge(s["xnT_ready"], t + 1)
                wait_count(pe, s["q_ready"], 4 * t + g - 1)
                for h in range(PER):
                    head = PER * g + h
                    for c in range(KC):
                        last = nc.tensor.matmul(ps_q[g % 2][:, h * P:(h + 1) * P], wq[:, c, head * DH:(head + 1) * DH],
                                                xnT[u][:, c, :], start=(c == 0), stop=(c == KC - 1))
                last.then_inc(s["q_made"], 1)

            def turn(t):
                pe.wait_ge(s["xn_ready"], t + 1)
                for c in range(KC):
                    last = nc.tensor.transpose(ps_T[:, c * P:(c + 1) * P], xn[:, c * P:(c + 1) * P], ident)
                last.then_inc(s["turned"], 1)

            def keys_values(t, u):
                pe.wait_ge(s["xnT_ready"], t + 1)
                wait_count(pe, s["kT_ready"], t)
                for c in range(KC):
                    last = nc.tensor.matmul(ps_kv[:, 0:2 * DH], xnT[u][:, c, :], wkv[:, c, :], start=(c == 0), stop=(c == KC - 1))
                last.then_inc(s["kv_made"], 1)

            def turn_keys(t):
                pe.wait_ge(s["k_normed"], t + 1)
                nc.tensor.transpose(ps_kT, k_norm[:, :], ident).then_inc(s["k_turned"], 1)

            def scores(t):
                pe.wait_ge(s["kT_ready"], t + 1)
                pe.wait_ge(s["q_ready"], 4 * t + 4)
                wait_count(pe, s["scores_out"], t)
                for b in range(TB):
                    rows = slice(b * SEQ, (b + 1) * SEQ)
                    nc.tensor.matmul(ps_scores[rows, :], kT[:, rows], qT[:, b, :, :].rearrange("p g n -> p (g n)"),
                                     start=True, stop=True)
                pe.wait_ge(s["squares_ready"], 4 * t + 4)
                for b in range(TB):
                    rows = slice(b * SEQ, (b + 1) * SEQ)
                    last = nc.tensor.matmul(ps_norms[rows, :], ones[:, :], qT_squared[:, b, :, :].rearrange("p g n -> p (g n)"),
                                            start=True, stop=True)
                last.then_inc(s["scores_made"], 1)

            def weigh(t, u, b):
                if b == 0:
                    pe.wait_ge(s["probs_ready"], t + 1)
                wait_count(pe, s["oT_ready"], 4 * t + b)
                rows = slice(SEQ * b, SEQ * (b + 1))
                nc.tensor.matmul(ps_o[:, :], v[u][rows, :], probsT[rows, :], start=True, stop=True).then_inc(s["o_made"], 1)

            def finish(t):
                wait_count(pe, s["x_ready"], t)
                pe.wait_ge(s["oT_ready"], 4 * t + 4)
                for h in range(HEADS):
                    last = nc.tensor.matmul(ps_out[:, 0:DIM], oT[:, h, :, :].rearrange("p b q -> p (b q)"), wo[:, h, :],
                                            start=(h == 0), stop=(h == HEADS - 1))
                last.then_inc(s["out_made"], 1)

            pe.wait_ge(s["ones_ready"], 1)

            def step(i, u, live):
                for g in range(GROUPS):
                    if live(0):
                        queries(i, u, g)
                    if live(0) and g == 2:
                        turn_keys(i)
                    if live(1) and g == 2:
                        turn(i + 1)
                    if live(-1):
                        weigh(i - 1, 1 - u, g)
                if live(1):
                    keys_values(i + 1, 1 - u)
                if live(0):
                    scores(i)
                if live(-1):
                    finish(i - 1)

            run_steps(pe, step, -1, TILES, 2, TILES - 2)

        @block.scalar
        def _(act):
            for semaphore, n in loaded:
                act.wait_ge(semaphore, n)

            def queries_out(t, g):
                act.wait_ge(s["q_made"], 4 * t + g + 1)
                nc.scalar.copy(qT[:, :, g, :].rearrange("p b (h q) -> p h b q", h=PER),
                               ps_q[g % 2][:, :].rearrange("p (h b q) -> p h b q", h=PER, b=TB)).then_inc(s["q_ready"], 1)

            def turned_out(t, u):
                act.wait_ge(s["turned"], t + 1)
                nc.scalar.copy(xnT[u][:, :, :], ps_T[:, 0:DIM].rearrange("p (c t) -> p c t", c=KC)).then_inc(s["xnT_ready"], 1)

            def values_out(t, u):
                act.wait_ge(s["kv_made"], t + 1)
                nc.scalar.copy(v[u][:, :], ps_v)
                nc.scalar.activation(k_squared[:, :], ps_k, ACT.Square, accum_out=k_sum[:, :]).then_inc(s["k_sum_ready"], 1)

            def keys_out(t):
                act.wait_ge(s["k_turned"], t + 1)
                nc.scalar.copy(kT[:, :], ps_kT).then_inc(s["kT_ready"], 1)

            def outputs_out(t, b):
                act.wait_ge(s["o_made"], 4 * t + b + 1)
                nc.scalar.copy(oT[:, :, b, :], ps_o[:, :].rearrange("p (h q) -> p h q", h=HEADS)).then_inc(s["oT_ready"], 1)

            def exponentials(t):
                act.wait_ge(s["scaled_ready"], t + 1)
                nc.scalar.activation(exps[:, :, :], scaled[:, :, :], ACT.Exp).then_inc(s["exps_ready"], 1)

            def step(i, u, live):
                for g in range(GROUPS):
                    if live(0):
                        queries_out(i, g)
                    if live(0) and g == 2:
                        keys_out(i)
                    if live(1) and g == 2:
                        turned_out(i + 1, 1 - u)
                    if live(-1):
                        outputs_out(i - 1, g)
                if live(1):
                    values_out(i + 1, 1 - u)
                if live(0):
                    exponentials(i)

            run_steps(act, step, -1, TILES, 2, TILES - 2)

        @block.gpsimd
        def _(pool):
            def step(i, u, live):
                for g in range(GROUPS):
                    if live(0):
                        pool.wait_ge(s["q_ready"], 4 * i + g + 1)
                        nc.gpsimd.tensor_tensor(qT_squared[:, :, g, :], qT[:, :, g, :], qT[:, :, g, :], ALU.mult)\
                          .then_inc(s["squares_ready"], 1)

            run_steps(pool, step, 0, TILES - 1, 0, TILES - 1, 1)

        @block.vector
        def _(dve):
            k_link, q_link = (Link(dve, s["dve_k"], Root.LINKS + 1),
                                  Link(dve, s["dve_q"], Root.LINKS + 4))
            nc.vector.memset(ones[:, :], 1.0).then_inc(s["ones_ready"], 1)
            tail, out_link = Link(dve, s["dve_tail"], 3), Link(dve, s["dve_out"], RowNorm.LINKS + 2)
            for semaphore, n in loaded:
                dve.wait_ge(semaphore, n)
            moments.roots(dve, s["dve_roots"], EPS_LN2, 1.0 + LN_EPS)

            def normalise(t):
                wait_count(dve, s["turned"], t)
                moments.apply(t, row(x_sb, t), xn[:, :]).then_inc(s["xn_ready"], 1)

            def normalise_keys(t):
                dve.wait_ge(s["k_sum_ready"], t + 1)
                k_link.tile(t)
                k_link(nc.vector.tensor_scalar(k_work[:, 0:1], k_sum[:, :], eps_l2, None, ALU.add))
                rstd = k_root(k_link)
                k_link.end()
                nc.vector.tensor_scalar(k_norm[:, :], ps_k, rstd, 256.0, ALU.mult, ALU.mult).then_inc(s["k_normed"], 1)

            def softmax_head(t):
                dve.wait_ge(s["scores_made"], t + 1)
                nc.vector.transpose(norms[:, :, :].rearrange("p h q -> p (h q)"), ps_norms[:, :])
                nc.vector.transpose(scores_sb[:, :, :].rearrange("p h q -> p (h q)"), ps_scores[:, :]).then_inc(s["scores_out"], 1)
                dve.wait_ge(s["scores_out"], t + 1)
                q_link.tile(t)
                q_link(nc.vector.tensor_scalar(q_work[:, 0:HEADS], norms[:, :, 0], 256.0, eps_l2, ALU.mult, ALU.add))
                rstd = q_root(q_link)
                nc.vector.tensor_tensor(scaled[:, :, :], scores_sb[:, :, :], rstd.unsqueeze(2).to_broadcast([P, HEADS, SEQ]),
                                        ALU.mult).then_inc(s["scaled_ready"], 1)
                q_link.end()

            def softmax_tail(t):
                dve.wait_ge(s["exps_ready"], t + 1)
                tail.tile(t)
                tail(nc.vector.reduce_sum(total[:, :], exps[:, :, :], axis=X_AXIS))
                tail(nc.vector.reciprocal(inverse[:, :], total[:, :]))
                tail(nc.vector.tensor_tensor(probs[:, :].rearrange("p (h k) -> p h k", h=HEADS), exps[:, :, :],
                                             inverse[:, :].unsqueeze(2).to_broadcast([P, HEADS, SEQ]), ALU.mult))
                nc.vector.transpose(probsT[:, :], probs[:, :]).then_inc(s["probs_ready"], 1)
                tail.end()

            def residual(t):
                dve.wait_ge(s["out_made"], t + 1)
                out_link.tile(t)
                out_link(out_norm(out_link, ps_out[:, 0:DIM], out_normed[:, :]))
                out_link(nc.vector.tensor_tensor(out_scaled[:, :], out_normed[:, :], g_out[:, :], ALU.mult))
                nc.vector.tensor_tensor(row(x_sb, t), row(x_sb, t), out_scaled[:, :], ALU.add).then_inc(s["x_ready"], 1)
                out_link.end()
                dve.wait_ge(s["x_ready"], t + 1)
                moments.take(t, row(x_sb, t))

            eps_l2 = consts[:, C_LN + EPS_L2:C_LN + EPS_L2 + 1]

            def step(i, u, live):
                if live(0):
                    softmax_head(i)
                if live(2):
                    normalise(i + 2)
                if live(0):
                    softmax_tail(i)
                if live(1):
                    normalise_keys(i + 1)
                if live(-1):
                    residual(i - 1)

            run_steps(dve, step, -2, TILES, 2, TILES - 3)


def block_routed_ffn(nc, name, scope, moments, x_sb, consts, ident, loaded, wr, br, w1, w2, sel16, background=None):
    sb, pb, sem = scope(name)
    blocks, top_k, chunks = 16, 4, 8
    xn = sb("xn", [P, DIM])
    xnT = sb("xnT", [P, KC, P])
    logits = sb("logits", [P, blocks])
    above = sb("above", [P, blocks, blocks])
    level = sb("level", [P, blocks, blocks])
    tied = sb("tied", [P, blocks, blocks])
    beaten = sb("beaten", [P, blocks, blocks])
    rank = sb("rank", [P, blocks])
    mask = sb("mask", [P, blocks])
    maskT = sb("maskT", [blocks, P], BF16)
    hidden = [sb(f"hidden{u}", [P, chunks, P]) for u in range(2)]
    masked = [sb(f"masked{u}", [P, chunks, P]) for u in range(2)]

    ps_T, ps_router, ps_out = pb("ps_T"), pb("ps_router"), pb("ps_out")
    ps_h = [pb("ps_h0"), pb("ps_h1")]
    ps_mask = pb("ps_mask", 1024)

    names = ("xn_ready turned xnT_ready logits_made mask_ready mask_turned maskT_ready h_made h_ready spread masked_ready "
             "out_made x_ready dve_roots dve_router").split()
    s = {n: sem(n) for n in names}

    with nc.Block() as block:
        if background:
            block.sync(background)

        @block.tensor
        def _(pe):
            for semaphore, n in loaded:
                pe.wait_ge(semaphore, n)

            def turn(t):
                pe.wait_ge(s["xn_ready"], t + 1)
                for c in range(KC):
                    last = nc.tensor.transpose(ps_T[:, c * P:(c + 1) * P], xn[:, c * P:(c + 1) * P], ident)
                last.then_inc(s["turned"], 1)

            def route(t):
                pe.wait_ge(s["xnT_ready"], t + 1)
                for c in range(KC):
                    last = nc.tensor.matmul(ps_router[:, 0:blocks], xnT[:, c, :], wr[:, c, :], start=(c == 0), stop=(c == KC - 1))
                last.then_inc(s["logits_made"], 1)

            def turn_mask(t):
                pe.wait_ge(s["mask_ready"], t + 1)
                nc.tensor.transpose(ps_router[0:blocks, P:2 * P], mask[:, :], ident).then_inc(s["mask_turned"], 1)

            def up(t):
                for half in range(2):
                    wait_count(pe, s["h_ready"], 2 * t + half - 1)
                    for j in range(chunks // 2):
                        f = half * chunks // 2 + j
                        for c in range(KC):
                            last = nc.tensor.matmul(ps_h[half][:, j * P:(j + 1) * P], w1[:, c, f * P:(f + 1) * P], xnT[:, c, :],
                                                    start=(c == 0), stop=(c == KC - 1))
                    last.then_inc(s["h_made"], 1)

            def spread(t):
                pe.wait_ge(s["maskT_ready"], t + 1)
                wait_count(pe, s["masked_ready"], t)
                for f in range(chunks):
                    last = nc.tensor.matmul(ps_mask[:, f * P:(f + 1) * P], sel16[:, f * P:(f + 1) * P], maskT[:, :],
                                            start=True, stop=True)
                last.then_inc(s["spread"], 1)

            def down(t, u, half):
                if half == 0:
                    pe.wait_ge(s["masked_ready"], t + 1)
                    wait_count(pe, s["x_ready"], t)
                for f in range(half * chunks // 2, (half + 1) * chunks // 2):
                    last = nc.tensor.matmul(ps_out[:, 0:DIM], masked[u][:, f, :], w2[:, f, :], start=(f == 0), stop=(f == chunks - 1))
                if half == 1:
                    last.then_inc(s["out_made"], 1)

            def step(i, u, live):
                if live(0):
                    up(i)
                if live(1):
                    turn(i + 1)
                if live(-1):
                    down(i - 1, 1 - u, 0)
                if live(0):
                    turn_mask(i)
                if live(-1):
                    down(i - 1, 1 - u, 1)
                if live(0):
                    spread(i)
                if live(1):
                    route(i + 1)

            run_steps(pe, step, -1, TILES, 2, TILES - 2)

        @block.scalar
        def _(act):
            def maskT_out(t):
                act.wait_ge(s["mask_turned"], t + 1)
                nc.scalar.copy(maskT[:, :], ps_router[0:blocks, P:2 * P]).then_inc(s["maskT_ready"], 1)

            def gelu(t, u):
                for half in range(2):
                    act.wait_ge(s["h_made"], 2 * t + half + 1)
                    n = chunks // 2
                    nc.scalar.activation(hidden[u][:, half * n:(half + 1) * n, :], ps_h[half][:, :].rearrange("p (f t) -> p f t", f=n),
                                         ACT.Gelu).then_inc(s["h_ready"], 1)

            def turned_out(t):
                act.wait_ge(s["turned"], t + 1)
                nc.scalar.copy(xnT[:, :, :], ps_T[:, 0:DIM].rearrange("p (c t) -> p c t", c=KC)).then_inc(s["xnT_ready"], 1)

            def step(i, u, live):
                if live(0):
                    gelu(i, u)
                if live(1):
                    turned_out(i + 1)
                if live(0):
                    maskT_out(i)

            run_steps(act, step, -1, TILES - 1, 2, TILES - 2)

        @block.vector
        def _(dve):
            router = Link(dve, s["dve_router"], 5)
            for semaphore, n in loaded:
                dve.wait_ge(semaphore, n)
            moments.roots(dve, s["dve_roots"], EPS_LN)

            def normalise(t):
                wait_count(dve, s["turned"], t)
                moments.apply(t, row(x_sb, t), xn[:, :]).then_inc(s["xn_ready"], 1)

            def choose(t):
                square = [P, blocks, blocks]
                dve.wait_ge(s["logits_made"], t + 1)
                router.tile(t)
                router(nc.vector.tensor_tensor(logits[:, :], ps_router[:, 0:blocks], br[:, :], ALU.add))
                own, other = logits[:, :].unsqueeze(2).to_broadcast(square), logits[:, :].unsqueeze(1).to_broadcast(square)
                nc.vector.tensor_tensor(above[:, :, :], other, own, ALU.is_gt)
                router(nc.vector.tensor_tensor(level[:, :, :], other, own, ALU.is_ge))
                router(nc.vector.tensor_tensor(tied[:, :, :], level[:, :, :],
                                               consts[:, C_LOWER:C_LOWER + 256].rearrange("p (i j) -> p i j", i=blocks), ALU.mult))
                router(nc.vector.tensor_tensor(beaten[:, :, :], above[:, :, :], tied[:, :, :], ALU.max))
                router(nc.vector.reduce_sum(rank[:, :], beaten[:, :, :], axis=X_AXIS))
                nc.vector.tensor_scalar(mask[:, :], rank[:, :], float(top_k), None, ALU.is_lt).then_inc(s["mask_ready"], 1)
                router.end()

            def apply_mask(t, u):
                dve.wait_ge(s["h_ready"], 2 * t + 2)
                dve.wait_ge(s["spread"], t + 1)
                nc.vector.tensor_tensor(masked[u][:, :, :].rearrange("p f t -> p (f t)"), ps_mask[:, :],
                                        hidden[u][:, :, :].rearrange("p f t -> p (f t)"), ALU.mult).then_inc(s["masked_ready"], 1)

            def residual(t):
                dve.wait_ge(s["out_made"], t + 1)
                nc.vector.tensor_tensor(row(x_sb, t), row(x_sb, t), ps_out[:, 0:DIM], ALU.add).then_inc(s["x_ready"], 1)
                dve.wait_ge(s["x_ready"], t + 1)
                moments.take(t, row(x_sb, t))

            def step(i, u, live):
                if live(-1):
                    residual(i - 1)
                if live(0):
                    apply_mask(i, u)
                if live(2):
                    normalise(i + 2)
                if live(1):
                    choose(i + 1)

            run_steps(dve, step, -2, TILES, 2, TILES - 3)

DC, DCQ, DR, HK = 64, 192, 64, 128
QC = DCQ // 2


def fold_weights(nc, name, scope, moments, consts, ident, loaded, raw, a_w, b_w, lastT, last_roped):
    sb, pb, sem = scope(name)
    half = HEADS // 2
    r1 = sb("r1", [QC, 2, half * DC])
    r2 = sb("r2", [P, half * DC])
    last_cos = sb("last_cos", [BATCH, CTX])
    last_sin = sb("last_sin", [BATCH, CTX])
    last_twice = sb("last_twice", [BATCH, 2, CTX])
    ps_r1 = [pb("ps_r1_0"), pb("ps_r1_1")]
    ps_r2, ps_last = pb("ps_r2"), pb("ps_last")
    ps_a = [pb("ps_a0"), pb("ps_a1")]
    ps_b = [pb("ps_b0"), pb("ps_b1")]
    names = ("r1_made r1_ready r2_made r2_ready a_made a_ready b_made b_ready last_products last_ready last_turned "
             "last_out stored dve_roots").split()
    s = {n: sem(n) for n in names}

    with nc.Block() as block:

        @block.gpsimd
        def _(pool):
            for semaphore, n in loaded:
                pool.wait_ge(semaphore, n)
            low, high = slice(0, CTX // 2), slice(CTX // 2, CTX)
            kv = raw["last"]
            cos = consts[0:BATCH, C_LASTCOS:C_LASTCOS + CTX]
            sin = consts[0:BATCH, C_LASTSIN:C_LASTSIN + CTX]
            nc.gpsimd.tensor_tensor(last_cos[:, :], kv[:, :], cos, ALU.mult).then_inc(s["last_products"], 1)
            nc.gpsimd.tensor_tensor(last_sin[:, low], kv[:, high], sin[:, low], ALU.mult).then_inc(s["last_products"], 1)
            nc.gpsimd.tensor_tensor(last_sin[:, high], kv[:, low], sin[:, high], ALU.mult).then_inc(s["last_products"], 1)
            pool.wait_ge(s["last_products"], 3)
            for n in range(2):
                nc.gpsimd.tensor_tensor(last_twice[:, n, :], last_cos[:, :], last_sin[:, :], ALU.add).then_inc(s["last_ready"], 1)

        @block.sync
        def _(sp):
            sp.wait_ge(s["last_ready"], 2)
            sp.dma_start(last_roped, last_twice[:, 0, :]).then_inc(s["stored"], 16)
            sp.wait_ge(s["stored"], 16)

        @block.tensor
        def _(pe):
            for semaphore, n in loaded:
                pe.wait_ge(semaphore, n)

            def out_weights(pair):
                if pair >= 2:
                    pe.wait_ge(s["b_ready"], pair - 1)
                for n in range(2):
                    for odd in range(2):
                        h = 4 * pair + 2 * n + odd
                        last = nc.tensor.matmul(ps_b[pair % 2][64 * odd:64 * odd + 64, n * DIM:(n + 1) * DIM],
                                                raw["ckv"][:, h, :], raw["o"][:, h, :], start=True, stop=True)
                last.then_inc(s["b_made"], 1)

            for g in range(2):
                if g:
                    pe.wait_ge(s["r1_ready"], g)
                for j in range(2):
                    for n in range(half):
                        h = g * half + n
                        last = nc.tensor.matmul(ps_r1[j][0:QC, n * DC:(n + 1) * DC], raw["qr"][:, h, j * QC:(j + 1) * QC],
                                                raw["kr"][:, h, :], start=True, stop=True)
                last.then_inc(s["r1_made"], 1)
                out_weights(2 * g)
                pe.wait_ge(s["r1_ready"], g + 1)
                if g:
                    pe.wait_ge(s["r2_ready"], g)
                for n in range(half):
                    for j in range(2):
                        last = nc.tensor.matmul(ps_r2[:, n * DC:(n + 1) * DC], raw["cq"][:, j, g * half + n, :],
                                                r1[:, j, n * DC:(n + 1) * DC], start=(j == 0), stop=(j == 1))
                last.then_inc(s["r2_made"], 1)
                out_weights(2 * g + 1)
                pe.wait_ge(s["r2_ready"], g + 1)
                if g:
                    pe.wait_ge(s["a_ready"], g)
                for c in range(KC):
                    for n in range(half):
                        last = nc.tensor.matmul(ps_a[c][:, n * DC:(n + 1) * DC], raw["q"][:, g * half + n, c * P:(c + 1) * P],
                                                r2[:, n * DC:(n + 1) * DC], start=True, stop=True)
                last.then_inc(s["a_made"], 1)
            pe.wait_ge(s["last_ready"], 2)
            nc.tensor.transpose(ps_last[:, 0:BATCH], last_twice[:, :, :].rearrange("b n d -> b (n d)"),
                                ident[0:BATCH, 0:BATCH]).then_inc(s["last_turned"], 1)

        @block.vector
        def _(dve):
            for g in range(2):
                dve.wait_ge(s["r1_made"], g + 1)
                if g:
                    dve.wait_ge(s["r2_made"], g)
                for j in range(2):
                    last = nc.vector.tensor_copy(r1[:, j, :], ps_r1[j][0:QC, :])
                last.then_inc(s["r1_ready"], 1)
                dve.wait_ge(s["r2_made"], g + 1)
                if g:
                    dve.wait_ge(s["a_made"], g)
                nc.vector.tensor_copy(r2[:, :], ps_r2[:, :]).then_inc(s["r2_ready"], 1)
                dve.wait_ge(s["a_made"], g + 1)
                for c in range(KC):
                    last = nc.vector.tensor_copy(a_w[:, c, g * half * DC:(g + 1) * half * DC], ps_a[c][:, :])
                last.then_inc(s["a_ready"], 1)
                if g == 0:
                    moments.roots(dve, s["dve_roots"], EPS_LN)

        @block.scalar
        def _(act):
            for pair in range(4):
                act.wait_ge(s["b_made"], pair + 1)
                nc.scalar.copy(b_w[:, 2 * pair:2 * pair + 2, :].rearrange("p m n -> p (m n)"), ps_b[pair % 2][:, :])\
                  .then_inc(s["b_ready"], 1)
            act.wait_ge(s["last_turned"], 1)
            nc.scalar.copy(lastT[:, :], ps_last[:, 0:BATCH]).then_inc(s["last_out"], 1)


def latent_attention(nc, name, scope, moments, x_sb, consts, ident, ctx_d, last_roped, a_w, b_w, lastT, background=None):
    sb, pb, sem = scope(name)
    blocks = 4
    nkeys = KEYS - 1
    xn = sb("xn", [P, DIM])
    xnT = sb("xnT", [P, KC, P])
    qT = [sb(f"qT{u}", [P, TB, HEADS // 2, SEQ]) for u in range(2)]
    kv_raw = [sb(f"kv_raw{u}", [P, TB, 2 * CTX]) for u in range(2)]
    kv_cos = sb("kv_cos", [P, TB, 2 * CTX])
    kv_sin = sb("kv_sin", [P, TB, 2, CTX])
    kv = [sb(f"kv{u}", [P, TB, 2, 2, CTX]) for u in range(2)]
    kT = [sb(f"kT{u}", [P, TB, KEYS]) for u in range(2)]
    exps = [sb(f"exps{u}", [P, blocks, KEYS]) for u in range(2)]
    top = sb("top", [P, blocks])
    total = [sb(f"total{u}", [P, blocks]) for u in range(2)]
    inverse = [sb(f"inverse{u}", [P, blocks]) for u in range(2)]
    expsT = [[sb(f"expsT{u}{j}", [P, blocks, P]) for j in range(2)] for u in range(2)]
    lastT_exps = [sb(f"last_exps{u}", [blocks, blocks, P]) for u in range(2)]
    last_raw = [sb(f"last_raw{u}", [blocks, P]) for u in range(2)]
    last_kv = [sb(f"last_kv{u}", [blocks, TB, CTX]) for u in range(2)]
    ctxT = [sb(f"ctxT{u}", [P, HEADS // 2, TB, SEQ]) for u in range(2)]

    ps_scores = pb("ps_scores", 2048)
    ps_t = [pb("ps_t0"), pb("ps_t1")]
    ps_o, ps_m = pb("ps_o"), pb("ps_m")

    names = ("xn_ready turned xnT_ready q_made q_out k_turned k_out kv_ready scores_made top_ready exps_ready scaled "
             "last_turned last_out last_spread turned0 turned1 out0 out1 weighed ctx_ready out_made x_ready "
             "raw_in0 raw_in1 last_in0 last_in1 pool_rope dve_inverse").split()
    s = {n: sem(n) for n in names}

    with nc.Block() as block:

        @block.sync
        def _(sp):
            def step(t, u, live):
                wait_count(sp, s["pool_rope"], t - 1)
                sp.dma_start(kv_raw[u][:, :, :], ctx_d[bass.ds(t * TB, TB), 0:nkeys * CTX].rearrange("b (p n) -> p b n", p=P))\
                  .then_inc(s[f"raw_in{u}"], 16)
                wait_count(sp, s["weighed"], TB * (t - 1))
                for n in range(blocks):
                    sp.dma_start(last_kv[u][n:n + 1, :, :], last_roped[bass.ds(t * TB, TB), :].unsqueeze(0))\
                      .then_inc(s[f"last_in{u}"], 16)

            run_steps(sp, step, 0, TILES - 1, 2, TILES - 1)
            if background:
                background(sp)

        @block.gpsimd
        def _(pool):
            rope = Link(pool, s["pool_rope"], 1)
            low, high = slice(0, CTX // 2), slice(CTX // 2, CTX)
            cos = consts[:, C_COS:C_COS + 2 * CTX].unsqueeze(1).to_broadcast([P, TB, 2 * CTX])
            sin = consts[:, C_SIN:C_SIN + 2 * CTX].rearrange("p (j d) -> p j d", j=2)

            def step(t, u, live):
                pool.wait_ge(s[f"raw_in{u}"], 8 * t + 16 - 8 * u)
                if not isinstance(t, int) or t > 0:
                    pool.wait_ge(s["kv_ready"], t)
                rope.tile(t)
                raw = kv_raw[u][:, :, :].rearrange("p b (j d) -> p b j d", j=2)
                nc.gpsimd.tensor_tensor(kv_cos[:, :, :], kv_raw[u][:, :, :], cos, ALU.mult)
                for to, come in ((low, high), (high, low)):
                    last = nc.gpsimd.tensor_tensor(kv_sin[:, :, :, to], raw[:, :, :, come],
                                                   sin[:, :, to].unsqueeze(1).to_broadcast([P, TB, 2, CTX // 2]), ALU.mult)
                rope(last)
                rope.end()
                wait_count(pool, s["weighed"], TB * (t - 1))
                twice = [P, TB * 2, 2, CTX]
                nc.gpsimd.tensor_tensor(kv[u][:, :, :, :, :].rearrange("p b j n d -> p (b j) n d"),
                                        kv_cos[:, :, :].rearrange("p b (j d) -> p (b j) d", j=2).unsqueeze(2).to_broadcast(twice),
                                        kv_sin[:, :, :, :].rearrange("p b j d -> p (b j) d").unsqueeze(2).to_broadcast(twice),
                                        ALU.add).then_inc(s["kv_ready"], 1)

            run_steps(pool, step, 0, TILES - 1, 2, TILES - 1)

        @block.tensor
        def _(pe):
            def turn(t):
                pe.wait_ge(s["xn_ready"], t + 1)
                wait_count(pe, s["k_out"], 2 * t)
                for c in range(KC):
                    last = nc.tensor.transpose(ps_m[:, c * P:(c + 1) * P], xn[:, c * P:(c + 1) * P], ident)
                last.then_inc(s["turned"], 1)

            def queries(t, part):
                if part == 0:
                    pe.wait_ge(s["xnT_ready"], t + 1)
                else:
                    pe.wait_ge(s["q_out"], 2 * t + 1)
                for n in range(4):
                    m = 4 * part + n
                    for c in range(KC):
                        last = nc.tensor.matmul(ps_m[:, n * P:(n + 1) * P], a_w[:, c, m * P:(m + 1) * P], xnT[:, c, :],
                                                start=(c == 0), stop=(c == KC - 1))
                last.then_inc(s["q_made"], 1)

            def keys(t, u, part):
                pe.wait_ge(s["kv_ready"], t + 1)
                for b in range(2):
                    for j in range(2):
                        last = nc.tensor.transpose(ps_m[:, (2 * b + j) * P:(2 * b + j + 1) * P],
                                                   kv[u][:, 2 * part + b, j, :, :].rearrange("p n d -> p (n d)"), ident)
                last.then_inc(s["k_turned"], 1)

            def finish(t, u):
                pe.wait_ge(s["ctx_ready"], TB * t + TB)
                for m in range(HEADS // 2):
                    last = nc.tensor.matmul(ps_m[:, 0:DIM], ctxT[u][:, m, :, :].rearrange("p b s -> p (b s)"), b_w[:, m, :],
                                            start=(m == 0), stop=(m == HEADS // 2 - 1))
                last.then_inc(s["out_made"], 1)

            def scores(t, u, b):
                if b == 0:
                    pe.wait_ge(s["q_out"], 2 * t + 2)
                    pe.wait_ge(s["k_out"], 2 * t + 1)
                if b == 2:
                    pe.wait_ge(s["k_out"], 2 * t + 2)
                for k in range(blocks):
                    wait_count(pe, s["exps_ready"], 4 * (TB * t + b) - 3 + k)
                    rows = slice(64 * (k % 2), 64 * (k % 2) + 64)
                    last = nc.tensor.matmul(ps_scores[:, 512 * k:512 * k + KEYS],
                                            qT[u][rows, b, 4 * (k // 2):4 * (k // 2) + 4, :].rearrange("p m q -> p (m q)"),
                                            kT[u][rows, b, :], start=True, stop=True)
                last.then_inc(s["scores_made"], 1)

            def turn_exps(n, v):
                pe.wait_ge(s["scaled"], n + 1)
                if isinstance(n, int) and n == 1:
                    pe.wait_ge(s["last_out"], 1)
                wait_count(pe, s["ctx_ready"], n - 1)
                nc.tensor.transpose(ps_o[0:blocks, DIM:DIM + P], exps[v][:, :, KEYS - 1], ident).then_inc(s["last_turned"], 1)
                for j in range(2):
                    wait_count(pe, s[f"out{j}"], n)
                    for k in range(blocks):
                        last = nc.tensor.transpose(ps_t[j][:, k * P:(k + 1) * P], exps[v][:, k, j * P:(j + 1) * P], ident)
                    last.then_inc(s[f"turned{j}"], 1)

            def weigh(n, v, t_par, last_count, b, is_last):
                if is_last:
                    pe.wait_ge(s["ctx_ready"], n)
                else:
                    pe.wait_ge(s["last_out"], n + 2)
                pe.wait_ge(s["last_spread"], n + 1)
                for j in range(2):
                    pe.wait_ge(s[f"out{j}"], n + 1)
                if b == 0:
                    pe.wait_ge(s[f"last_in{t_par}"], last_count)
                terms = [(last_kv[t_par][:, b, :], lastT_exps[v])]
                terms += [(kv[t_par][:, b, j, 0, :], expsT[v][j]) for j in range(2)]
                for n_term, (keys_of, weights) in enumerate(terms):
                    for odd in range(2):
                        last = nc.tensor.matmul(ps_o[64 * odd:64 * odd + 64, 0:DIM], keys_of,
                                                weights[:, :, :].rearrange("p (a k) q -> p k a q", k=2)[:, odd, :, :],
                                                start=(n_term == 0), stop=(n_term == 2), skip_group_check=True)
                last.then_inc(s["weighed"], 1)

            def step(t, u, live):
                for b in range(TB):
                    if live(0):
                        scores(t, u, b)
                    if b == 0 and live(1):
                        turn(t + 1)
                    if b == 1 and live(1):
                        queries(t + 1, 1)
                    if b == 2 and live(-1):
                        if live(1):
                            pe.wait_ge(s["q_out"], 2 * t + 4)
                        elif not live(0):
                            pe.wait_ge(s["x_ready"], t - 1)
                        finish(t - 1, 1 - u)
                    if b == 3 and live(1):
                        pe.wait_ge(s["k_out"], 2 * t + 3)
                        keys(t + 1, 1 - u, 1)
                    if live(0) if b else live(-1):
                        turn_exps(TB * t + b - 1, (b - 1) % 2)
                    if live(0) if b >= 2 else live(-1):
                        tile_d = 0 if b >= 2 else -1
                        tu = u if b >= 2 else 1 - u
                        is_last = b == 1 and not live(0)
                        weigh(TB * t + b - 2, b % 2, tu, 32 * (t + tile_d) + 64 - 32 * tu, (b - 2) % TB, is_last)
                    if b == 0 and live(1):
                        queries(t + 1, 0)
                    if b == 2 and live(1):
                        if live(-1):
                            pe.wait_ge(s["x_ready"], t)
                        else:
                            pe.wait_ge(s["q_out"], 2 * t + 4)
                        keys(t + 1, 1 - u, 0)

            run_steps(pe, step, -1, TILES, 3, TILES - 2)

        @block.scalar
        def _(act):
            def exponentials(t, b, k):
                if k == 0:
                    act.wait_ge(s["top_ready"], TB * t + b + 1)
                v = b % 2
                nc.scalar.activation(exps[v][:, k, :], ps_scores[:, 512 * k:512 * k + KEYS], ACT.Exp, bias=top[:, k:k + 1],
                                     accum_out=total[v][:, k:k + 1]).then_inc(s["exps_ready"], 1)

            def turned_out(t):
                act.wait_ge(s["turned"], t + 1)
                nc.scalar.copy(xnT[:, :, :], ps_m[:, 0:DIM].rearrange("p (c t) -> p c t", c=KC)).then_inc(s["xnT_ready"], 1)

            def queries_out(t, u, part):
                act.wait_ge(s["q_made"], 2 * t + part + 1)
                nc.scalar.copy(qT[u][:, :, 4 * part:4 * part + 4, :].rearrange("p b m q -> p m b q"),
                               ps_m[:, :].rearrange("p (m b q) -> p m b q", m=4, b=TB)).then_inc(s["q_out"], 1)

            def keys_out(t, u, part):
                if part == 0:
                    nc.scalar.copy(kT[u][:, :, KEYS - 1], lastT[:, bass.ds(t * TB, TB)])
                act.wait_ge(s["k_turned"], 2 * t + part + 1)
                nc.scalar.copy(kT[u][:, 2 * part:2 * part + 2, 0:nkeys], ps_m[:, :].rearrange("p (b n) -> p b n", b=2))\
                  .then_inc(s["k_out"], 1)

            def last_out(n, v):
                act.wait_ge(s["last_turned"], n + 1)
                nc.scalar.copy(last_raw[v][:, :], ps_o[0:blocks, DIM:DIM + P]).then_inc(s["last_out"], 1)

            def exps_out(n, v):
                act.wait_ge(s["turned1"], n + 1)
                nc.scalar.copy(expsT[v][1][:, :, :], ps_t[1][:, :].rearrange("p (k q) -> p k q", k=blocks)).then_inc(s["out1"], 1)

            def step(t, u, live):
                for b in range(TB):
                    if b == 0 and live(-1) or b == 3 and live(0):
                        last_out(TB * t + b - 1, (b - 1) % 2)
                    if live(0):
                        exponentials(t, b, 0)
                        exponentials(t, b, 1)
                    if b == 1 and live(0):
                        last_out(TB * t + b - 1, (b - 1) % 2)
                    if b == 0 and live(1):
                        turned_out(t + 1)
                    if b == 1 and live(1):
                        queries_out(t + 1, 1 - u, 1)
                    if live(0):
                        exponentials(t, b, 2)
                        exponentials(t, b, 3)
                    if b == 2 and live(0):
                        last_out(TB * t + b - 1, (b - 1) % 2)
                    if b == 3 and live(1):
                        keys_out(t + 1, 1 - u, 1)
                    if live(0) if b else live(-1):
                        exps_out(TB * t + b - 1, (b - 1) % 2)
                    if b == 0 and live(1):
                        queries_out(t + 1, 1 - u, 0)
                    if b == 2 and live(1):
                        keys_out(t + 1, 1 - u, 0)

            run_steps(act, step, -1, TILES, 2, TILES - 2)

        @block.vector
        def _(dve):

            def normalise(t):
                wait_count(dve, s["turned"], t)
                moments.apply(t, row(x_sb, t), xn[:, :]).then_inc(s["xn_ready"], 1)

            def maxima(n):
                dve.wait_ge(s["scores_made"], n + 1)
                view = ps_scores[:, :].rearrange("p (k n) -> p k n", k=blocks)[:, :, 0:KEYS]
                nc.vector.tensor_reduce(top[:, :], view, X_AXIS, ALU.max, negate=True).then_inc(s["top_ready"], 1)

            def scale(n, v):
                dve.wait_ge(s["exps_ready"], 4 * n + 4)
                nc.vector.reciprocal(inverse[v][:, :], total[v][:, :]).then_inc(s["dve_inverse"], 1)
                dve.wait_ge(s["dve_inverse"], n + 1)
                nc.vector.tensor_tensor(exps[v][:, :, :], exps[v][:, :, :],
                                        inverse[v][:, :].unsqueeze(2).to_broadcast([P, blocks, KEYS]), ALU.mult).then_inc(s["scaled"], 1)

            def exps_out(n, v):
                dve.wait_ge(s["turned0"], n + 1)
                nc.vector.tensor_copy(expsT[v][0][:, :, :], ps_t[0][:, :].rearrange("p (k q) -> p k q", k=blocks))\
                  .then_inc(s["out0"], 1)

            def spread_last(n, v):
                dve.wait_ge(s["last_out"], n + 1)
                square = [blocks, blocks, P]
                nc.vector.tensor_tensor(lastT_exps[v][:, :, :], last_raw[v][:, :].unsqueeze(1).to_broadcast(square),
                                        ident[0:blocks, 0:blocks].unsqueeze(2).to_broadcast(square), ALU.mult)\
                  .then_inc(s["last_spread"], 1)

            def ctx_out(n, tu, b):
                dve.wait_ge(s["weighed"], n + 1)
                nc.vector.tensor_copy(ctxT[tu][:, :, b, :], ps_o[:, 0:DIM].rearrange("p (m q) -> p m q", q=SEQ))\
                  .then_inc(s["ctx_ready"], 1)

            def residual(t):
                dve.wait_ge(s["out_made"], t + 1)
                nc.vector.tensor_tensor(row(x_sb, t), row(x_sb, t), ps_m[:, 0:DIM], ALU.add).then_inc(s["x_ready"], 1)

            def statistics(t):
                dve.wait_ge(s["x_ready"], t + 1)
                moments.take(t, row(x_sb, t))

            def step(t, u, live):
                for b in range(TB):
                    if b != 3 and (live(0) if b else live(-1)):
                        scale(TB * t + b - 1, (b - 1) % 2)
                    if live(0):
                        maxima(TB * t + b)
                    if live(0) if b else live(-1):
                        exps_out(TB * t + b - 1, (b - 1) % 2)
                    if b == 2 and live(-1):
                        residual(t - 1)
                    if live(0) if b >= 2 else live(-1):
                        ctx_out(TB * t + b - 2, u if b >= 2 else 1 - u, (b - 2) % TB)
                    if live(0) if b else live(-1):
                        spread_last(TB * t + b - 1, (b - 1) % 2)
                    if b == 2 and live(0):
                        scale(TB * t + b, b % 2)
                    if b == 2 and live(-1):
                        statistics(t - 1)
                    if b == 2 and live(2):
                        normalise(t + 2)

            run_steps(dve, step, -2, TILES, 2, TILES - 3)

EXPERTS, INNER = 8, 512
SLOTS = TILES + EXPERTS - 1


def route_tokens(nc, name, scope, moments, x_sb, consts, ident, loaded, router_w, xn_all, best_prob, position, slot_expert, sorted_x):
    sb, pb, sem = scope(name)
    flat = TILES * EXPERTS
    xn = [sb(f"xn{u}", [P, DIM]) for u in range(2)]
    xnT = [sb(f"xnT{u}", [P, KC, P]) for u in range(2)]
    ones = sb("ones", [P, P])
    logits, exps, denominator, prob, score, own, counts, sum_a, sum_b, rows = (
        sb(n, [P, TILES, EXPERTS]) for n in "logits exps denominator prob score own counts sum_a sum_b rows".split())
    started = sb("started", [P, EXPERTS, TILES])
    needed, end_a, end_b, base = (sb(n, [P, EXPERTS]) for n in "needed end_a end_b base".split())
    best = sb("best", [P, TILES])
    row_of = sb("row_of", [P, TILES])
    passed = sb("passed", [P, SLOTS, EXPERTS])
    slot_sum = sb("slot_sum", [P, SLOTS])
    ps_T, ps_logits = [pb("ps_T0"), pb("ps_T1")], [pb("ps_logits0"), pb("ps_logits1")]
    ps_before, ps_counts = pb("ps_before"), pb("ps_counts")
    names = ("xn_ready turned xnT_ready xn_kept logits_made logits_out exps_ready chosen counted placed ones_ready "
             "dve_roots dve_route scattered").split()
    s = {n: sem(n) for n in names}

    with nc.Block() as block:

        @block.tensor
        def _(pe):
            for semaphore, n in loaded:
                pe.wait_ge(semaphore, n)

            def turn(t, u):
                pe.wait_ge(s["xn_ready"], t + 1)
                for c in range(KC):
                    last = nc.tensor.transpose(ps_T[u][:, c * P:(c + 1) * P], xn[u][:, c * P:(c + 1) * P], ident)
                last.then_inc(s["turned"], 1)

            def route(t, u):
                pe.wait_ge(s["xnT_ready"], t + 1)
                wait_count(pe, s["logits_out"], t - 1)
                for c in range(KC):
                    last = nc.tensor.matmul(ps_logits[u][:, 0:EXPERTS], xnT[u][:, c, :], router_w[:, c, :],
                                            start=(c == 0), stop=(c == KC - 1))
                last.then_inc(s["logits_made"], 1)

            def step(i, u, live):
                if live(1):
                    turn(i + 1, 1 - u)
                if live(0):
                    route(i, u)

            run_steps(pe, step, -1, TILES - 1, 2, TILES - 2)
            pe.wait_ge(s["chosen"], 1)
            pe.wait_ge(s["ones_ready"], 1)
            chosen = own[:, :, :].rearrange("p t e -> p (t e)")
            nc.tensor.matmul(ps_before[:, 0:flat], consts[:, C_BEFORE:C_BEFORE + P], chosen, start=True, stop=True)
            nc.tensor.matmul(ps_counts[:, 0:flat], ones[:, :], chosen, start=True, stop=True).then_inc(s["counted"], 1)

        @block.scalar
        def _(act):
            def step(t, u, live):
                act.wait_ge(s["turned"], t + 1)
                wait_count(act, s["logits_made"], t - 1)
                nc.scalar.copy(xnT[u][:, :, :], ps_T[u][:, 0:DIM].rearrange("p (c t) -> p c t", c=KC)).then_inc(s["xnT_ready"], 1)
                nc.scalar.copy(row(xn_all, t), xn[u][:, :]).then_inc(s["xn_kept"], 1)

            run_steps(act, step, 0, TILES - 1, 2, TILES - 1)
            act.wait_ge(s["logits_out"], TILES)
            nc.scalar.activation(exps[:, :, :], logits[:, :, :], ACT.Exp, scale=-1.0).then_inc(s["exps_ready"], 1)

        @block.vector
        def _(dve):
            nc.vector.memset(ones[:, :], 1.0).then_inc(s["ones_ready"], 1)
            for semaphore, n in loaded:
                dve.wait_ge(semaphore, n)
            moments.roots(dve, s["dve_roots"], EPS_LN)

            def step(t, u, live):
                if live(2):
                    wait_count(dve, s["xn_kept"], t + 1)
                    moments.apply(t + 2, row(x_sb, t + 2), xn[u][:, :]).then_inc(s["xn_ready"], 1)
                if live(0):
                    dve.wait_ge(s["logits_made"], t + 1)
                    nc.vector.tensor_copy(row(logits, t), ps_logits[u][:, 0:EXPERTS]).then_inc(s["logits_out"], 1)

            run_steps(dve, step, -2, TILES - 1, 2, TILES - 3)

            link = Link(dve, s["dve_route"], 64)
            link.tile(0)
            v = nc.vector
            wide = [P, TILES, EXPERTS]
            dve.wait_ge(s["exps_ready"], 1)
            link(v.tensor_scalar(denominator[:, :, :], exps[:, :, :], 1.0, None, ALU.add))
            link(v.reciprocal(prob[:, :, :], denominator[:, :, :]))
            link(v.reduce_max(best_prob[:, :], prob[:, :, :], axis=X_AXIS))
            link(v.tensor_tensor(own[:, :, :], prob[:, :, :], best_prob[:, :].unsqueeze(2).to_broadcast(wide), ALU.is_equal))
            link(v.tensor_tensor(score[:, :, :], own[:, :, :],
                                 consts[:, C_RANKS:C_RANKS + EXPERTS].unsqueeze(1).to_broadcast(wide), ALU.mult))
            link(v.reduce_max(best[:, :], score[:, :, :], axis=X_AXIS))
            v.tensor_tensor(own[:, :, :], score[:, :, :], best[:, :].unsqueeze(2).to_broadcast(wide), ALU.is_equal)\
             .then_inc(s["chosen"], 1)
            dve.wait_ge(s["counted"], 1)
            link(v.tensor_copy(counts[:, :, :], ps_counts[:, 0:flat].rearrange("p (t e) -> p t e", t=TILES)))
            a, b = counts, sum_a
            for n in (1, 2, 4, 8):
                v.tensor_copy(b[:, 0:n, :], a[:, 0:n, :])
                link(v.tensor_tensor(b[:, n:TILES, :], a[:, n:TILES, :], a[:, 0:TILES - n, :], ALU.add))
                a, b = b, (sum_b if b is sum_a else sum_a)
            running = a
            square = [P, EXPERTS, TILES]
            link(v.tensor_tensor(started[:, :, :], running[:, TILES - 1, :].unsqueeze(2).to_broadcast(square),
                                 consts[:, C_STEPS:C_STEPS + TILES].unsqueeze(1).to_broadcast(square), ALU.is_gt))
            link(v.reduce_sum(needed[:, :], started[:, :, :], axis=X_AXIS))
            a, b = needed, end_a
            for n in (1, 2, 4):
                v.tensor_copy(b[:, 0:n], a[:, 0:n])
                link(v.tensor_tensor(b[:, n:EXPERTS], a[:, n:EXPERTS], a[:, 0:EXPERTS - n], ALU.add))
                a, b = b, (end_b if b is end_a else end_a)
            ends = a
            link(v.tensor_tensor(base[:, :], ends[:, :], needed[:, :], ALU.subtract))
            link(v.tensor_scalar(base[:, :], base[:, :], float(P), None, ALU.mult))
            link(v.tensor_tensor(rows[:, :, :], running[:, :, :], counts[:, :, :], ALU.subtract))
            link(v.tensor_tensor(rows[:, :, :], rows[:, :, :], ps_before[:, 0:flat].rearrange("p (t e) -> p t e", t=TILES), ALU.add))
            link(v.tensor_tensor(rows[:, :, :], rows[:, :, :], base[:, :].unsqueeze(1).to_broadcast(wide), ALU.add))
            link(v.tensor_tensor(rows[:, :, :], rows[:, :, :], own[:, :, :], ALU.mult))
            link(v.reduce_sum(row_of[:, :], rows[:, :, :], axis=X_AXIS))
            v.tensor_copy(position[:, :], row_of[:, :]).then_inc(s["placed"], 1)
            slot = [P, SLOTS, EXPERTS]
            link(v.tensor_tensor(passed[:, :, :], ends[:, :].unsqueeze(1).to_broadcast(slot),
                                 consts[:, C_SLOT:C_SLOT + SLOTS].unsqueeze(2).to_broadcast(slot), ALU.is_le))
            link(v.reduce_sum(slot_sum[:, :], passed[:, :, :], axis=X_AXIS))
            v.tensor_scalar(slot_expert[:, :], slot_sum[:, :], float(EXPERTS - 1), None, ALU.min).then_inc(s["placed"], 1)

        @block.gpsimd
        def _(pool):
            pool.wait_ge(s["placed"], 1)
            pool.wait_ge(s["xn_kept"], TILES)
            for t in range(TILES):
                nc.gpsimd.indirect_dma_start(sorted_x, bass.IndirectOffsetOnAxis(position[:, t:t + 1], 0), xn_all[:, t, :], None)\
                  .then_inc(s["scattered"], 16)
            pool.wait_ge(s["scattered"], 16 * TILES)


def expert_ffn(nc, name, scope, ident, loaded, gate_w, up_w, down_w, slot_expert, sorted_x, sorted_y):
    sb, pb, sem = scope(name)
    fc = INNER // P
    x_in = [sb(f"x_in{u}", [P, DIM]) for u in range(2)]
    xT = [sb(f"xT{u}", [P, KC, P]) for u in range(2)]
    silu = sb("silu", [P, INNER])
    hidden = sb("hidden", [P, INNER])
    hT = sb("hT", [P, fc, P])
    y_out = [sb(f"y_out{u}", [P, DIM]) for u in range(2)]
    ps_x, ps_h, ps_y = pb("ps_x"), pb("ps_h"), pb("ps_y")
    ps_g, ps_u = [pb("ps_g0"), pb("ps_g1")], [pb("ps_u0"), pb("ps_u1")]
    names = ("x_got0 x_got1 x_turned xT_ready gated lifted silu_ready hidden_ready h_turned hT_ready y_made y_ready "
             "y_stored0 y_stored1").split()
    s = {n: sem(n) for n in names}

    with nc.Block() as block:

        @block.sync
        def _(sp):
            def step(j, u, live):
                wait_count(sp, s["x_turned"], j - 1)
                sp.dma_start(x_in[u][:, :], sorted_x[bass.ds(j * P, P), :]).then_inc(s[f"x_got{u}"], 16)

            run_steps(sp, step, 0, SLOTS - 1, 2, SLOTS - 1, 2, SLOTS)

        @block.gpsimd
        def _(pool):
            def step(j, u, live):
                pool.wait_ge(s["y_ready"], j + 1)
                pool.dma_start(sorted_y[bass.ds(j * P, P), :], y_out[u][:, :]).then_inc(s[f"y_stored{u}"], 16)

            run_steps(pool, step, 0, SLOTS - 1, 0, SLOTS - 1, 2, SLOTS)
            for u in range(2):
                pool.wait_ge(s[f"y_stored{u}"], 16 * ((SLOTS + 1 - u) // 2))

        @block.tensor
        def _(pe):
            for semaphore, n in loaded:
                pe.wait_ge(semaphore, n)

            def expert_of(j):
                return pe.value_load(slot_expert[0:1, bass.ds(j, 1)], min_val=0, max_val=EXPERTS - 1)

            def turn(j, u):
                pe.wait_ge(s[f"x_got{u}"], 8 * j + 16 - 8 * u)
                for c in range(KC):
                    last = nc.tensor.transpose(ps_x[:, c * P:(c + 1) * P], x_in[u][:, c * P:(c + 1) * P], ident)
                last.then_inc(s["x_turned"], 1)

            def product(j, u, expert, w, out, made):
                for c in range(KC):
                    last = nc.tensor.matmul(out[u][:, :], xT[u][:, c, :], w[:, bass.ds(expert, 1), c, :].rearrange("p a n -> p (a n)"),
                                            start=(c == 0), stop=(c == KC - 1))
                last.then_inc(made, 1)

            def turn_hidden(j):
                pe.wait_ge(s["hidden_ready"], j + 1)
                for f in range(fc):
                    last = nc.tensor.transpose(ps_h[:, f * P:(f + 1) * P], hidden[:, f * P:(f + 1) * P], ident)
                last.then_inc(s["h_turned"], 1)

            def down(j, expert):
                pe.wait_ge(s["hT_ready"], j + 1)
                wait_count(pe, s["y_ready"], j)
                for f in range(fc):
                    last = nc.tensor.matmul(ps_y[:, 0:DIM], hT[:, f, :], down_w[:, bass.ds(expert, 1), f, :].rearrange("p a n -> p (a n)"),
                                            start=(f == 0), stop=(f == fc - 1))
                last.then_inc(s["y_made"], 1)

            def step(j, u, live):
                if live(0):
                    expert = expert_of(j)
                    pe.wait_ge(s["xT_ready"], j + 1)
                    product(j, u, expert, gate_w, ps_g, s["gated"])
                if live(-1):
                    turn_hidden(j - 1)
                if live(1):
                    turn(j + 1, 1 - u)
                if live(0):
                    product(j, u, expert, up_w, ps_u, s["lifted"])
                if live(-1):
                    down(j - 1, expert_of(j - 1))

            run_steps(pe, step, -1, SLOTS, 1, SLOTS - 2, 2, SLOTS)

        @block.scalar
        def _(act):
            def step(j, u, live):
                if live(0):
                    act.wait_ge(s["gated"], j + 1)
                    wait_count(act, s["hidden_ready"], j)
                    nc.scalar.activation(silu[:, :], ps_g[u][:, :], ACT.Silu).then_inc(s["silu_ready"], 1)
                if live(1):
                    act.wait_ge(s["x_turned"], j + 2)
                    nc.scalar.copy(xT[1 - u][:, :, :], ps_x[:, 0:DIM].rearrange("p (c t) -> p c t", c=KC)).then_inc(s["xT_ready"], 1)
                if live(-1):
                    act.wait_ge(s["y_made"], j)
                    if not isinstance(j, int) or j >= 3:
                        act.wait_ge(s[f"y_stored{1 - u}"], 8 * (j - 1) - 8 * (1 - u))
                    nc.scalar.copy(y_out[1 - u][:, :], ps_y[:, 0:DIM]).then_inc(s["y_ready"], 1)

            run_steps(act, step, -1, SLOTS, 3, SLOTS - 2, 2, SLOTS)

        @block.vector
        def _(dve):
            def step(j, u, live):
                if live(-1):
                    dve.wait_ge(s["h_turned"], j)
                    nc.vector.tensor_copy(hT[:, :, :], ps_h[:, :].rearrange("p (f t) -> p f t", f=fc)).then_inc(s["hT_ready"], 1)
                if live(0):
                    dve.wait_ge(s["silu_ready"], j + 1)
                    dve.wait_ge(s["lifted"], j + 1)
                    nc.vector.tensor_tensor(hidden[:, :], silu[:, :], ps_u[u][:, :], ALU.mult).then_inc(s["hidden_ready"], 1)

            run_steps(dve, step, 0, SLOTS, 1, SLOTS - 1, 2, SLOTS)


def combine(nc, name, scope, x_sb, best_prob, position, sorted_y, out):
    sb, pb, sem = scope(name)
    y_in = sb("y_in", [P, TILES, DIM])
    got = [sem(f"got{t}") for t in range(TILES)]
    added, stored = sem("added"), sem("stored")
    out_v = out.rearrange("(t p) n -> p t n", p=P)
    part = 4

    with nc.Block() as block:

        @block.gpsimd
        def _(pool):
            for t in range(TILES):
                nc.gpsimd.indirect_dma_start(y_in[:, t, :], None, sorted_y, bass.IndirectOffsetOnAxis(position[:, t:t + 1], 0))\
                  .then_inc(got[t], 16)

        @block.vector
        def _(dve):
            for t in range(TILES):
                dve.wait_ge(got[t], 16)
                nc.vector.scalar_tensor_tensor(out=x_sb[:, t, :], in0=y_in[:, t, :], scalar=best_prob[:, t:t + 1],
                                               in1=x_sb[:, t, :], op0=ALU.mult, op1=ALU.add).then_inc(added, 1)

        @block.sync
        def _(sp):
            for t in range(0, TILES, part):
                sp.wait_ge(added, t + part)
                sp.dma_start(out_v[:, t:t + part, :], x_sb[:, t:t + part, :]).then_inc(stored, 16)
            sp.wait_ge(stored, 16 * TILES // part)


def program(nc, d, out):
    outer = ExitStack()
    of_phase = []

    def release_semaphores():
        nc.clear_and_free_semaphores(of_phase)
        of_phase.clear()
        nc.all_engine_barrier()

    with outer:
        def scope(name, stack=outer):
            def sb(n, shape, dt=F32):
                return stack.enter_context(nc.sbuf_tensor(f"{name}_{n}", shape, dt))

            def pb(n, width=512, dt=F32):
                return stack.enter_context(nc.psum_tensor(f"{name}_{n}", [P, width], dt))

            def sem(n):
                semaphore = nc.alloc_semaphore(f"{name}_{n}")
                if stack is not outer:
                    of_phase.append(semaphore)
                return semaphore

            return sb, pb, sem

        sb, pb, sem = scope("all")
        x_sb = sb("x", [P, TILES, DIM])
        consts = sb("consts", [P, C_ALL])
        ident16 = sb("ident16", [P, P], BF16)
        causal16 = sb("causal16", [P, HEADS * SEQ // 2], BF16)
        ident = consts[:, C_IDENT:C_IDENT + P]
        x_part = 4
        got_consts, got_x = sem("got_consts"), [sem(f"got_x{n}") for n in range(TILES // x_part)]
        made16 = sem("made16")
        moments = Moments(nc, sb, consts)

        c_r = sb("c_r", [P, KC, 16])
        c_br = sb("c_br", [P, 16])
        c_1 = sb("c_1", [P, KC, 1024])
        c_2 = sb("c_2", [P, 8, DIM])
        sel16 = sb("sel16", [16, 1024], BF16)
        got_c = sem("got_c")

        d_a = sb("d_a", [P, KC, HEADS * DC])
        d_b = sb("d_b", [P, HEADS // 2, DIM])
        zeros = sb("zeros", [P, DIM])
        lastT = sb("lastT", [P, BATCH])
        last_roped = nc.dram_tensor("last_roped", (BATCH, CTX), F32, kind="Internal").ap()
        got_d = sem("got_d")
        e_q = sb("e_q", [P, KC, DIM])
        e_k = sb("e_k", [P, KC, DIM])
        e_v = sb("e_v", [P, KC, GROUPS * HD])
        e_bias = {n: sb(f"e_{n}", [P, KC]) for n in ("bq", "bk", "bv")}
        f_r = sb("f_r", [P, KC, EXPERTS])
        got_e = sem("got_e")
        sorted_x = nc.dram_tensor("sorted_x", (SLOTS * P, DIM), F32, kind="Internal").ap()
        sorted_y = nc.dram_tensor("sorted_y", (SLOTS * P, DIM), F32, kind="Internal").ap()
        zero_filled, zeros_made, got_f = sem("zero_filled"), sem("zeros_made"), sem("got_f")

        era1 = outer.enter_context(ExitStack())
        sb1, _, _ = scope("w", era1)
        a_q = sb1("a_q", [P, KC, DIM])
        a_kv = sb1("a_kv", [CTX, 1, 2 * DIM])
        a_o = sb1("a_o", [P, KC, DIM])
        ctx32 = sb1("ctx32", [CTX, TILES, P])
        got_a = sem("got_a")
        b_q = sb1("b_q", [P, KC, HEADS * DH])
        b_kv = sb1("b_kv", [P, KC, 2 * DH])
        b_o = sb1("b_o", [P, HEADS, DIM])
        b_g = sb1("b_g", [P, KC])
        b_gout = sb1("b_gout", [P, DIM])
        got_b, b_scaled = sem("got_b"), sem("b_scaled")

        def chunks(ap):
            return ap.rearrange("(c p) n -> p c n", p=P)

        with nc.Block() as block:

            @block.sync
            def _(sp):
                sp.dma_start(consts[:, :], d["consts"]).then_inc(got_consts, 16)
                for n in range(0, TILES, x_part):
                    sp.dma_start(x_sb[:, n:n + x_part, :], chunks(d["x"])[:, n:n + x_part, :]).then_inc(got_x[n // x_part], 16)
                sp.dma_start(a_q[:, :, :], chunks(d["a_wq"])).then_inc(got_a, 16)
                sp.dma_start(a_kv[:, 0, :], d["a_wkv"]).then_inc(got_a, 16)
                sp.dma_start(ctx32[:, :, :], d["ctx32"].rearrange("c (t k) -> c t k", t=TILES)).then_inc(got_a, 16)
                sp.dma_start(a_o[:, :, :], chunks(d["a_wo"])).then_inc(got_a, 16)
                sp.dma_start(b_q[:, :, :], chunks(d["b_wq"])).then_inc(got_b, 16)
                sp.dma_start(b_kv[:, :, :], chunks(d["b_wkv"])).then_inc(got_b, 16)
                sp.dma_start(b_g[:, :], d["b_g"]).then_inc(got_b, 16)
                sp.dma_start(b_gout[:, :], d["b_gout"].partition_broadcast(P)).then_inc(got_b, 16)
                sp.dma_start(b_o[:, :, :], chunks(d["b_wo"])).then_inc(got_b, 16)
                sp.dma_start(c_r[:, :, :], chunks(d["c_wr"])).then_inc(got_c, 16)
                sp.dma_start(c_br[:, :], d["c_br"].partition_broadcast(P)).then_inc(got_c, 16)
                sp.dma_start(c_1[:, :, :], chunks(d["c_w1"])).then_inc(got_c, 16)
                sp.dma_start(c_2[:, :, :], chunks(d["c_w2"])).then_inc(got_c, 16)

            @block.vector
            def _(dve):
                dve.wait_ge(got_consts, 16)
                nc.vector.memset(zeros[:, :], 0.0).then_inc(zeros_made, 1)
                nc.vector.tensor_copy(sel16[:, :], consts[0:16, C_SEL:C_SEL + 1024]).then_inc(made16, 1)
                nc.vector.tensor_copy(ident16[:, :], ident).then_inc(made16, 1)
                nc.vector.tensor_copy(causal16[:, :].rearrange("p (h k) -> p h k", h=HEADS // 2),
                                      consts[:, C_CAUSAL:C_CAUSAL + SEQ].unsqueeze(1).to_broadcast([P, HEADS // 2, SEQ]))\
                  .then_inc(made16, 1)
                for t in range(TILES):
                    if t % x_part == 0:
                        dve.wait_ge(got_x[t // x_part], 16)
                    moments.take(t, x_sb[:, t, :])

        def scale_b(pool):
            pool.wait_ge(got_b, 80)
            for c in range(KC):
                nc.gpsimd.tensor_scalar(b_q[:, c, :], b_q[:, c, :], b_g[:, c:c + 1], None, ALU.mult).then_inc(b_scaled, 1)
                nc.gpsimd.tensor_scalar(b_kv[:, c, :], b_kv[:, c, :], b_g[:, c:c + 1], None, ALU.mult).then_inc(b_scaled, 1)

        phase = ExitStack()
        with phase:
            small_attention(nc, "xattn0", lambda n: scope(n, phase), moments, x_sb, consts, ident, ident16[:, :], causal16[:, :],
                            [(got_consts, 16), (made16, 3), (got_a, 64)], True,
                            {"q": a_q, "k": a_kv[:, :, 0:DIM], "v": a_kv[:, :, DIM:2 * DIM], "o": a_o}, ctx32, scale_b)

        phase = ExitStack()
        with phase:
            shared_key_attention(nc, "attn0", lambda n: scope(n, phase), moments, x_sb, consts, ident, [(got_b, 80), (b_scaled, 2 * KC)],
                                 b_q, b_kv, b_o, b_gout)
        era1.close()

        era2 = outer.enter_context(ExitStack())
        sb2, _, _ = scope("raw", era2)
        raw = {
            "q": sb2("q", [P, HEADS, DIM]),
            "cq": sb2("cq", [QC, 2, HEADS, HK]),
            "qr": sb2("qr", [DR, HEADS, DCQ]),
            "kr": sb2("kr", [DR, HEADS, DC]),
            "ckv": sb2("ckv", [HK, HEADS, DC]),
            "o": sb2("o", [HK, HEADS, DIM]),
            "last": sb2("last", [BATCH, CTX]),
        }

        def load_d(sp):
            sp.dma_start(raw["qr"][:, :, :], d["d_wqr"]).then_inc(got_d, 16)
            sp.dma_start(raw["kr"][:, :, :], d["d_wkr"]).then_inc(got_d, 16)
            sp.dma_start(raw["cq"][:, :, :, :], d["d_wcq"].rearrange("(j q) h k -> q j h k", j=2)).then_inc(got_d, 16)
            sp.dma_start(raw["ckv"][:, :, :], d["d_wckv"]).then_inc(got_d, 16)
            sp.dma_start(raw["o"][:, :, :], chunks(d["d_wo"])).then_inc(got_d, 16)
            sp.dma_start(raw["q"][:, :, :], chunks(d["d_wq"])).then_inc(got_d, 16)
            sp.dma_start(raw["last"][:, :], d["ctx"][:, (KEYS - 1) * CTX:]).then_inc(got_d, 16)
            for dst, src in ((e_q, d["e_wq"]), (e_k, d["e_wk"]), (e_v, d["e_wv"]), (f_r, d["f_wr"])):
                sp.dma_start(dst[:, :, :], chunks(src)).then_inc(got_e, 16)
            for n in ("bq", "bk", "bv"):
                sp.dma_start(e_bias[n][:, :], d[f"e_{n}"]).then_inc(got_e, 16)
            sp.wait_ge(zeros_made, 1)
            sp.dma_start(sorted_x.rearrange("(j p) n -> p j n", p=P), zeros[:, :].unsqueeze(1).to_broadcast([P, SLOTS, DIM]))\
              .then_inc(zero_filled, 16)

        phase = ExitStack()
        with phase:
            block_routed_ffn(nc, "ffn0", lambda n: scope(n, phase), moments, x_sb, consts, ident, [(got_c, 64)],
                             c_r, c_br, c_1, c_2, sel16, load_d)

        phase = ExitStack()
        with phase:
            fold_weights(nc, "fold", lambda n: scope(n, phase), moments, consts, ident, [(got_d, 7 * 16)], raw,
                         d_a, d_b, lastT, last_roped)
        release_semaphores()
        era2.close()

        era3 = outer.enter_context(ExitStack())
        sb3, _, _ = scope("moe", era3)
        f_gate = sb3("gate", [P, EXPERTS, KC, INNER])
        f_up = sb3("up", [P, EXPERTS, KC, INNER])

        def load_experts(sp, dst, src):
            for e in range(EXPERTS):
                sp.dma_start(dst[:, e, :, :], chunks(src[e])).then_inc(got_f, 16)

        def load_gates(sp):
            load_experts(sp, f_gate, d["f_gate"])
            load_experts(sp, f_up, d["f_up"])

        def load_downs(sp):
            load_experts(sp, f_down, d["f_down"])

        phase = ExitStack()
        with phase:
            latent_attention(nc, "xattn1", lambda n: scope(n, phase), moments, x_sb, consts, ident, d["ctx"], last_roped,
                             d_a, d_b, lastT, load_gates)
        f_down = sb3("down", [P, EXPERTS, INNER // P, DIM])

        phase = ExitStack()
        with phase:
            small_attention(nc, "attn1", lambda n: scope(n, phase), moments, x_sb, consts, ident, ident16[:, :], causal16[:, :],
                            [(got_e, 7 * 16)], False, {"q": e_q, "k": e_k, "v": e_v, **e_bias}, background=load_downs)
        release_semaphores()

        phase = ExitStack()
        with phase:
            own_sb, _, _ = scope("moe_tokens", phase)
            best_prob = own_sb("best_prob", [P, TILES])
            position = own_sb("position", [P, TILES], U32)
            slot_expert = own_sb("slot_expert", [P, SLOTS], I32)
            with ExitStack() as inner:
                xn_all = scope("moe_x", inner)[0]("xn_all", [P, TILES, DIM])
                route_tokens(nc, "route", lambda n: scope(n, inner), moments, x_sb, consts, ident, [(got_e, 7 * 16), (zero_filled, 16)],
                             f_r, xn_all, best_prob, position, slot_expert, sorted_x)
            with ExitStack() as inner:
                expert_ffn(nc, "experts", lambda n: scope(n, inner), ident, [(got_f, 16 * 3 * EXPERTS)],
                           f_gate, f_up, f_down, slot_expert, sorted_x, sorted_y)
            with ExitStack() as inner:
                combine(nc, "combine", lambda n: scope(n, inner), x_sb, best_prob, position, sorted_y, out)


def _tables(np):
    t = np.zeros((P, C_ALL), np.float32)
    p = np.arange(P)
    t[:, C_IDENT:C_IDENT + P] = np.eye(P)
    t[:, C_QMASK:C_QMASK + PER] = ((p // HD % PER)[:, None] == np.arange(PER)) * HD ** -0.5
    t[:, C_RMASK:C_RMASK + 4] = (p // SEQ)[:, None] == np.arange(4)
    t[:, C_CAUSAL:C_CAUSAL + SEQ] = np.where(np.arange(SEQ) < (p % SEQ)[:, None], MASKED, 0.0)
    t[:, C_BEFORE:C_BEFORE + P] = p[:, None] < p
    t[:, C_LN:C_LN + 3] = LN_EPS, LN_EPS ** 2, 1e-12
    i = np.arange(16)
    t[:, C_LOWER:C_LOWER + 256] = (i < i[:, None]).reshape(-1)
    t[:, C_STEPS:C_STEPS + 16] = 128 * i
    t[:, C_RANKS:C_RANKS + 8] = 8 - i[:8]
    t[:, C_SLOT:C_SLOT + 24] = np.arange(24)
    t[:16, C_SEL:C_SEL + 1024] = (np.arange(1024) // 64) == i[:, None]
    freq = (np.float32(1.0) / np.float32(10000.0) ** (np.arange(0, CTX, 2, dtype=np.float32) / np.float32(CTX)))
    angle = np.arange(KEYS, dtype=np.float32)[:, None] * freq[None, :].astype(np.float32)
    cos = np.repeat(np.cos(angle), 2, axis=-1)
    sin = np.repeat(np.sin(angle), 2, axis=-1)
    sin[:, :CTX // 2] *= -1
    t[:, C_COS:C_COS + P] = cos[:2 * P].reshape(P, 2 * CTX)
    t[:, C_SIN:C_SIN + P] = sin[:2 * P].reshape(P, 2 * CTX)
    t[:, C_LASTCOS:C_LASTCOS + CTX] = cos[-1]
    t[:, C_LASTSIN:C_LASTSIN + CTX] = sin[-1]
    return t


def kernel(**inputs):
    import numpy as _np
    import concourse.bacc as _bacc
    from concourse import mybir as _mybir
    from concourse.bass_utils import run_bass_kernel_spmd as _run

    a = {k: _np.asarray(v) for k, v in inputs.items()}
    ctx = a["ctx_512"]
    laid = {
        "consts": _tables(_np),
        "x": a["x"].reshape(TOKENS, DIM),
        "ctx32": ctx[:, :SEQ].transpose(2, 0, 1).reshape(CTX, TOKENS),
        "a_wq": a["L0_xattn_Wq"].T,
        "a_wkv": a["L0_xattn_Wkv_expand"].T,
        "a_wo": a["L0_xattn_Wout"].T,
        "b_wq": a["L0_attn_Wq"],
        "b_wkv": a["L0_attn_Wkv"],
        "b_wo": a["L0_attn_Wout"],
        "b_g": a["L0_attn_g_norm"].reshape(KC, P).T,
        "b_gout": a["L0_attn_g_out"].reshape(1, DIM),
        "c_wr": a["L0_ffn_Wr"].T,
        "c_br": a["L0_ffn_br"].reshape(1, 16),
        "c_w1": a["L0_ffn_W1"].T,
        "c_w2": a["L0_ffn_W2"].T,
        "ctx": ctx.reshape(BATCH, KEYS * CTX),
        "d_wq": a["L1_xattn_Wq"],
        "d_wcq": a["L1_xattn_w_kc_q"].transpose(2, 0, 1),
        "d_wqr": a["L1_xattn_W_qr"].transpose(2, 0, 1),
        "d_wkr": a["L1_xattn_W_kr"].transpose(2, 0, 1),
        "d_wckv": a["L1_xattn_w_kc_kv"].transpose(1, 0, 2),
        "d_wo": a["L1_xattn_Wo"].T,
        "e_wq": a["L1_attn_Wq"].transpose(1, 0, 2).reshape(DIM, DIM),
        "e_wk": _np.repeat(a["L1_attn_Wk"].transpose(1, 0, 2), PER, axis=1).reshape(DIM, DIM),
        "e_wv": a["L1_attn_Wv"].transpose(1, 0, 2).reshape(DIM, GROUPS * HD),
        "e_bq": a["L1_attn_bq"].reshape(KC, P).T,
        "e_bk": _np.repeat(a["L1_attn_bk"], PER, axis=0).reshape(KC, P).T,
        "e_bv": _np.repeat(a["L1_attn_bv"], PER, axis=0).reshape(KC, P).T,
        "f_wr": a["L1_ffn_router_w"],
        "f_gate": a["L1_ffn_gate_w"],
        "f_up": a["L1_ffn_up_w"],
        "f_down": a["L1_ffn_down_w"],
    }
    nc = _bacc.Bacc("TRN2", target_bir_lowering=False, num_devices=1)
    arrays, drams = {}, {}
    for name, v in laid.items():
        v = _np.ascontiguousarray(v)
        arrays[f"in_{name}"] = v
        drams[name] = nc.dram_tensor(f"in_{name}", v.shape, _mybir.dt.from_np(v.dtype), kind="ExternalInput").ap()
    out = nc.dram_tensor("out", (TOKENS, DIM), _mybir.dt.float32, kind="ExternalOutput").ap()
    program(nc, drams, out)
    r = _run(nc, [arrays], core_ids=[0])
    return r.results[0]["out"].reshape(BATCH, SEQ, DIM)
```
